# Optimizing a Trainium2 kernel written in Bass

```python
import numpy as np
import jax
import jax.numpy as jnp

def _softmax(x, axis=-1):
    return jax.nn.softmax(x, axis=axis)

def _gelu(x):
    return jax.nn.gelu(x, approximate=True)

def _silu(x):
    return jax.nn.silu(x)

def _sigmoid(x):
    return jax.nn.sigmoid(x)

def _layernorm(x, axis=-1, eps=1e-05):
    m = jnp.mean(x, axis=axis, keepdims=True)
    v = jnp.var(x, axis=axis, keepdims=True)
    return (x - m) / jnp.sqrt(v + eps)

def _scatter_add(tgt, idx, src, axis=0):
    return tgt.at[idx].add(src)

def _segment_sum(src, seg, n):
    return jax.ops.segment_sum(src, seg, n)
kernel_name = 'mk_prb_d2_jaxref_r8_492191'

def setup_inputs(seed: int=0):
    np.random.seed(seed)
    _w = jnp.asarray

    def _L0_attn_setup():
        import jax, jax.numpy as jnp
        import numpy as np
        D_MODEL = 256
        N_QUERY = 4
        N_HEAD = 8
        D_HEAD = D_MODEL // (N_QUERY * N_HEAD)
        D_KV = D_HEAD * N_HEAD
        BATCH, SEQ = (2, 256)
        key = jax.random.key(seed)
        ks = jax.random.split(key, 5)
        w_scale = 1.0 / np.sqrt(D_MODEL).astype(np.float32)
        x = jax.random.normal(ks[0], (BATCH, SEQ, D_MODEL), jnp.float32)
        Wq = jax.random.normal(ks[1], (D_MODEL, D_MODEL), jnp.float32) * w_scale
        Wk = jax.random.normal(ks[2], (D_KV, D_MODEL), jnp.float32) * w_scale
        Wv = jax.random.normal(ks[3], (D_KV, D_MODEL), jnp.float32) * w_scale
        memory = jax.random.normal(ks[4], (D_KV, D_KV), jnp.float32) * 0.02
        memory_norm = jnp.ones((D_KV, 1), jnp.float32)
        memory_weight = jnp.ones((1,), jnp.float32)
        return dict(x=x, Wq=Wq, Wk=Wk, Wv=Wv, memory=memory, memory_norm=memory_norm, memory_weight=memory_weight)
    _L0_attn_in = _L0_attn_setup()

    def _L0_ffn_setup():
        import jax, jax.numpy as jnp
        import numpy as np
        NUM_EXPERTS = 32
        TOP_K = 4
        key = jax.random.key(seed)
        k0, k1, k2, k3, k4 = jax.random.split(key, 5)
        B, S, H, I = (4, 256, 256, 128)
        sh = 1.0 / np.sqrt(H).astype(np.float32)
        si = 1.0 / np.sqrt(I).astype(np.float32)
        return {'hidden_states': jax.random.normal(k0, (B, S, H), jnp.float32), 'router_w': jax.random.normal(k1, (NUM_EXPERTS, H), jnp.float32) * sh, 'w_gate': jax.random.normal(k2, (NUM_EXPERTS, I, H), jnp.float32) * sh, 'w_up': jax.random.normal(k3, (NUM_EXPERTS, I, H), jnp.float32) * sh, 'w_down': jax.random.normal(k4, (NUM_EXPERTS, H, I), jnp.float32) * si}
    _L0_ffn_in = _L0_ffn_setup()

    def _L1_attn_setup():
        import jax, jax.numpy as jnp
        import numpy as np
        H = 16
        CHUNK = 64
        EPS = 1e-05

        def _forward(x, wq, wk, wv, wo, fq1_w, fq1_b, fq2_w, fq2_b, fk1_w, fk1_b, fk2_w, fk2_b, norm_w):
            B, L, D = x.shape
            dk = D // H

            def proj(w):
                return (x @ w.T).reshape(B, L, H, dk).transpose(0, 2, 1, 3)
            q, k, v = (proj(wq), proj(wk), proj(wv))
            q = (q @ fq1_w.T + fq1_b) * (q @ fq2_w.T + fq2_b)
            k = (k @ fk1_w.T + fk1_b) * (k @ fk2_w.T + fk2_b)
            scale = dk ** (-0.5)
            n = L // CHUNK
            qc = q.reshape(B, H, n, CHUNK, dk) * scale
            kc = k.reshape(B, H, n, CHUNK, dk)
            vc = v.reshape(B, H, n, CHUNK, dk)
            kv = jnp.einsum('bhncd,bhnce->bhnde', kc, vc)
            kv = jnp.cumsum(kv, axis=2)
            kv = jnp.concatenate([jnp.zeros_like(kv[:, :, :1]), kv[:, :, :-1]], axis=2)
            inter = jnp.einsum('bhncd,bhnde->bhnce', qc, kv)
            s = jnp.einsum('bhncd,bhnmd->bhncm', qc, kc)
            mask = jnp.tril(jnp.ones((CHUNK, CHUNK), bool))
            s = jnp.where(mask, s, 0.0)
            intra = jnp.einsum('bhncm,bhnmd->bhncd', s, vc)
            o = (inter + intra).reshape(B, H, L, dk)
            o = o * jax.lax.rsqrt(jnp.mean(o * o, axis=-1, keepdims=True) + EPS) * norm_w
            o = o.transpose(0, 2, 1, 3).reshape(B, L, D)
            return o @ wo.T
        key = jax.random.key(seed)
        ks = jax.random.split(key, 16)
        B, L, D = (2, 512, 256)
        dk = D // H
        g = 2 ** (-2.5)

        def xav(k, n):
            lim = g * np.sqrt(6.0 / (2 * n))
            return jax.random.uniform(k, (n, n), jnp.float32, -lim, lim)
        return {'x': jax.random.normal(ks[0], (B, L, D), jnp.float32), 'wq': xav(ks[1], D), 'wk': xav(ks[2], D), 'wv': xav(ks[3], D), 'wo': xav(ks[4], D), 'fq1_w': xav(ks[5], dk), 'fq1_b': jnp.zeros((dk,), jnp.float32), 'fq2_w': xav(ks[6], dk), 'fq2_b': jnp.zeros((dk,), jnp.float32), 'fk1_w': xav(ks[7], dk), 'fk1_b': jnp.zeros((dk,), jnp.float32), 'fk2_w': xav(ks[8], dk), 'fk2_b': jnp.zeros((dk,), jnp.float32), 'norm_w': jnp.ones((dk,), jnp.float32)}
    _L1_attn_in = _L1_attn_setup()

    def _L1_ffn_setup():
        import jax, jax.numpy as jnp
        import numpy as np
        DIM_IN = 256
        DIM_HIDDEN = 1024
        key = jax.random.key(seed)
        k_x, k_g, k_u, k_d = jax.random.split(key, 4)
        s_in = 1.0 / np.sqrt(DIM_IN)
        s_hid = 1.0 / np.sqrt(DIM_HIDDEN)
        x = jax.random.normal(k_x, (4, 256, DIM_IN), dtype=jnp.float32)
        w_gate = jax.random.uniform(k_g, (DIM_HIDDEN, DIM_IN), jnp.float32, -s_in, s_in)
        w_up = jax.random.uniform(k_u, (DIM_HIDDEN, DIM_IN), jnp.float32, -s_in, s_in)
        w_down = jax.random.uniform(k_d, (DIM_IN, DIM_HIDDEN), jnp.float32, -s_hid, s_hid)
        return {'x': x, 'w_gate': w_gate, 'w_up': w_up, 'w_down': w_down}
    _L1_ffn_in = _L1_ffn_setup()
    _d = {'L0_attn_x': _L0_attn_in['x'], 'L0_attn_Wq': _L0_attn_in['Wq'], 'L0_attn_Wk': _L0_attn_in['Wk'], 'L0_attn_Wv': _L0_attn_in['Wv'], 'L0_attn_memory': _L0_attn_in['memory'], 'L0_attn_memory_norm': _L0_attn_in['memory_norm'], 'L0_attn_memory_weight': _L0_attn_in['memory_weight'], 'L0_ffn_router_w': _L0_ffn_in['router_w'], 'L0_ffn_w_gate': _L0_ffn_in['w_gate'], 'L0_ffn_w_up': _L0_ffn_in['w_up'], 'L0_ffn_w_down': _L0_ffn_in['w_down'], 'L1_attn_wq': _L1_attn_in['wq'], 'L1_attn_wk': _L1_attn_in['wk'], 'L1_attn_wv': _L1_attn_in['wv'], 'L1_attn_wo': _L1_attn_in['wo'], 'L1_attn_fq1_w': _L1_attn_in['fq1_w'], 'L1_attn_fq1_b': _L1_attn_in['fq1_b'], 'L1_attn_fq2_w': _L1_attn_in['fq2_w'], 'L1_attn_fq2_b': _L1_attn_in['fq2_b'], 'L1_attn_fk1_w': _L1_attn_in['fk1_w'], 'L1_attn_fk1_b': _L1_attn_in['fk1_b'], 'L1_attn_fk2_w': _L1_attn_in['fk2_w'], 'L1_attn_fk2_b': _L1_attn_in['fk2_b'], 'L1_attn_norm_w': _L1_attn_in['norm_w'], 'L1_ffn_w_gate': _L1_ffn_in['w_gate'], 'L1_ffn_w_up': _L1_ffn_in['w_up'], 'L1_ffn_w_down': _L1_ffn_in['w_down']}
    _x0 = _d['L0_attn_x']
    _d['L0_attn_x'] = jax.random.normal(jax.random.fold_in(jax.random.key(seed), 1), (2, 1024, 256), dtype=_x0.dtype)
    del _x0
    return _d

def reference(L0_attn_x, L0_attn_Wq, L0_attn_Wk, L0_attn_Wv, L0_attn_memory, L0_attn_memory_norm, L0_attn_memory_weight, L0_ffn_router_w, L0_ffn_w_gate, L0_ffn_w_up, L0_ffn_w_down, L1_attn_wq, L1_attn_wk, L1_attn_wv, L1_attn_wo, L1_attn_fq1_w, L1_attn_fq1_b, L1_attn_fq2_w, L1_attn_fq2_b, L1_attn_fk1_w, L1_attn_fk1_b, L1_attn_fk2_w, L1_attn_fk2_b, L1_attn_norm_w, L1_ffn_w_gate, L1_ffn_w_up, L1_ffn_w_down):

    def _L0_attn_ref(x, Wq, Wk, Wv, memory, memory_norm, memory_weight):
        import jax, jax.numpy as jnp
        import numpy as np
        D_MODEL = 256
        N_QUERY = 4
        N_HEAD = 8
        D_HEAD = D_MODEL // (N_QUERY * N_HEAD)
        D_KV = D_HEAD * N_HEAD
        BATCH, SEQ = (2, 256)
        b, s, d = x.shape
        q = x @ Wq.T
        k = x @ Wk.T
        v = x @ Wv.T
        qh = q.reshape(b, s, N_QUERY, N_HEAD, D_HEAD)
        kh = k.reshape(b, s, N_HEAD, D_HEAD)
        vh = v.reshape(b, s, N_HEAD, D_HEAD)
        scale = np.float32(1.0 / np.sqrt(np.float32(D_HEAD)))
        scores = jnp.einsum('bsqhd,bthd->bqhst', qh, kh) * scale
        probs = jax.nn.softmax(scores, axis=-1)
        a_dot = jnp.einsum('bqhst,bthd->bsqhd', probs, vh)
        a_dot = a_dot.reshape(b, s, N_QUERY * N_HEAD, D_HEAD)
        sigma_q = jax.nn.elu(q.reshape(b, s, N_QUERY, D_KV))
        a_mem = sigma_q @ memory / (sigma_q @ memory_norm)
        a_mem = a_mem.reshape(b, s, N_QUERY * N_HEAD, D_HEAD)
        w = jax.nn.sigmoid(memory_weight)
        out = a_dot * (1.0 - w) + a_mem * w
        return out.reshape(b, s, D_MODEL)

    def _L0_ffn_ref(hidden_states, router_w, w_gate, w_up, w_down):
        import jax, jax.numpy as jnp
        import numpy as np
        NUM_EXPERTS = 32
        TOP_K = 4
        B, S, H = hidden_states.shape
        x = hidden_states.reshape(-1, H)
        T = x.shape[0]
        logits = x @ router_w.T
        probs = jax.nn.softmax(logits.astype(jnp.float32), axis=-1)
        top_w, top_i = jax.lax.top_k(probs, TOP_K)
        top_w = top_w / jnp.sum(top_w, axis=-1, keepdims=True)
        top_w = top_w.astype(x.dtype)
        comb = jnp.zeros((T, NUM_EXPERTS), x.dtype).at[jnp.arange(T)[:, None], top_i].add(top_w)

        def body(acc, ws):
            wg, wu, wd, c = ws
            h = jax.nn.silu(x @ wg.T) * (x @ wu.T) @ wd.T
            return (acc + h * c[:, None], None)
        out, _ = jax.lax.scan(body, jnp.zeros_like(x), (w_gate, w_up, w_down, comb.T))
        return out.reshape(B, S, H)

    def _L1_attn_ref(x, wq, wk, wv, wo, fq1_w, fq1_b, fq2_w, fq2_b, fk1_w, fk1_b, fk2_w, fk2_b, norm_w):
        import jax, jax.numpy as jnp
        import numpy as np
        H = 16
        CHUNK = 64
        EPS = 1e-05

        def _forward(x, wq, wk, wv, wo, fq1_w, fq1_b, fq2_w, fq2_b, fk1_w, fk1_b, fk2_w, fk2_b, norm_w):
            B, L, D = x.shape
            dk = D // H

            def proj(w):
                return (x @ w.T).reshape(B, L, H, dk).transpose(0, 2, 1, 3)
            q, k, v = (proj(wq), proj(wk), proj(wv))
            q = (q @ fq1_w.T + fq1_b) * (q @ fq2_w.T + fq2_b)
            k = (k @ fk1_w.T + fk1_b) * (k @ fk2_w.T + fk2_b)
            scale = dk ** (-0.5)
            n = L // CHUNK
            qc = q.reshape(B, H, n, CHUNK, dk) * scale
            kc = k.reshape(B, H, n, CHUNK, dk)
            vc = v.reshape(B, H, n, CHUNK, dk)
            kv = jnp.einsum('bhncd,bhnce->bhnde', kc, vc)
            kv = jnp.cumsum(kv, axis=2)
            kv = jnp.concatenate([jnp.zeros_like(kv[:, :, :1]), kv[:, :, :-1]], axis=2)
            inter = jnp.einsum('bhncd,bhnde->bhnce', qc, kv)
            s = jnp.einsum('bhncd,bhnmd->bhncm', qc, kc)
            mask = jnp.tril(jnp.ones((CHUNK, CHUNK), bool))
            s = jnp.where(mask, s, 0.0)
            intra = jnp.einsum('bhncm,bhnmd->bhncd', s, vc)
            o = (inter + intra).reshape(B, H, L, dk)
            o = o * jax.lax.rsqrt(jnp.mean(o * o, axis=-1, keepdims=True) + EPS) * norm_w
            o = o.transpose(0, 2, 1, 3).reshape(B, L, D)
            return o @ wo.T
        return _forward(x, wq, wk, wv, wo, fq1_w, fq1_b, fq2_w, fq2_b, fk1_w, fk1_b, fk2_w, fk2_b, norm_w)

    def _L1_ffn_ref(x, w_gate, w_up, w_down):
        import jax, jax.numpy as jnp
        import numpy as np
        DIM_IN = 256
        DIM_HIDDEN = 1024
        gate = jnp.einsum('bsd,hd->bsh', x, w_gate)
        up = jnp.einsum('bsd,hd->bsh', x, w_up)
        gated = jax.nn.silu(gate) * up
        return jnp.einsum('bsh,dh->bsd', gated, w_down)
    x = L0_attn_x
    xn = _layernorm(x, axis=-1)
    x = x + _L0_attn_ref(xn, L0_attn_Wq, L0_attn_Wk, L0_attn_Wv, L0_attn_memory, L0_attn_memory_norm, L0_attn_memory_weight) + _L0_ffn_ref(xn, L0_ffn_router_w, L0_ffn_w_gate, L0_ffn_w_up, L0_ffn_w_down)
    xn = _layernorm(x, axis=-1)
    x = x + _L1_attn_ref(xn, L1_attn_wq, L1_attn_wk, L1_attn_wv, L1_attn_wo, L1_attn_fq1_w, L1_attn_fq1_b, L1_attn_fq2_w, L1_attn_fq2_b, L1_attn_fk1_w, L1_attn_fk1_b, L1_attn_fk2_w, L1_attn_fk2_b, L1_attn_norm_w) + _L1_ffn_ref(xn, L1_ffn_w_gate, L1_ffn_w_up, L1_ffn_w_down)
    return x

_drawn_inputs = setup_inputs


def setup_inputs(seed=0):
    import zlib

    import numpy as np

    out = dict(_drawn_inputs(seed))
    spreads = {'L0_attn_memory_norm': (1.0, 0.2),
     'L1_attn_fq1_b': (0.0, 0.414),
     'L1_attn_fq2_b': (0.0, 0.439),
     'L1_attn_fk1_b': (0.0, 0.639),
     'L1_attn_fk2_b': (0.0, 0.523),
     'L1_attn_norm_w': (1.0, 0.6)}
    factors = {'L0_attn_Wk': 3.064,
     'L0_attn_Wv': 2.895,
     'L1_attn_wq': 5.306,
     'L1_attn_wk': 3.283,
     'L1_attn_wv': 2.933,
     'L1_attn_wo': 2.918,
     'L1_attn_fq1_w': 8.0,
     'L1_attn_fq2_w': 5.515,
     'L1_attn_fk1_w': 5.064,
     'L1_attn_fk2_w': 5.666}
    for name, (base, spread) in spreads.items():
        noise = np.random.default_rng([zlib.crc32(name.encode()), seed]).standard_normal(out[name].shape)
        drawn = base * np.exp(spread * noise) if base else spread * noise
        out[name] = jnp.asarray(drawn.astype(out[name].dtype))
    for name, factor in factors.items():
        out[name] = (out[name] * factor).astype(out[name].dtype)
    return out
```

```python
from collections import namedtuple
from contextlib import ExitStack

import concourse.bass as bass
from concourse import mybir

F32 = mybir.dt.float32
BF16 = mybir.dt.bfloat16
I32 = mybir.dt.int32
U32 = mybir.dt.uint32
ALU = mybir.AluOpType
ACT = mybir.ActivationFunctionType
AX = mybir.AxisListType

P = 128
EPS = 1e-5

BATCH, SEQ, D = 2, 1024, 256
TOKENS = BATCH * SEQ
TILES = TOKENS // P
KD = D // P
NQ, NKV, DH = 4, 8, 8
HEADS = BATCH * NKV
DKV = NKV * DH
SM_SCALE = DH ** -0.5

PIECES = 3
PROD_ROWS = PIECES * PIECES * DH
STACK = 96
HALF = 512
CHUNK_TILES = HALF // P


class Buffers:
    pass


def named(names, make):
    names = names.split()
    return namedtuple("Named", names)(*[make(name) for name in names])


def wait(engine, sem, value):
    if not isinstance(value, int) or value > 0:
        engine.wait_ge(sem, value)


def wait_own(pool, passed, sem, value):
    wait(pool, sem, value)
    if not isinstance(value, int):
        pool.sem_inc(passed, 1)


class Chain:

    def __init__(self, engine, sem, base=0):
        self.engine, self.sem, self.base, self.n = engine, sem, base, 0

    def link(self, instruction):
        self.n += 1
        instruction.then_inc(self.sem, 1)
        self.engine.wait_ge(self.sem, self.base + self.n)


def layernorm_statistics(nc, g, tag):
    with ExitStack() as ctx:
        sem = lambda name: ctx.enter_context(nc.semaphore(f"{tag}_{name}"))
        stats_done, var_ready, sqrt_done, rstd_done = sem("stats"), sem("var"), sem("sqrt"), sem("rstd")
        bn = ctx.enter_context(nc.sbuf_tensor(f"{tag}_bn", [P, TILES, 6], F32))
        sd = ctx.enter_context(nc.sbuf_tensor(f"{tag}_sd", [P, TILES, 2], F32))
        y = ctx.enter_context(nc.sbuf_tensor(f"{tag}_y", [P, TILES, 4], F32))
        with nc.Block() as block:
            @block.vector
            def _(dve):
                with dve.Fori(0, TILES) as t:
                    dve.bn_stats(bn[:, bass.ds(t, 1), :], g.acc[:, bass.ds(t, 1), :]).then_inc(stats_done, 1)
                dve.wait_ge(stats_done, TILES)
                for t in range(TILES):
                    last = dve.bn_aggr(g.mean_var[:, t, :], bn[:, t, :])
                last.then_inc(var_ready, 1)
                dve.wait_ge(var_ready, 1)
                dve.tensor_scalar(sd[:, :, 0], g.mean_var[:, :, 1], EPS, None, ALU.add).then_inc(var_ready, 1)
                dve.wait_ge(sqrt_done, 1)
                dve.reciprocal(y[:, :, 0], sd[:, :, 1]).then_inc(rstd_done, 1)
                dve.wait_ge(rstd_done, 1)
                dve.tensor_tensor(y[:, :, 1], y[:, :, 0], y[:, :, 0], ALU.mult).then_inc(rstd_done, 1)
                dve.wait_ge(rstd_done, 2)
                dve.tensor_tensor(y[:, :, 2], y[:, :, 1], sd[:, :, 0], ALU.mult).then_inc(rstd_done, 1)
                dve.wait_ge(rstd_done, 3)
                dve.tensor_scalar(y[:, :, 3], y[:, :, 2], -0.5, 1.5, ALU.mult, ALU.add).then_inc(rstd_done, 1)
                dve.wait_ge(rstd_done, 4)
                dve.tensor_tensor(g.rstd[:, :], y[:, :, 3], y[:, :, 0], ALU.mult).then_inc(rstd_done, 1)

            @block.scalar
            def _(act):
                act.wait_ge(var_ready, 2)
                act.activation(sd[:, :, 1], sd[:, :, 0], ACT.Sqrt).then_inc(sqrt_done, 1)


def load_inputs(nc, g, a):
    with ExitStack() as ctx:
        sem = lambda name: ctx.enter_context(nc.semaphore(name))
        x_loaded, w_loaded, ident_zeroed = sem("x_loaded"), sem("w_loaded"), sem("ident_zeroed")
        with nc.Block() as block:
            @block.sync
            def _(sp):
                for b in range(4):
                    sp.dma_start(g.acc[:, 4 * b:4 * b + 4, :], a.x[:, 4 * b:4 * b + 4, :]).then_inc(x_loaded, 16)
                sp.wait_ge(x_loaded, 64)

            @block.scalar
            def _(act):
                loads = ((g.wq, a.wq), (g.wk, a.wk), (g.wvr, a.wvr), (g.mem, a.mem), (g.memn, a.memn), (g.mw, a.mw))
                for dst, src in loads:
                    act.dma_start(dst[:], src).then_inc(w_loaded, 16)
                act.dma_start(g.wgu[:], a.wgu).then_inc(g.experts_loaded, 16)
                act.dma_start(g.wd[:], a.wd).then_inc(g.experts_loaded, 16)
                act.wait_ge(w_loaded, 16 * len(loads))

            @block.gpsimd
            def _(pool):
                pool.memset(g.ident[:], 0.0).then_inc(ident_zeroed, 1)
                pool.wait_ge(ident_zeroed, 1)
                pool.affine_select(out=g.ident[:], in_=g.ident[:], compare_op=ALU.not_equal, fill=1.0, base=0,
                                   pattern=[[-1, P]], channel_multiplier=1).then_inc(ident_zeroed, 1)


def project(nc, g, a):
    with ExitStack() as ctx:
        sb = lambda name, shape, dt: ctx.enter_context(nc.sbuf_tensor(name, shape, dt))
        sem = lambda name: ctx.enter_context(nc.semaphore(name))
        bank = [ctx.enter_context(nc.psum_tensor(f"prj{i}", [P, HALF], F32)) for i in range(8)]
        xn = sb("xn", [P, CHUNK_TILES, D], F32)
        xt = sb("xt", [P, KD, HALF], F32)
        qp = sb("qp", [P, KD, PIECES, HALF], BF16)
        kp = sb("kp", [DKV, PIECES, HALF], BF16)
        rest = sb("rest", [P, 3, HALF], F32)
        qneg = sb("qneg", [P, KD, HALF], F32)
        th = sb("th", [P, KD, HALF], F32)
        ex = sb("ex", [P, KD, HALF], F32)
        expm1 = sb("expm1", [P, KD, HALF], F32)
        sigma = sb("sigma", [P, KD, HALF], F32)
        rden = sb("rden", [P, CHUNK_TILES * NQ], F32)
        wden = sb("wden", [P, CHUNK_TILES, KD, 2], F32)
        amem = sb("amem", [P, CHUNK_TILES, KD, 2, DKV], F32)
        gate = sb("gate", [P, 2], F32)
        names = ("gate_exp gate_ready xn_ready xt_ps xt_ready q_ps k_ps vr_ps piece0 rest1 piece1 piece2 vr_read "
                 "qneg_ready th_ready sigma_ready mem_ps amem_ready acc_added dve_own stored xn_stored")
        s = named(names, lambda n: sem("p_" + n))
        STORES = 16 * (KD * PIECES * 2 + 1)
        LINKS = 4 * KD + 2

        def chunks(engine, body):
            with engine.Fori(0, BATCH) as b:
                with engine.Fori(0, SEQ // HALF) as half:
                    body(b, half, b * 2 + half)

        with nc.Block() as block:
            @block.vector
            def _(dve):
                dve.wait_ge(s.gate_exp, 1)
                own = Chain(dve, s.dve_own)
                own.link(dve.tensor_scalar(gate[:, 1:2], gate[:, 0:1], 1.0, None, ALU.add))
                own.link(dve.reciprocal(g.w[:, 0:1], gate[:, 1:2]))
                dve.tensor_scalar(g.w[:, 1:2], g.w[:, 0:1], -1.0, 1.0, ALU.mult, ALU.add).then_inc(s.gate_ready, 1)

                def body(b, half, n):
                    own = Chain(dve, s.dve_own, n * LINKS + 2)
                    dve.wait_ge(s.xt_ps, n * 2)
                    dve.wait_ge(s.xn_stored, n * 16)
                    for t in range(CHUNK_TILES):
                        dve.tensor_scalar(xn[:, t, :], g.acc[:, bass.ds(n * 4 + t, 1), :],
                                          g.mean_var[:, bass.ds(n * 4 + t, 1), 0:1].rearrange("p a b -> p (a b)"),
                                          g.rstd[:, bass.ds(n * 4 + t, 1)],
                                          ALU.subtract, ALU.mult).then_inc(s.xn_ready, 1)
                    for c in range(3):
                        rows = slice(0, DKV) if c == 2 else slice(0, P)
                        pieces = kp[:, :, :] if c == 2 else qp[:, c, :, :]
                        dve.wait_ge(s.piece0, n * 3 + c + 1)
                        dve.tensor_tensor(rest[rows, c, :], bank[2 + c][rows, :], pieces[:, 0, :],
                                          ALU.subtract).then_inc(s.rest1, 1)
                        if c < 2:
                            dve.tensor_scalar(qneg[:, c, :], bank[2 + c][:, :], 0.0, None,
                                              ALU.min).then_inc(s.qneg_ready, 1)
                    for c in range(3):
                        rows = slice(0, DKV) if c == 2 else slice(0, P)
                        pieces = kp[:, :, :] if c == 2 else qp[:, c, :, :]
                        dve.wait_ge(s.piece1, n * 3 + c + 1)
                        dve.tensor_tensor(pieces[:, 2, :], rest[rows, c, :], pieces[:, 1, :],
                                          ALU.subtract).then_inc(s.piece2, 1)
                    for c in range(KD):
                        dve.wait_ge(s.th_ready, (n * KD + c + 1) * 2)
                        rec, res, t = ex[:, c, :], expm1[:, c, :], th[:, c, :]
                        own.link(dve.tensor_scalar(rec, rec, 1.0, 0.5, ALU.add, ALU.mult))
                        own.link(dve.scalar_tensor_tensor(out=res, in0=t, scalar=-1.0, in1=rec,
                                                          op0=ALU.add, op1=ALU.mult))
                        own.link(dve.scalar_tensor_tensor(out=rec, in0=res, scalar=2.0, in1=rec,
                                                          op0=ALU.add, op1=ALU.mult))
                        own.link(dve.scalar_tensor_tensor(out=res, in0=t, scalar=2.0, in1=rec,
                                                          op0=ALU.mult, op1=ALU.mult))
                        dve.scalar_tensor_tensor(out=sigma[:, c, :], in0=bank[2 + c][:, :], scalar=0.0,
                                                 in1=expm1[:, c, :], op0=ALU.max,
                                                 op1=ALU.add).then_inc(s.sigma_ready, 1)
                    dve.wait_ge(s.mem_ps, n + 1)
                    own.link(dve.reciprocal(rden[:, :], bank[0][:, 0:CHUNK_TILES * NQ]))
                    own.link(dve.tensor_scalar(wden[:].rearrange("p t c g -> p (t c g)"), rden[:, :],
                                               g.w[:, 0:1], None, ALU.mult))
                    dve.wait_ge(s.acc_added, n)
                    for c in range(KD):
                        dve.tensor_tensor(amem[:, :, c, :, :],
                                          bank[6 + c][:, :].rearrange("p (t g e) -> p t g e", t=CHUNK_TILES, g=2),
                                          wden[:, :, c, :].unsqueeze(3).to_broadcast([P, CHUNK_TILES, 2, DKV]),
                                          ALU.mult).then_inc(s.amem_ready, 1)
                    assert own.n == LINKS
                chunks(dve, body)

            @block.scalar
            def _(act):
                act.activation(gate[:, 0:1], g.mw[:], ACT.Exp, scale=-1.0).then_inc(s.gate_exp, 1)
                act.wait_ge(s.gate_ready, 1)

                def body(b, half, n):
                    act.wait_ge(s.vr_ps, n)
                    for k in range(KD):
                        act.wait_ge(s.xt_ps, n * 2 + k + 1)
                        act.activation(xt[:, k, :], bank[k][:, :], ACT.Copy).then_inc(s.xt_ready, 1)
                    act.wait_ge(s.stored, n * STORES)
                    for c in range(3):
                        rows = slice(0, DKV) if c == 2 else slice(0, P)
                        pieces = kp[:, :, :] if c == 2 else qp[:, c, :, :]
                        act.wait_ge(s.q_ps, n * 3 + c + 1)
                        act.activation(pieces[:, 0, :], bank[2 + c][rows, :], ACT.Copy).then_inc(s.piece0, 1)
                    for c in range(3):
                        rows = slice(0, DKV) if c == 2 else slice(0, P)
                        pieces = kp[:, :, :] if c == 2 else qp[:, c, :, :]
                        act.wait_ge(s.rest1, n * 3 + c + 1)
                        act.activation(pieces[:, 1, :], rest[rows, c, :], ACT.Copy).then_inc(s.piece1, 1)
                    for c in range(KD):
                        act.wait_ge(s.qneg_ready, n * KD + c + 1)
                        act.activation(th[:, c, :], qneg[:, c, :], ACT.Tanh, scale=0.5).then_inc(s.th_ready, 1)
                        act.activation(ex[:, c, :], qneg[:, c, :], ACT.Exp).then_inc(s.th_ready, 1)
                    act.wait_ge(s.vr_ps, n + 1)
                    vr = bank[5][:, :].rearrange("p (t c) -> p t c", t=CHUNK_TILES)
                    for t in range(CHUNK_TILES):
                        act.activation(g.vp[:, bass.ds(b, 1), :, bass.ds(half * 4 + t, 1), :].rearrange("p b h t d -> p (b h t) d"),
                                       vr[:, t, 0:DKV].rearrange("p (h d) -> p h d", d=DH), ACT.Copy,
                                       scale=g.w[:, 1:2])
                    act.activation(g.logits[:, bass.ds(n * 4, 4), :], vr[:, :, DKV:DKV + 32],
                                   ACT.Copy).then_inc(s.vr_read, 1)
                chunks(act, body)

            @block.tensor
            def _(pe):
                def body(b, half, n):
                    pe.wait_ge(s.xn_ready, n * 4 + 4)
                    pe.wait_ge(s.amem_ready, n * 2)
                    for k in range(KD):
                        for t in range(CHUNK_TILES):
                            last = pe.transpose(bank[k][:, t * P:(t + 1) * P], xn[:, t, k * P:(k + 1) * P], g.ident[:])
                        last.then_inc(s.xt_ps, 1)
                    pe.wait_ge(s.sigma_ready, n * 2)
                    pe.wait_ge(s.xt_ready, n * 2 + 2)
                    for c in range(3):
                        w = g.wk if c == 2 else g.wq
                        cols = slice(0, DKV) if c == 2 else slice(c * P, (c + 1) * P)
                        rows = slice(0, DKV) if c == 2 else slice(0, P)
                        for k in range(KD):
                            last = pe.matmul(bank[2 + c][rows, :], w[:, k, cols], xt[:, k, :],
                                             start=(k == 0), stop=(k == KD - 1))
                        last.then_inc(s.q_ps, 1)
                    pe.wait_ge(s.vr_read, n)
                    for t in range(CHUNK_TILES):
                        for k in range(KD):
                            last = pe.matmul(bank[5][:, t * P:(t + 1) * P], xt[:, k, t * P:(t + 1) * P], g.wvr[:, k, :],
                                             start=(k == 0), stop=(k == KD - 1))
                    last.then_inc(s.vr_ps, 1)
                    for c in range(KD):
                        pe.wait_ge(s.sigma_ready, n * 2 + c + 1)
                        for t in range(CHUNK_TILES):
                            pe.matmul(bank[6 + c][:, t * P:(t + 1) * P], sigma[:, c, t * P:(t + 1) * P], g.mem[:],
                                      start=True, stop=True)
                    for t in range(CHUNK_TILES):
                        for c in range(KD):
                            o = (t * KD + c) * 2
                            last = pe.matmul(bank[0][:, o:o + 2], sigma[:, c, t * P:(t + 1) * P], g.memn[:],
                                             start=True, stop=True)
                    last.then_inc(s.mem_ps, 1)
                chunks(pe, body)

            @block.gpsimd
            def _(pool):
                def body(b, half, n):
                    wait_own(pool, g.passed, s.xn_ready, n * 4 + 4)
                    wait_own(pool, g.passed, s.amem_ready, n * 2 + 2)
                    rows = g.acc[:, bass.ds(n * 4, 4), :]
                    pool.tensor_tensor(rows, rows, amem[:].rearrange("p t c g e -> p t (c g e)"),
                                       ALU.add).then_inc(s.acc_added, 1)
                chunks(pool, body)

            @block.sync
            def _(sp):
                def body(b, half, n):
                    sp.wait_ge(s.xn_ready, n * 4 + 4)
                    sp.dma_start(a.xn_rows[:, bass.ds(n * 4, 4), :], xn[:]).then_inc(s.xn_stored, 16)
                    sp.wait_ge(s.piece2, n * 3 + 3)
                    for c in range(KD):
                        for p in range(PIECES):
                            for q in range(2):
                                dst = a.q_pieces[p, bass.ds(half, 1), bass.ds(b, 1), :, 2 * c + q, :]
                                sp.dma_start(dst.rearrange("x y r s -> (x y r) s"),
                                             qp[q * DKV:(q + 1) * DKV, c, p, :]).then_inc(s.stored, 16)
                    dst = a.k_pieces[:, bass.ds(b, 1), :, bass.ds(half * HALF, HALF)]
                    sp.dma_start(dst.rearrange("p x r s -> (x r) p s"), kp[:]).then_inc(s.stored, 16)
                chunks(sp, body)
                sp.wait_ge(s.xn_stored, 4 * 16)
                sp.wait_ge(s.stored, 4 * STORES)


def attention(nc, g, a, first, heads):
    units = 2 * heads
    pairs = heads // 2
    STEPS = SEQ // P
    MAXES = 2 * NQ * CHUNK_TILES
    with ExitStack() as ctx:
        sb = lambda name, shape, dt: ctx.enter_context(nc.sbuf_tensor(name, shape, dt))
        sem = lambda name: ctx.enter_context(nc.semaphore(name))
        st_bank = [ctx.enter_context(nc.psum_tensor(f"st{i}", [P, 2, HALF], F32)) for i in range(2)]
        mx_bank = [ctx.enter_context(nc.psum_tensor(f"mx{i}", [P, HALF], F32)) for i in range(2)]
        o_bank = ctx.enter_context(nc.psum_tensor("o_bank", [P, HALF], F32))
        t_bank = ctx.enter_context(nc.psum_tensor("t_bank", [P, HALF], F32))
        q_stack = [sb(f"q_stack{i}", [STACK, NQ, HALF], BF16) for i in range(4)]
        k_max = [sb(f"k_max{i}", [STACK, SEQ], BF16) for i in range(2)]
        k_st = [sb(f"k_st{i}", [STACK, SEQ], BF16) for i in range(2)]
        v_stack = [sb(f"v_stack{i}", [P, STEPS, 32], F32) for i in range(2)]
        probs = [sb(f"probs{i}", [P, NQ, HALF], F32) for i in range(2)]
        partial_max = sb("partial_max", [P, NQ * CHUNK_TILES, 2], F32)
        neg_max = [sb(f"neg_max{i}", [P, NQ * CHUNK_TILES], F32) for i in range(2)]
        m_pieces = [sb(f"m_pieces{i}", [NQ * CHUNK_TILES, PIECES, P], BF16) for i in range(2)]
        m_rest = sb("m_rest", [NQ * CHUNK_TILES, P], F32)
        o_sb = [sb(f"o_sb{i}", [P, HALF], F32) for i in range(2)]
        rsum = sb("rsum", [P, CHUNK_TILES, NQ], F32)
        q_loaded = [sem(f"q_loaded{i}") for i in range(4)]
        km_loaded = [sem(f"km_loaded{i}") for i in range(2)]
        kt_loaded = [sem(f"kt_loaded{i}") for i in range(2)]
        m_loaded = [sem(f"m_loaded{i}") for i in range(2)]
        names = ("stacks_set v_set st_done exp_done mx_done max_read negm_done mt_done mt_read m_pieces_ready pv_done "
                 "o_copied ot_done norm_done v_ready m_own rsum_done")
        s = named(names, lambda n: sem("a_" + n))

        def each_pair(engine, body):
            body(0)
            with engine.Fori(1, pairs - 1) as j:
                body(j)
            body(pairs - 1)

        def after(j, w, k, ahead):
            return not (isinstance(j, int) and j == pairs - 1) or k + ahead < 4

        with nc.Block() as block:
            @block.sync
            def _(sp):
                def load_q_unit(buf, half, head):
                    src = a.q_pieces_by_head[:, half, bass.ds(first + head, 1), :, :]
                    for copy in range(PIECES):
                        rows = slice(copy * PIECES * DH, (copy + 1) * PIECES * DH)
                        sp.dma_start(q_stack[buf][rows, :, :].rearrange("r q s -> r (q s)"),
                                     src.rearrange("p x d c -> p (x d) c")).then_inc(q_loaded[buf], 16)

                def load_k(stack, sem, head):
                    for p in range(PIECES):
                        rows = slice(p * PIECES * DH, (p + 1) * PIECES * DH)
                        src = a.k_pieces_by_head[p, bass.ds(first + head, 1), :, :]
                        sp.dma_start(stack[rows, :], src.to_broadcast([PIECES, DH, SEQ])).then_inc(sem, 16)

                sp.wait_ge(s.stacks_set, 8)
                load_k(k_max[0], km_loaded[0], 0)
                load_q_unit(0, 0, 0)
                load_q_unit(1, 1, 0)
                load_k(k_st[0], kt_loaded[0], 0)
                load_k(k_max[1], km_loaded[1], 1)
                load_q_unit(2, 0, 1)

                def body(j):
                    for k in range(4):
                        w = 4 * j + k
                        if after(j, w, k, 3):
                            wait(sp, s.st_done, 2 * STEPS * w)
                            load_q_unit((k + 3) % 4, (k + 3) % 2, 2 * j + (k + 3) // 2)
                        if k % 2 == 0 and after(j, w, k, 2):
                            wait(sp, s.st_done, 2 * STEPS * w)
                            load_k(k_st[(k // 2 + 1) % 2], kt_loaded[(k // 2 + 1) % 2], 2 * j + k // 2 + 1)
                            if after(j, w, k, 4):
                                sp.wait_ge(s.mx_done, MAXES * (w + 2))
                                load_k(k_max[k // 2], km_loaded[k // 2], 2 * j + k // 2 + 2)
                        if after(j, w, k, 1):
                            send_max((k + 1) % 4, (k + 1) % 2, w + 1)
                def send_max(buf, par, w):
                    sp.wait_ge(s.m_pieces_ready, w + 1)
                    for p in range(PIECES):
                        row = q_stack[buf][PROD_ROWS + p:PROD_ROWS + p + 1, :, :]
                        sp.dma_start(row.rearrange("o q (t c) -> o (q t) c", c=P),
                                     m_pieces[par][:, p, :]).then_inc(m_loaded[par], 16)
                send_max(0, 0, 0)
                each_pair(sp, body)

            @block.gpsimd
            def _(pool):
                for i in range(4):
                    pool.memset(q_stack[i][:], 0.0).then_inc(s.stacks_set, 1)
                for i in range(2):
                    pool.memset(k_max[i][:], 0.0).then_inc(s.stacks_set, 1)
                    pool.memset(k_st[i][:], 1.0).then_inc(s.stacks_set, 1)
                for i in range(2):
                    pool.memset(v_stack[i][:], 0.0).then_inc(s.v_set, 1)
                pool.wait_ge(s.v_set, 2)
                for i in range(2):
                    pool.memset(v_stack[i][:, :, DH:DH + 1], 1.0).then_inc(s.v_set, 1)
                pool.wait_ge(s.v_set, 4)

                def body(j):
                    for u in range(2):
                        head = 2 * j + u
                        wait_own(pool, g.passed, s.pv_done, 2 * STEPS * (head - 1))
                        pool.tensor_copy(v_stack[u][:, :, 0:DH],
                                         g.vp[:].rearrange("p b h t d -> p (b h) t d")[:, bass.ds(first + head, 1), :, :]
                                         .rearrange("p x t d -> p (x t) d")).then_inc(s.v_ready, 1)
                each_pair(pool, body)

            @block.tensor
            def _(pe):
                def max_scores(buf, w, j2, m):
                    tile, half = m // 2, m % 2
                    if m == 0:
                        pe.wait_ge(q_loaded[buf], 16 * PIECES * (j2 + 1))
                        pe.wait_ge(km_loaded[buf // 2], 16 * PIECES * (j2 + 1))
                    wait(pe, s.max_read, MAXES * w + m - 1)
                    q, t = tile // CHUNK_TILES, tile % CHUNK_TILES
                    pe.matmul(mx_bank[half][:, :], q_stack[buf][:, q, t * P:(t + 1) * P],
                              k_max[buf // 2][:, half * HALF:(half + 1) * HALF],
                              start=True, stop=True).then_inc(s.mx_done, 1)

                def turn_max(par, w):
                    pe.wait_ge(s.negm_done, w + 1)
                    wait(pe, s.norm_done, w - 2)
                    pe.transpose(t_bank[0:NQ * CHUNK_TILES, 0:P], neg_max[par][:, :], g.ident[:]).then_inc(s.mt_done, 1)

                def scores(k, w, j, n, pair):
                    wait(pe, s.exp_done, 2 * STEPS * w + 2 * n + pair - 1)
                    if n == 0 and pair == 0:
                        pe.wait_ge(m_loaded[k % 2], 16 * PIECES * (2 * j + k // 2 + 1))
                        pe.wait_ge(kt_loaded[k // 2], 16 * PIECES * (j + 1))
                    for q in range(2):
                        last = pe.matmul(st_bank[pair][:, q, :], k_st[k // 2][:, n * P:(n + 1) * P],
                                         q_stack[k][:, 2 * pair + q, :], start=True, stop=True)
                    last.then_inc(s.st_done, 1)

                def values(u, w, n, head):
                    pe.wait_ge(s.exp_done, 2 * STEPS * w + 2 * n + 2)
                    if n == 0:
                        wait(pe, s.o_copied, w)
                        pe.wait_ge(s.v_ready, head + 1)
                    for q in range(NQ):
                        last = pe.matmul(o_bank[32 * q:32 * q + 32, :], v_stack[u][:, n, :], probs[n % 2][:, q, :],
                                         start=(n == 0), stop=(n == STEPS - 1))
                    last.then_inc(s.pv_done, 1)

                def turn_outputs(par, w, mt):
                    pe.wait_ge(s.o_copied, w + 1)
                    wait(pe, s.norm_done, w)
                    pe.wait_ge(s.mt_read, mt)
                    for t in range(CHUNK_TILES):
                        last = pe.transpose(t_bank[:, t * P:(t + 1) * P], o_sb[par][:, t * P:(t + 1) * P], g.ident[:])
                    last.then_inc(s.ot_done, 1)

                for m in range(MAXES):
                    max_scores(0, 0, 0, m)
                turn_max(0, 0)
                for m in range(MAXES):
                    max_scores(1, 1, 0, m)

                def body(j):
                    for k in range(4):
                        w = 4 * j + k
                        ahead = after(j, w, k, 2)
                        buf, j2 = (k + 2) % 4, j + (k + 2) // 4
                        for n in range(STEPS):
                            if ahead:
                                max_scores(buf, w + 2, j2, 4 * n)
                            scores(k, w, j, n, 0)
                            if ahead:
                                max_scores(buf, w + 2, j2, 4 * n + 1)
                            scores(k, w, j, n, 1)
                            if ahead:
                                max_scores(buf, w + 2, j2, 4 * n + 2)
                            if n > 0:
                                values(k // 2, w, n - 1, 2 * j + k // 2)
                            elif not (isinstance(j, int) and j == 0 and k == 0):
                                values((k + 3) % 4 // 2, w - 1, STEPS - 1, 2 * j + (k - 1) // 2)
                            if ahead:
                                max_scores(buf, w + 2, j2, 4 * n + 3)
                            if n == 2 and after(j, w, k, 1):
                                turn_max((k + 1) % 2, w + 1)
                            if n == 4 and not (isinstance(j, int) and j == 0 and k == 0):
                                turn_outputs((k + 1) % 2, w - 1, w + 2 if after(j, w, k, 1) else w + 1)
                each_pair(pe, body)
                values(1, units - 1, STEPS - 1, heads - 1)
                turn_outputs((units - 1) % 2, units - 1, units)

            @block.scalar
            def _(act):
                def copy_outputs(par, w):
                    act.wait_ge(s.pv_done, STEPS * (w + 1))
                    wait(act, s.ot_done, w - 1)
                    act.activation(o_sb[par][:, :], o_bank[:, :], ACT.Copy).then_inc(s.o_copied, 1)

                def body(j):
                    for k in range(4):
                        w = 4 * j + k
                        for n in range(STEPS):
                            for pair in range(2):
                                act.wait_ge(s.st_done, 2 * STEPS * w + 2 * n + pair + 1)
                                wait(act, s.pv_done, STEPS * w + n - 1)
                                act.activation(probs[n % 2][:, 2 * pair:2 * pair + 2, :], st_bank[pair][:, :, :],
                                               ACT.Exp, scale=SM_SCALE).then_inc(s.exp_done, 1)
                            if n == 0 and not (isinstance(j, int) and j == 0 and k == 0):
                                copy_outputs((k + 1) % 2, w - 1)
                each_pair(act, body)
                copy_outputs((units - 1) % 2, units - 1)

            @block.vector
            def _(dve):
                def take_max(w, m):
                    if m == 0:
                        wait(dve, s.negm_done, w)
                    dve.wait_ge(s.mx_done, MAXES * w + m + 1)
                    dve.tensor_reduce(partial_max[:, m // 2, m % 2:m % 2 + 1], mx_bank[m % 2][:, :], AX.X,
                                      ALU.max).then_inc(s.max_read, 1)

                def join_max(par, w):
                    dve.wait_ge(s.max_read, MAXES * (w + 1))
                    dve.tensor_reduce(neg_max[par][:, :], partial_max[:, :, :], AX.X, ALU.max,
                                      negate=True).then_inc(s.negm_done, 1)

                def split_max(par, w, sent, links):
                    own = Chain(dve, s.m_own, links)
                    dve.wait_ge(s.mt_done, w + 1)
                    wait(dve, m_loaded[par], 16 * PIECES * sent)
                    m, turned = m_pieces[par], t_bank[0:NQ * CHUNK_TILES, 0:P]
                    own.link(dve.tensor_copy(m[:, 0, :], turned))
                    dve.tensor_tensor(m_rest[:, :], turned, m[:, 0, :], ALU.subtract).then_inc(s.mt_read, 1)
                    dve.wait_ge(s.mt_read, w + 1)
                    own.link(dve.tensor_copy(m[:, 1, :], m_rest[:, :]))
                    dve.tensor_tensor(m[:, 2, :], m_rest[:, :], m[:, 1, :], ALU.subtract).then_inc(s.m_pieces_ready, 1)

                def normalise(w):
                    dve.wait_ge(s.ot_done, w + 1)
                    turned = t_bank[:, :].rearrange("p (t q c) -> p t q c", t=CHUNK_TILES, q=NQ)
                    dve.reciprocal(rsum[:, :, :], turned[:, :, :, DH]).then_inc(s.rsum_done, 1)
                    dve.wait_ge(s.rsum_done, w + 1)
                    out = g.attn[:, bass.ds(2 * first + w, 1), :, :, :].rearrange("p x t q d -> p (x t) q d")
                    dve.tensor_tensor(out, turned[:, :, :, 0:DH],
                                      rsum[:, :, :].unsqueeze(3).to_broadcast([P, CHUNK_TILES, NQ, DH]),
                                      ALU.mult).then_inc(s.norm_done, 1)

                for m in range(MAXES):
                    take_max(0, m)
                join_max(0, 0)
                split_max(0, 0, 0, 0)
                for m in range(MAXES):
                    take_max(1, m)
                join_max(1, 1)

                def body(j):
                    for k in range(4):
                        w = 4 * j + k
                        for m in range(MAXES):
                            if after(j, w, k, 2):
                                take_max(w + 2, m)
                            if m == 14 and after(j, w, k, 1):
                                split_max((k + 1) % 2, w + 1, 2 * j + (k + 1) // 2, 2 * (w + 1))
                            if m == 22 and not (isinstance(j, int) and j == 0 and k == 0):
                                normalise(w - 1)
                        if after(j, w, k, 2):
                            join_max(k % 2, w + 2)
                each_pair(dve, body)
                normalise(units - 1)


EXPERTS, TOP_K, INNER = 32, 4, 128
ROW_TILES = TOKENS * TOP_K // P + EXPERTS


def dispatch(nc, g, a):
    with ExitStack() as ctx:
        sb = lambda name, shape, dt=F32: ctx.enter_context(nc.sbuf_tensor(name, shape, dt))
        sem = lambda name: ctx.enter_context(nc.semaphore(name))
        prefix = ctx.enter_context(nc.psum_tensor("prefix", [P, TILES, EXPERTS], F32))
        total = ctx.enter_context(nc.psum_tensor("total", [P, TILES, EXPERTS], F32))
        turned = ctx.enter_context(nc.psum_tensor("turned", [P, ROW_TILES], F32))
        top = sb("top", [P, TILES, 8])
        top_at = sb("top_at", [P, TILES, 8], U32)
        at = sb("at", [P, TOP_K, TILES])
        less = sb("less", [P, TILES, TOP_K])
        power = sb("power", [P, TILES, TOP_K])
        norm = sb("norm", [P, TILES, 2])
        lane = sb("lane", [P, EXPERTS])
        tile_no = sb("tile_no", [P, ROW_TILES])
        row_no = sb("row_no", [P, TILES])
        before = sb("before", [P, P])
        ones = sb("ones", [P, P])
        zeros = sb("zeros", [ROW_TILES, P])
        chosen = sb("chosen", [P, TOP_K, TILES, EXPERTS])
        mask = sb("mask", [P, TILES, EXPERTS])
        slot_of = sb("slot_of", [P, TILES, EXPERTS])
        start = sb("start", [P, 6, EXPERTS])
        tiles_i = sb("tiles_i", [P, EXPERTS], I32)
        picked = sb("picked", [P, TOP_K, TILES, EXPERTS])
        slot_f = sb("slot_f", [P, TOP_K, TILES])
        ended = sb("ended", [P, ROW_TILES, EXPERTS])
        expert_f = sb("expert_f", [P, 2, ROW_TILES])
        slots_now = [sb(f"slots_now{i}", [P, 1], I32) for i in range(TOP_K)]
        row_now = sb("row_now", [P, 2])
        rows_back = sb("rows_back", [ROW_TILES, P])
        names = ("consts table_zeroed top_done less_ready power_ready own mask_ready counted slots_ready now_ready "
                 "scattered turned_back turned_ready")
        s = named(names, lambda n: sem("d_" + n))

        with nc.Block() as block:
            @block.gpsimd
            def _(pool):
                pool.memset(zeros[:], 0.0).then_inc(s.consts, 1)
                pool.iota(lane[:], [[1, EXPERTS]], base=0, channel_multiplier=0,
                          allow_small_or_imprecise_dtypes=True).then_inc(s.consts, 1)
                pool.iota(tile_no[:], [[1, ROW_TILES]], base=0, channel_multiplier=0,
                          allow_small_or_imprecise_dtypes=True).then_inc(s.consts, 1)
                pool.iota(row_no[:], [[P, TILES]], base=0, channel_multiplier=1,
                          allow_small_or_imprecise_dtypes=True).then_inc(s.consts, 1)
                pool.memset(ones[:], 1.0).then_inc(s.consts, 1)
                pool.wait_ge(s.consts, 5)
                pool.affine_select(out=before[:], in_=ones[:], compare_op=ALU.is_gt, fill=0.0, base=0,
                                   pattern=[[1, P]], channel_multiplier=-1).then_inc(s.consts, 1)
                pool.wait_ge(s.slots_ready, 1)
                pool.wait_ge(s.table_zeroed, 16)

                def number(t):
                    for k in range(TOP_K):
                        wait_own(pool, g.passed, s.scattered, t * (16 * TOP_K))
                        pool.tensor_copy(slots_now[k][:], g.slot[:, k, bass.ds(t, 1)]).then_inc(s.now_ready, 1)
                    pool.tensor_copy(row_now[:, 0:1], row_no[:, bass.ds(t, 1)]).then_inc(s.now_ready, 1)
                    wait_own(pool, g.passed, s.now_ready, (t + 1) * (TOP_K + 1))
                    for k in range(TOP_K):
                        pool.indirect_dma_start(a.slot_row, bass.IndirectOffsetOnAxis(slots_now[k][:], 0),
                                                row_now[:, 0:1], None).then_inc(s.scattered, 16)
                number(0)
                with pool.Fori(1, TILES) as t:
                    number(t)

            @block.sync
            def _(sp):
                sp.wait_ge(s.consts, 1)
                sp.dma_start(a.slot_row.rearrange("(j p) o -> j (p o)", p=P), zeros[:]).then_inc(s.table_zeroed, 16)
                sp.wait_ge(s.table_zeroed, 16)
                sp.wait_ge(s.scattered, 16 * TOP_K * TILES)
                sp.dma_start(rows_back[:], a.slot_row.rearrange("(j p) o -> j (p o)", p=P)).then_inc(s.turned_back, 16)

            @block.scalar
            def _(act):
                act.wait_ge(s.less_ready, 1)
                act.activation(power[:], less[:], ACT.Exp).then_inc(s.power_ready, 1)

            @block.tensor
            def _(pe):
                pe.wait_ge(s.mask_ready, 1)
                pe.wait_ge(s.consts, 6)
                flat = mask[:].rearrange("p t e -> p (t e)")
                pe.matmul(prefix[:].rearrange("p t e -> p (t e)"), before[:], flat, start=True, stop=True).then_inc(s.counted, 1)
                pe.matmul(total[:].rearrange("p t e -> p (t e)"), ones[:], flat, start=True, stop=True).then_inc(s.counted, 1)
                pe.wait_ge(s.turned_back, 16)
                pe.transpose(turned[:, :], rows_back[:], g.ident[0:ROW_TILES, 0:ROW_TILES]).then_inc(s.turned_ready, 1)

            @block.vector
            def _(dve):
                own = Chain(dve, s.own)
                for t in range(TILES):
                    dve.max(top[:, t, :], g.logits[:, t, :]).then_inc(s.top_done, 1)
                dve.wait_ge(s.top_done, TILES)
                for t in range(TILES):
                    last = dve.max_index(top_at[:, t, :], top[:, t, :], g.logits[:, t, :])
                own.link(last)
                dve.tensor_tensor(less[:], top[:, :, 0:TOP_K], top[:, :, 0:1].to_broadcast([P, TILES, TOP_K]),
                                  ALU.subtract).then_inc(s.less_ready, 1)
                own.link(dve.tensor_copy(at[:], top_at[:, :, 0:TOP_K].rearrange("p t k -> p k t")))
                dve.wait_ge(s.consts, 6)
                for k in range(TOP_K):
                    own.link(dve.tensor_tensor(chosen[:, k, :, :], lane[:].unsqueeze(1).to_broadcast([P, TILES, EXPERTS]),
                                               at[:, k, :].unsqueeze(2).to_broadcast([P, TILES, EXPERTS]), ALU.is_equal))
                own.link(dve.tensor_tensor(mask[:], chosen[:, 0, :, :], chosen[:, 1, :, :], ALU.add))
                own.link(dve.tensor_tensor(mask[:], mask[:], chosen[:, 2, :, :], ALU.add))
                dve.tensor_tensor(mask[:], mask[:], chosen[:, 3, :, :], ALU.add).then_inc(s.mask_ready, 1)
                dve.wait_ge(s.power_ready, 1)
                own.link(dve.tensor_reduce(norm[:, :, 0], power[:], AX.X, ALU.add))
                own.link(dve.reciprocal(norm[:, :, 1], norm[:, :, 0]))
                own.link(dve.tensor_tensor(g.weight[:], power[:], norm[:, :, 1:2].to_broadcast([P, TILES, TOP_K]), ALU.mult))
                dve.wait_ge(s.counted, 2)
                own.link(dve.memset(slot_of[:, 0, :], 0.0))
                for t in range(1, TILES):
                    own.link(dve.tensor_tensor(slot_of[:, t, :], total[:, t - 1, :], slot_of[:, t - 1, :], ALU.add))
                own.link(dve.tensor_tensor(start[:, 0, :], total[:, TILES - 1, :], slot_of[:, TILES - 1, :], ALU.add))
                own.link(dve.tensor_scalar(tiles_i[:], start[:, 0, :], float(P - 1), None, ALU.add))
                own.link(dve.tensor_scalar(tiles_i[:], tiles_i[:], 7, None, ALU.arith_shift_right))
                own.link(dve.tensor_copy(start[:, 1, :], tiles_i[:]))
                own.link(dve.tensor_tensor_scan(start[:, 2, :], ones[:, 0:EXPERTS], start[:, 1, :], 0.0, ALU.mult, ALU.add))
                own.link(dve.tensor_tensor(start[:, 3, :], start[:, 2, :], start[:, 1, :], ALU.subtract))
                own.link(dve.tensor_scalar(start[:, 4, :], start[:, 3, :], float(P), None, ALU.mult))
                own.link(dve.tensor_tensor(slot_of[:], slot_of[:], prefix[:], ALU.add))
                own.link(dve.tensor_tensor(slot_of[:], slot_of[:], start[:, 4:5, :].to_broadcast([P, TILES, EXPERTS]), ALU.add))
                for k in range(TOP_K):
                    own.link(dve.tensor_tensor(picked[:, k, :, :], chosen[:, k, :, :], slot_of[:], ALU.mult))
                own.link(dve.tensor_reduce(slot_f[:].rearrange("p k t -> p (k t)"),
                                           picked[:].rearrange("p k t e -> p (k t) e"), AX.X, ALU.add))
                dve.tensor_copy(g.slot[:], slot_f[:]).then_inc(s.slots_ready, 1)
                own.link(dve.tensor_tensor(ended[:], tile_no[:].unsqueeze(2).to_broadcast([P, ROW_TILES, EXPERTS]),
                                           start[:, 2:3, :].to_broadcast([P, ROW_TILES, EXPERTS]), ALU.is_ge))
                own.link(dve.tensor_reduce(expert_f[:, 0, :], ended[:], AX.X, ALU.add))
                own.link(dve.tensor_scalar(g.tile_expert[:], expert_f[:, 0, :], float(EXPERTS - 1), None, ALU.min))
                dve.wait_ge(s.turned_ready, 1)
                own.link(dve.tensor_copy(g.tile_rows[:], turned[:]))


def experts(nc, g, a):
    STAGES = 4
    with ExitStack() as ctx:
        sb = lambda name, shape, dt=F32: ctx.enter_context(nc.sbuf_tensor(name, shape, dt))
        sem = lambda name: ctx.enter_context(nc.semaphore(name))
        two = lambda name, cols: [ctx.enter_context(nc.psum_tensor(f"{name}{i}", [P, cols], F32)) for i in range(2)]
        xt_ps, gu_ps, ht_ps, y_ps = two("xt_ps", D), two("gu_ps", 2 * INNER), two("ht_ps", INNER), two("y_ps", D)
        rows_now = [sb(f"rows_now{i}", [P, 1], I32) for i in range(4)]
        rows = [sb(f"rows{i}", [P, D]) for i in range(4)]
        xt = [sb(f"xt{i}", [P, KD, P]) for i in range(2)]
        silu = [sb(f"silu{i}", [P, INNER]) for i in range(2)]
        h = [sb(f"h{i}", [P, INNER]) for i in range(2)]
        ht = [sb(f"ht{i}", [P, INNER]) for i in range(2)]
        y = [sb(f"y{i}", [P, D]) for i in range(4)]
        names = ("rows_at xt_turned xt_ready gu_done silu_done h_ready h_turned ht_ready y_done y_ready")
        s = named(names, lambda n: sem("e_" + n))
        gathered = [sem(f"e_gathered{i}") for i in range(4)]
        stored = [sem(f"e_stored{i}") for i in range(4)]

        def tiles(engine, body, lag):
            for n in range(4):
                body(0, n, n)
            with engine.Fori(1, ROW_TILES // 4) as j:
                for u in range(4):
                    body(j, 4 * j + u, u)
            for n in range(ROW_TILES, ROW_TILES + lag):
                body(n // 4, n, n % 4)

        with nc.Block() as block:
            @block.gpsimd
            def _(pool):
                def body(j, n, u):
                    wait_own(pool, g.passed, s.xt_turned, n - 3)
                    pool.tensor_copy(rows_now[u][:], g.tile_rows[:, bass.ds(n, 1)]).then_inc(s.rows_at, 1)
                    wait_own(pool, g.passed, s.rows_at, n + 1)
                    pool.indirect_dma_start(rows[u][:], None, a.xn_flat,
                                            bass.IndirectOffsetOnAxis(rows_now[u][:], 0)).then_inc(gathered[u], 16)
                tiles(pool, body, 0)

            @block.tensor
            def _(pe):
                pe.wait_ge(g.experts_loaded, 32)

                def body(j, n, u):
                    whole = not isinstance(n, int)
                    if whole or n < ROW_TILES:
                        pe.wait_ge(gathered[u], 16 * (j + 1))
                        wait(pe, s.xt_ready, n - 1)
                        for k in range(KD):
                            last = pe.transpose(xt_ps[u % 2][:, k * P:(k + 1) * P], rows[u][:, k * P:(k + 1) * P], g.ident[:])
                        last.then_inc(s.xt_turned, 1)
                    if whole or 0 <= n - 1 < ROW_TILES:
                        m = n - 1
                        e = expert_of(m)
                        pe.wait_ge(s.xt_ready, m + 1)
                        wait(pe, s.h_ready, m - 1)
                        for k in range(KD):
                            last = pe.matmul(gu_ps[(u - 1) % 2][:, :], xt[(u - 1) % 2][:, k, :],
                                             g.wgu[:, bass.ds(e, 1), k, :].rearrange("p x c -> p (x c)"),
                                             start=(k == 0), stop=(k == KD - 1))
                        last.then_inc(s.gu_done, 1)
                    if whole or 0 <= n - 2 < ROW_TILES:
                        m = n - 2
                        pe.wait_ge(s.h_ready, m + 1)
                        wait(pe, s.ht_ready, m - 1)
                        pe.transpose(ht_ps[u % 2][:, :], h[u % 2][:, :], g.ident[:]).then_inc(s.h_turned, 1)
                    if whole or 0 <= n - 3 < ROW_TILES:
                        m = n - 3
                        e = expert_of(m)
                        pe.wait_ge(s.ht_ready, m + 1)
                        wait(pe, s.y_ready, m - 1)
                        pe.matmul(y_ps[(u - 3) % 2][:, :], ht[(u - 3) % 2][:, :],
                                  g.wd[:, bass.ds(e, 1), :].rearrange("p x c -> p (x c)"),
                                  start=True, stop=True).then_inc(s.y_done, 1)

                def expert_of(m):
                    return pe.value_load(g.tile_expert[0:1, bass.ds(m, 1)], min_val=0, max_val=EXPERTS - 1)
                tiles(pe, body, STAGES - 1)

            @block.scalar
            def _(act):
                def body(j, n, u):
                    whole = not isinstance(n, int)
                    if whole or n < ROW_TILES:
                        act.wait_ge(s.xt_turned, n + 1)
                        wait(act, s.gu_done, n - 1)
                        act.activation(xt[u % 2][:].rearrange("p k c -> p (k c)"), xt_ps[u % 2][:, :],
                                       ACT.Copy).then_inc(s.xt_ready, 1)
                    if whole or 0 <= n - 1 < ROW_TILES:
                        m = n - 1
                        act.wait_ge(s.gu_done, m + 1)
                        wait(act, s.h_ready, m - 1)
                        act.activation(silu[(u - 1) % 2][:], gu_ps[(u - 1) % 2][:, 0:INNER], ACT.Silu).then_inc(s.silu_done, 1)
                    if whole or 0 <= n - 2 < ROW_TILES:
                        m = n - 2
                        act.wait_ge(s.h_turned, m + 1)
                        wait(act, s.y_done, m - 1)
                        act.activation(ht[u % 2][:], ht_ps[u % 2][:, :], ACT.Copy).then_inc(s.ht_ready, 1)
                tiles(act, body, 2)

            @block.vector
            def _(dve):
                def body(j, n, u):
                    whole = not isinstance(n, int)
                    if whole or 0 <= n - 1 < ROW_TILES:
                        m = n - 1
                        dve.wait_ge(s.silu_done, m + 1)
                        wait(dve, s.h_turned, m - 1)
                        dve.tensor_tensor(h[(u - 1) % 2][:], gu_ps[(u - 1) % 2][:, INNER:2 * INNER],
                                          silu[(u - 1) % 2][:], ALU.mult).then_inc(s.h_ready, 1)
                    if whole or 0 <= n - 3 < ROW_TILES:
                        m = n - 3
                        dve.wait_ge(s.y_done, m + 1)
                        wait(dve, stored[(u - 3) % 4], 16 * (j if u == 3 else j - 1))
                        dve.tensor_copy(y[(u - 3) % 4][:], y_ps[(u - 3) % 2][:, :]).then_inc(s.y_ready, 1)
                tiles(dve, body, 3)

            @block.sync
            def _(sp):
                def body(j, n, u):
                    sp.wait_ge(s.y_ready, n + 1)
                    sp.dma_start(a.expert_out_tiles[:, bass.ds(n, 1), :].rearrange("p x c -> p (x c)"),
                                 y[u][:]).then_inc(stored[u], 16)
                tiles(sp, body, 0)
                for u in range(4):
                    sp.wait_ge(stored[u], 16 * (ROW_TILES // 4))


def combine(nc, g, a):
    with ExitStack() as ctx:
        sb = lambda name, shape, dt=F32: ctx.enter_context(nc.sbuf_tensor(name, shape, dt))
        sem = lambda name: ctx.enter_context(nc.semaphore(name))
        slots_now = [sb(f"c_slots{i}", [P, 1], I32) for i in range(TOP_K)]
        part = [sb(f"part{i}", [P, D]) for i in range(TOP_K)]
        slot_at, added = sem("c_slot_at"), sem("c_added")
        gathered = [sem(f"c_gathered{i}") for i in range(TOP_K)]
        with nc.Block() as block:
            @block.gpsimd
            def _(pool):
                def body(t):
                    for k in range(TOP_K):
                        wait_own(pool, g.passed, added, TOP_K * t + k - 3)
                        pool.tensor_copy(slots_now[k][:], g.slot[:, k, bass.ds(t, 1)]).then_inc(slot_at, 1)
                        wait_own(pool, g.passed, slot_at, TOP_K * t + k + 1)
                        pool.indirect_dma_start(part[k][:], None, a.expert_out,
                                                bass.IndirectOffsetOnAxis(slots_now[k][:], 0)).then_inc(gathered[k], 16)
                body(0)
                with pool.Fori(1, TILES) as t:
                    body(t)

            @block.vector
            def _(dve):
                def body(t):
                    for k in range(TOP_K):
                        dve.wait_ge(gathered[k], 16 * (t + 1))
                        wait(dve, added, TOP_K * t + k)
                        row = g.acc[:, bass.ds(t, 1), :].rearrange("p x c -> p (x c)")
                        dve.scalar_tensor_tensor(out=row, in0=part[k][:],
                                                 scalar=g.weight[:, bass.ds(t, 1), k:k + 1].rearrange("p x k -> p (x k)"),
                                                 in1=row, op0=ALU.mult, op1=ALU.add).then_inc(added, 1)
                body(0)
                with dve.Fori(1, TILES) as t:
                    body(t)


HEADS1, DK1 = 16, 16
GROUP = 4
GROUPS = HEADS1 // GROUP
PER_TILE = P // DK1
SCALE1 = DK1 ** -0.5
HIDDEN = 1024
HID_TILES = HIDDEN // P


def load_second(nc, g, a):
    with ExitStack() as ctx:
        sem = lambda name: ctx.enter_context(nc.semaphore(name))
        loaded, zeroed, cut = sem("l1_loaded"), sem("l1_zeroed"), sem("l1_cut")
        loads = ((g.wqkv1, a.wqkv1), (g.feat, a.feat), (g.fbias, a.fbias), (g.nw, a.nw), (g.wo1, a.wo1),
                 (g.wg1, a.wg1), (g.wu1, a.wu1), (g.wd1, a.wd1))
        with nc.Block() as block:
            @block.sync
            def _(sp):
                for dst, src in loads:
                    sp.dma_start(dst[:], src).then_inc(loaded, 16)
                sp.wait_ge(loaded, 16 * len(loads))

            @block.gpsimd
            def _(pool):
                pool.memset(g.causal[:], SCALE1).then_inc(zeroed, 1)
                pool.memset(g.same_head[:], 1.0).then_inc(zeroed, 1)
                pool.memset(g.kv_mask[:], SCALE1).then_inc(zeroed, 1)
                pool.memset(g.mean32[:], 1.0 / DK1).then_inc(zeroed, 1)
                pool.memset(g.v_pad[:], 0.0).then_inc(zeroed, 1)
                pool.memset(g.eps[:], EPS).then_inc(zeroed, 1)
                pool.wait_ge(zeroed, 6)
                pool.affine_select(out=g.causal[:], in_=g.causal[:], compare_op=ALU.is_ge, fill=0.0, base=0,
                                   pattern=[[1, P]], channel_multiplier=-1).then_inc(cut, 1)
                pool.affine_select(out=g.same_head[:], in_=g.same_head[:], compare_op=ALU.is_ge, fill=0.0, base=0,
                                   pattern=[[-DK1, PER_TILE]], channel_multiplier=1).then_inc(cut, 1)
                pool.wait_ge(cut, 2)
                pool.affine_select(out=g.same_head[:], in_=g.same_head[:], compare_op=ALU.is_ge, fill=0.0,
                                   base=DK1 - 1, pattern=[[DK1, PER_TILE]], channel_multiplier=-1).then_inc(cut, 1)
                pool.affine_select(out=g.kv_mask[:], in_=g.kv_mask[:], compare_op=ALU.is_ge, fill=0.0, base=0,
                                   pattern=[[-DK1, PER_TILE], [0, 32]], channel_multiplier=1).then_inc(cut, 1)
                pool.wait_ge(cut, 4)
                pool.affine_select(out=g.kv_mask[:], in_=g.kv_mask[:], compare_op=ALU.is_ge, fill=0.0,
                                   base=DK1 - 1, pattern=[[DK1, PER_TILE], [0, 32]],
                                   channel_multiplier=-1).then_inc(cut, 1)
                pool.affine_select(out=g.mean32[:], in_=g.mean32[:], compare_op=ALU.is_ge, fill=0.0, base=0,
                                   pattern=[[-32, GROUP], [0, 32]], channel_multiplier=1).then_inc(cut, 1)
                pool.wait_ge(cut, 6)
                pool.affine_select(out=g.mean32[:], in_=g.mean32[:], compare_op=ALU.is_ge, fill=0.0,
                                   base=31, pattern=[[32, GROUP], [0, 32]], channel_multiplier=-1).then_inc(cut, 1)


def linear_attention(nc, g, a):
    SUB = CHUNK_TILES
    with ExitStack() as ctx:
        sb = lambda name, shape, dt=F32: ctx.enter_context(nc.sbuf_tensor(name, shape, dt))
        sem = lambda name: ctx.enter_context(nc.semaphore(name))
        bank = [ctx.enter_context(nc.psum_tensor(f"la{i}", [P, HALF], F32)) for i in range(8)]
        xn = sb("l_xn", [P, CHUNK_TILES, D])
        xt = sb("l_xt", [P, KD, HALF])
        qk = sb("l_qk", [P, 4, HALF])
        f2 = sb("l_f2", [P, 4, HALF])
        qkf = sb("l_qkf", [P, 4, HALF])
        kt = sb("l_kt", [P, SUB, KD, P])
        qm = [sb(f"l_qm{i}", [P, PER_TILE, P]) for i in range(2)]
        sm = [sb(f"l_sm{i}", [P, PER_TILE, P]) for i in range(2)]
        kv = sb("l_kv", [P, KD, 2 * P])
        kv_new = sb("l_kv_new", [P, KD, 2 * P])
        sq = sb("l_sq", [P, GROUPS, P])
        ln = sb("l_ln", [P, GROUPS, P])
        rs = sb("l_rs", [P, GROUPS, P])
        on = sb("l_on", [P, GROUPS, P])
        names = ("xn_ready xt_ps xt_ready xt_kept qk_ps qk_ready feat_ps f2_ready feat_ready v_ps v_ready kt_ps kt_ready "
                 "qm_ready sc_ps sm_ready kv_ps kv_cut kv_ready kv_zero o_ps sq_ready msq_ps ln_ready rs_ready on_ready "
                 "wo_ps acc_ready")
        s = named(names, lambda n: sem("l_s_" + n))

        def chunks(engine, body, behind=None):
            with engine.Fori(0, BATCH) as b:
                with engine.Fori(0, SEQ // HALF) as half:
                    body(b, b * 2 + half)
                if behind:
                    behind(b)

        with nc.Block() as block:
            @block.tensor
            def _(pe):
                def body(b, n):
                    pe.wait_ge(s.xn_ready, n * 4 + 4)
                    pe.wait_ge(s.acc_ready, n * SUB)
                    pe.wait_ge(s.sm_ready, n * SUB * 2)
                    pe.wait_ge(s.kv_cut, n * SUB)
                    for k in range(KD):
                        for t in range(CHUNK_TILES):
                            last = pe.transpose(bank[k][:, t * P:(t + 1) * P], xn[:, t, k * P:(k + 1) * P], g.ident[:])
                        last.then_inc(s.xt_ps, 1)
                    pe.wait_ge(s.xt_ready, n * 2 + 2)
                    for c in range(4):
                        for k in range(KD):
                            last = pe.matmul(bank[2 + c][:, :], g.wqkv1[:, k, c * P:(c + 1) * P], xt[:, k, :],
                                             start=(k == 0), stop=(k == KD - 1))
                        last.then_inc(s.qk_ps, 1)
                    for t in range(CHUNK_TILES):
                        for k in range(KD):
                            last = pe.matmul(bank[6 + t // 2][:, t % 2 * D:(t % 2 + 1) * D], xt[:, k, t * P:(t + 1) * P],
                                             g.wqkv1[:, k, 2 * D:3 * D], start=(k == 0), stop=(k == KD - 1))
                        if t % 2:
                            last.then_inc(s.v_ps, 1)
                    for c in range(4):
                        pe.wait_ge(s.qk_ready, n * 4 + (1, 2, 4, 4)[c])
                        if c == 3:
                            pe.wait_ge(s.v_ready, n * 2 + 2)
                        for f in range(2):
                            last = pe.matmul(bank[2 * c + f][:, :], g.feat[:, c // 2 * 2 + f, :], qk[:, c, :],
                                             start=True, stop=True)
                        last.then_inc(s.feat_ps, 1)
                    pe.wait_ge(s.feat_ready, n * 4 + 4)
                    for t in range(SUB):
                        for c in range(KD):
                            last = pe.transpose(bank[t // 2][:, (t % 2 * 2 + c) * P:(t % 2 * 2 + c + 1) * P],
                                                qkf[:, 2 + c, t * P:(t + 1) * P], g.ident[:])
                        if t % 2:
                            last.then_inc(s.kt_ps, 1)

                    def scores(u):
                        t, c = u // 2, u % 2
                        pe.wait_ge(s.qm_ready, n * 2 * SUB + u + 1)
                        if u > 1:
                            pe.wait_ge(s.sm_ready, n * 2 * SUB + u - 1)
                        for half in range(2):
                            last = pe.matmul(bank[4 + 2 * c + half][:, :], qkf[:, 2 + c, t * P:(t + 1) * P],
                                             qm[c][:, 4 * half:4 * half + 4, :], start=True, stop=True)
                        last.then_inc(s.sc_ps, 1)

                    def outputs(u):
                        t, c = u // 2, u % 2
                        if c == 0:
                            pe.wait_ge(s.kv_ready, n * SUB + t)
                            pe.wait_ge(s.on_ready, n * SUB + t)
                        if u == 0:
                            pe.wait_ge(s.kv_zero, b + 1)
                            pe.wait_ge(s.kt_ready, n * 2 + 2)
                        pe.wait_ge(s.sm_ready, n * 2 * SUB + u + 1)
                        for gr in (2 * c, 2 * c + 1):
                            o = bank[0][:, gr * P:(gr + 1) * P]
                            pe.matmul(o, kv[:, c, gr % 2 * P:(gr % 2 + 1) * P], qkf[:, c, t * P:(t + 1) * P],
                                      start=True, stop=False, skip_group_check=True)
                            for h in range(GROUP):
                                last = pe.matmul(o[32 * h:32 * h + 32, :], g.v_pad[:, t, gr * GROUP + h, :],
                                                 sm[c][:, gr % 2 * GROUP + h, :], start=False, stop=True,
                                                 skip_group_check=True)
                        if c:
                            last.then_inc(s.o_ps, 1)

                    def state(t):
                        pe.wait_ge(s.kv_cut, n * SUB + t)
                        for c in range(KD):
                            last = pe.matmul(bank[2][:, c * 2 * P:(c + 1) * 2 * P], kt[:, t, c, :],
                                             g.v_pad[:, t, c * PER_TILE:(c + 1) * PER_TILE, :], start=True, stop=True)
                        last.then_inc(s.kv_ps, 1)

                    def mean_square(t):
                        pe.wait_ge(s.sq_ready, n * SUB + t + 1)
                        pe.wait_ge(s.ln_ready, n * SUB + t)
                        pe.matmul(bank[3][:, :], g.mean32[:], sq[:].rearrange("p g c -> p (g c)"),
                                  start=True, stop=True).then_inc(s.msq_ps, 1)

                    def project_out(t):
                        pe.wait_ge(s.on_ready, n * SUB + t + 1)
                        pe.wait_ge(s.acc_ready, n * SUB + t)
                        for gr in range(GROUPS):
                            last = pe.matmul(bank[1][:, 0:D], on[:, gr, :], g.wo1[:, gr, :],
                                             start=(gr == 0), stop=(gr == GROUPS - 1))
                        last.then_inc(s.wo_ps, 1)

                    scores(0)
                    for t in range(SUB):
                        scores(2 * t + 1)
                        outputs(2 * t)
                        if t + 1 < SUB:
                            scores(2 * t + 2)
                        outputs(2 * t + 1)
                        state(t)
                        mean_square(t)
                        project_out(t)

                chunks(pe, body)

            @block.scalar
            def _(act):
                def body(b, n):
                    act.wait_ge(s.v_ps, n * 2)
                    act.wait_ge(s.xt_kept, n)
                    for k in range(KD):
                        act.wait_ge(s.xt_ps, n * 2 + k + 1)
                        act.activation(xt[:, k, :], bank[k][:, :], ACT.Copy).then_inc(s.xt_ready, 1)
                    for c in range(4):
                        act.wait_ge(s.qk_ps, n * 4 + c + 1)
                        act.activation(qk[:, c, :], bank[2 + c][:, :], ACT.Copy).then_inc(s.qk_ready, 1)
                    act.wait_ge(s.kv_ps, n * SUB)
                    for i in range(2):
                        act.wait_ge(s.v_ps, n * 2 + i + 1)
                        act.activation(g.v_pad[:, 2 * i:2 * i + 2, :, 0:DK1].rearrange("p t h e -> p (t h) e"),
                                       bank[6 + i][:, :].rearrange("p (x e) -> p x e", e=DK1), ACT.Copy).then_inc(s.v_ready, 1)
                    for c in range(4):
                        act.wait_ge(s.feat_ps, n * 4 + c + 1)
                        act.activation(f2[:, c, :], bank[2 * c + 1][:, :], ACT.Identity,
                                       bias=g.fbias[:, c // 2 * 2 + 1:c // 2 * 2 + 2]).then_inc(s.f2_ready, 1)
                    for i in range(2):
                        act.wait_ge(s.kt_ps, n * 2 + i + 1)
                        act.activation(kt[:, 2 * i:2 * i + 2, :, :].rearrange("p t c m -> p (t c m)"), bank[i][:, :],
                                       ACT.Copy).then_inc(s.kt_ready, 1)
                    for t in range(SUB):
                        act.wait_ge(s.o_ps, n * SUB + t + 1)
                        act.activation(sq[:].rearrange("p g c -> p (g c)"), bank[0][:, :], ACT.Square).then_inc(s.sq_ready, 1)
                        act.wait_ge(s.msq_ps, n * SUB + t + 1)
                        act.wait_ge(s.rs_ready, n * SUB + t)
                        act.activation(ln[:].rearrange("p g c -> p (g c)"), bank[3][:, :], ACT.Ln,
                                       bias=g.eps[:]).then_inc(s.ln_ready, 1)
                        act.wait_ge(s.ln_ready, n * SUB + t + 1)
                        act.wait_ge(s.on_ready, n * SUB + t)
                        act.activation(rs[:].rearrange("p g c -> p (g c)"), ln[:].rearrange("p g c -> p (g c)"), ACT.Exp,
                                       scale=-0.5).then_inc(s.rs_ready, 1)
                chunks(act, body)

            @block.vector
            def _(dve):
                def body(b, n):
                    dve.wait_ge(s.xt_ps, n * 2)
                    for t in range(CHUNK_TILES):
                        dve.tensor_scalar(xn[:, t, :], g.acc[:, bass.ds(n * 4 + t, 1), :],
                                          g.mean_var[:, bass.ds(n * 4 + t, 1), 0:1].rearrange("p a b -> p (a b)"),
                                          g.rstd[:, bass.ds(n * 4 + t, 1)],
                                          ALU.subtract, ALU.mult).then_inc(s.xn_ready, 1)
                    for c in range(4):
                        dve.wait_ge(s.f2_ready, n * 4 + c + 1)
                        i = c // 2 * 2
                        dve.scalar_tensor_tensor(out=qkf[:, c, :], in0=bank[2 * c][:, :], scalar=g.fbias[:, i:i + 1],
                                                 in1=f2[:, c, :], op0=ALU.add, op1=ALU.mult).then_inc(s.feat_ready, 1)
                    dve.wait_ge(s.feat_ready, n * 4 + 4)

                    def spread(u):
                        t, c = u // 2, u % 2
                        if u > 1:
                            dve.wait_ge(s.sc_ps, n * 2 * SUB + u - 1)
                        dve.tensor_tensor(qm[c][:], qkf[:, c:c + 1, t * P:(t + 1) * P].to_broadcast([P, PER_TILE, P]),
                                          g.same_head[:].unsqueeze(2).to_broadcast([P, PER_TILE, P]),
                                          ALU.mult).then_inc(s.qm_ready, 1)

                    def mask(u):
                        t, c = u // 2, u % 2
                        dve.wait_ge(s.sc_ps, n * 2 * SUB + u + 1)
                        if c == 0:
                            dve.wait_ge(s.o_ps, n * SUB + t)
                        for half in range(2):
                            last = dve.tensor_tensor(sm[c][:, 4 * half:4 * half + 4, :],
                                                     bank[4 + 2 * c + half][:, :].rearrange("p (h c) -> p h c", h=4),
                                                     g.causal[:].unsqueeze(1).to_broadcast([P, 4, P]), ALU.mult)
                        last.then_inc(s.sm_ready, 1)

                    spread(0)
                    spread(1)
                    for t in range(SUB):
                        mask(2 * t)
                        if t + 1 < SUB:
                            spread(2 * t + 2)
                        mask(2 * t + 1)
                        if t + 1 < SUB:
                            spread(2 * t + 3)
                        dve.wait_ge(s.kv_ps, n * SUB + t + 1)
                        dve.wait_ge(s.kv_ready, n * SUB + t)
                        dve.tensor_tensor(kv_new[:], bank[2][:, :].rearrange("p (c e) -> p c e", c=KD),
                                          g.kv_mask[:].rearrange("p h e -> p (h e)").unsqueeze(1).to_broadcast([P, KD, 2 * P]),
                                          ALU.mult).then_inc(s.kv_cut, 1)
                        dve.wait_ge(s.rs_ready, n * SUB + t + 1)
                        dve.wait_ge(s.wo_ps, n * SUB + t)
                        dve.scalar_tensor_tensor(out=on[:].rearrange("p g c -> p (g c)"), in0=bank[0][:, :],
                                                 scalar=g.nw[:, 0:1], in1=rs[:].rearrange("p g c -> p (g c)"),
                                                 op0=ALU.mult, op1=ALU.mult).then_inc(s.on_ready, 1)
                        dve.wait_ge(s.wo_ps, n * SUB + t + 1)
                        row = g.acc[:, bass.ds(n * 4 + t, 1), :].rearrange("p x c -> p (x c)")
                        dve.tensor_tensor(row, row, bank[1][:, 0:D], ALU.add).then_inc(s.acc_ready, 1)
                chunks(dve, body)

            @block.gpsimd
            def _(pool):
                def clear(b):
                    wait_own(pool, g.passed, s.o_ps, (b + 1) * (TILES // BATCH))
                    wait_own(pool, g.passed, s.kv_ready, (b + 1) * (TILES // BATCH))
                    pool.memset(kv[:], 0.0).then_inc(s.kv_zero, 1)
                    wait_own(pool, g.passed, s.kv_zero, b + 2)

                def body(b, n):
                    wait_own(pool, g.passed, s.xt_ready, n * 2 + 2)
                    pool.tensor_copy(g.xt_all[:, :, bass.ds(n * HALF, HALF)], xt[:]).then_inc(s.xt_kept, 1)
                    for t in range(SUB):
                        wait_own(pool, g.passed, s.o_ps, n * SUB + t + 1)
                        wait_own(pool, g.passed, s.kv_cut, n * SUB + t + 1)
                        pool.tensor_tensor(kv[:], kv[:], kv_new[:], ALU.add).then_inc(s.kv_ready, 1)
                        wait_own(pool, g.passed, s.kv_ready, n * SUB + t + 1)
                pool.memset(kv[:], 0.0).then_inc(s.kv_zero, 1)
                pool.wait_ge(s.kv_zero, 1)
                chunks(pool, body, clear)


def feed_forward(nc, g, a):
    with ExitStack() as ctx:
        sb = lambda name, shape, dt=F32: ctx.enter_context(nc.sbuf_tensor(name, shape, dt))
        sem = lambda name: ctx.enter_context(nc.semaphore(name))
        gate = [ctx.enter_context(nc.psum_tensor(f"gate{i}", [P, HALF], F32)) for i in range(2)]
        up = [ctx.enter_context(nc.psum_tensor(f"up{i}", [P, HALF], F32)) for i in range(2)]
        down = [ctx.enter_context(nc.psum_tensor(f"down{i}", [P, HALF], F32)) for i in range(4)]
        silu = [sb(f"f_silu{i}", [P, HALF]) for i in range(2)]
        h = [sb(f"f_h{i}", [P, HALF]) for i in range(2)]
        names = "gate_done up_done silu_done h_ready down_step down_done acc_done stored"
        s = named(names, lambda n: sem("f_" + n))
        T = HID_TILES
        with nc.Block() as block:
            @block.tensor
            def _(pe):
                def body(n):
                    rows = [g.xt_all[:, k, bass.ds(n * HALF, HALF)] for k in range(KD)]

                    def gate_up(i):
                        wait(pe, s.h_ready, T * n + i - 1)
                        for w, out, done in ((g.wg1, gate, s.gate_done), (g.wu1, up, s.up_done)):
                            for k in range(KD):
                                last = pe.matmul(out[i % 2][:, :], w[:, k, i * P:(i + 1) * P], rows[k],
                                                 start=(k == 0), stop=(k == KD - 1))
                            last.then_inc(done, 1)

                    def down_part(i):
                        pe.wait_ge(s.h_ready, T * n + i + 1)
                        if i == 0:
                            wait(pe, s.acc_done, 4 * n)
                        for t in range(CHUNK_TILES):
                            last = pe.matmul(down[t][:, 0:D], h[i % 2][:, t * P:(t + 1) * P], g.wd1[:, i, :],
                                             start=(i == 0), stop=(i == T - 1))
                            if i == T - 1:
                                last.then_inc(s.down_done, 1)
                        if i < T - 1:
                            last.then_inc(s.down_step, 1)
                    gate_up(0)
                    for i in range(1, T):
                        gate_up(i)
                        down_part(i - 1)
                    down_part(T - 1)
                body(0)
                with pe.Fori(1, TOKENS // HALF) as n:
                    body(n)

            @block.scalar
            def _(act):
                def body(n):
                    for i in range(T):
                        act.wait_ge(s.gate_done, T * n + i + 1)
                        wait(act, s.h_ready, T * n + i - 1)
                        act.activation(silu[i % 2][:], gate[i % 2][:, :], ACT.Silu).then_inc(s.silu_done, 1)
                body(0)
                with act.Fori(1, TOKENS // HALF) as n:
                    body(n)

            @block.vector
            def _(dve):
                def body(n):
                    for i in range(T):
                        dve.wait_ge(s.silu_done, T * n + i + 1)
                        dve.wait_ge(s.up_done, T * n + i + 1)
                        if i > 1:
                            dve.wait_ge(s.down_step, (T - 1) * n + i - 1)
                        dve.tensor_tensor(h[i % 2][:], up[i % 2][:, :], silu[i % 2][:], ALU.mult).then_inc(s.h_ready, 1)
                    for t in range(CHUNK_TILES):
                        dve.wait_ge(s.down_done, 4 * n + t + 1)
                        row = g.acc[:, bass.ds(n * 4 + t, 1), :].rearrange("p x c -> p (x c)")
                        dve.tensor_tensor(row, row, down[t][:, 0:D], ALU.add).then_inc(s.acc_done, 1)
                body(0)
                with dve.Fori(1, TOKENS // HALF) as n:
                    body(n)

            @block.sync
            def _(sp):
                with sp.Fori(0, TOKENS // HALF) as n:
                    sp.wait_ge(s.acc_done, 4 * n + 4)
                    sp.dma_start(a.out[:, bass.ds(n * 4, 4), :], g.acc[:, bass.ds(n * 4, 4), :]).then_inc(s.stored, 16)
                sp.wait_ge(s.stored, 16 * (TOKENS // HALF))


def attn_join(nc, g):
    with ExitStack() as ctx:
        added = ctx.enter_context(nc.semaphore("attn_added"))
        with nc.Block() as block:
            @block.vector
            def _(dve):
                for b in range(BATCH):
                    for q in range(NQ):
                        rows = g.acc[:, b * 8:(b + 1) * 8, q * DKV:(q + 1) * DKV].rearrange("p t (h d) -> p t h d", d=DH)
                        part = g.attn[:, b * 16:(b + 1) * 16, :, q, :].rearrange("p (h s) t d -> p (s t) h d", s=2)
                        dve.tensor_tensor(rows, rows, part, ALU.add).then_inc(added, 1)
                dve.wait_ge(added, BATCH * NQ)


def build(nc, a):
    g = Buffers()
    with ExitStack() as ctx:
        def sb(name, shape, dt=F32, scope=ctx):
            return scope.enter_context(nc.sbuf_tensor(name, shape, dt))

        g.passed = ctx.enter_context(nc.semaphore("pool_passed"))
        g.experts_loaded = ctx.enter_context(nc.semaphore("experts_loaded"))
        g.acc = sb("acc", [P, TILES, D])
        g.ident = sb("ident", [P, P])
        g.mean_var = sb("mean_var", [P, TILES, 2])
        g.rstd = sb("rstd", [P, TILES])
        with ExitStack() as first:
            g.wq = sb("wq", [P, KD, D], scope=first)
            g.wk = sb("wk", [P, KD, DKV], scope=first)
            g.wvr = sb("wvr", [P, KD, P], scope=first)
            g.mem = sb("mem", [P, P], scope=first)
            g.memn = sb("memn", [P, 2], scope=first)
            g.mw = sb("mw", [P, 1], scope=first)
            g.w = sb("w", [P, 2], scope=first)
            g.vp = sb("vp", [P, BATCH, NKV, SEQ // P, DH], scope=first)
            g.attn = sb("attn", [P, 2 * HEADS, CHUNK_TILES, NQ, DH], scope=first)
            g.logits = sb("logits", [P, TILES, EXPERTS], scope=first)
            g.weight = sb("weight", [P, TILES, TOP_K], scope=first)
            g.slot = sb("slot", [P, TOP_K, TILES], I32, scope=first)
            g.tile_expert = sb("tile_expert", [P, ROW_TILES], I32, scope=first)
            g.tile_rows = sb("tile_rows", [P, ROW_TILES], I32, scope=first)
            with ExitStack() as weights:
                g.wgu = sb("wgu", [P, EXPERTS, KD, 2 * INNER], scope=weights)
                g.wd = sb("wd", [P, EXPERTS, D], scope=weights)
                load_inputs(nc, g, a)
                layernorm_statistics(nc, g, "ln0")
                project(nc, g, a)
                dispatch(nc, g, a)
                experts(nc, g, a)
                combine(nc, g, a)
            attention(nc, g, a, 0, HEADS)
            attn_join(nc, g)
        g.wqkv1 = sb("wqkv1", [P, KD, 3 * D])
        g.feat = sb("feat", [P, 4, P])
        g.fbias = sb("fbias", [P, 4])
        g.nw = sb("nw", [P, 1])
        g.wo1 = sb("wo1", [P, GROUPS, D])
        g.wg1 = sb("wg1", [P, KD, HIDDEN])
        g.wu1 = sb("wu1", [P, KD, HIDDEN])
        g.wd1 = sb("wd1", [P, HID_TILES, D])
        g.causal = sb("causal", [P, P])
        g.same_head = sb("same_head", [P, PER_TILE])
        g.kv_mask = sb("kv_mask", [P, PER_TILE, 32])
        g.mean32 = sb("mean32", [P, GROUP, 32])
        g.v_pad = sb("v_pad", [P, CHUNK_TILES, HEADS1, 32])
        g.eps = sb("eps", [P, 1])
        g.xt_all = sb("xt_all", [P, KD, TOKENS])
        load_second(nc, g, a)
        layernorm_statistics(nc, g, "ln1")
        linear_attention(nc, g, a)
        feed_forward(nc, g, a)


def kernel(**inputs):
    import numpy as np
    import concourse.bacc as bacc
    from concourse.bass_utils import run_bass_kernel_spmd

    x = {name: np.asarray(value) for name, value in inputs.items()}

    def by_rows(w):
        return w.T.reshape(w.shape[1] // P, P, w.shape[0]).transpose(1, 0, 2)

    def blocks(w, n):
        out = np.zeros((n * w.shape[0], n * w.shape[1]), w.dtype)
        for i in range(n):
            out[i * w.shape[0]:(i + 1) * w.shape[0], i * w.shape[1]:(i + 1) * w.shape[1]] = w
        return out

    def pad_heads(w):
        out = np.zeros((w.shape[0] // DK1, 32, w.shape[1]), w.dtype)
        out[:, 0:DK1] = w.reshape(-1, DK1, w.shape[1])
        return out.reshape(-1, w.shape[1])

    wv_router = np.concatenate([x["L0_attn_Wv"], x["L0_ffn_router_w"], np.zeros((P - DKV - EXPERTS, D), np.float32)])
    gate_up = np.concatenate([x["L0_ffn_w_gate"], x["L0_ffn_w_up"]], axis=1)
    features = [x[f"L1_attn_{n}_w"] for n in ("fq1", "fq2", "fk1", "fk2")]
    biases = [x[f"L1_attn_{n}_b"] for n in ("fq1", "fq2", "fk1", "fk2")]
    host = {
        "x": x["L0_attn_x"].reshape(TILES, P, D).transpose(1, 0, 2),
        "wq": by_rows(x["L0_attn_Wq"]),
        "wk": by_rows(x["L0_attn_Wk"]),
        "wvr": by_rows(wv_router),
        "mem": blocks(x["L0_attn_memory"], 2),
        "memn": blocks(x["L0_attn_memory_norm"], 2),
        "mw": np.broadcast_to(x["L0_attn_memory_weight"], (P, 1)),
        "wgu": gate_up.transpose(2, 0, 1).reshape(KD, P, EXPERTS, 2 * INNER).transpose(1, 2, 0, 3),
        "wd": x["L0_ffn_w_down"].transpose(2, 0, 1),
        "wqkv1": by_rows(np.concatenate([x["L1_attn_wq"], x["L1_attn_wk"], x["L1_attn_wv"]])),
        "feat": np.stack([blocks(w.T, PER_TILE) for w in features], axis=1),
        "fbias": np.stack([np.tile(b, PER_TILE) for b in biases], axis=1),
        "nw": np.tile(pad_heads(x["L1_attn_norm_w"].reshape(DK1, 1)), (GROUP, 1)),
        "wo1": pad_heads(x["L1_attn_wo"].T).reshape(GROUPS, P, D).transpose(1, 0, 2),
        "wg1": by_rows(x["L1_ffn_w_gate"]),
        "wu1": by_rows(x["L1_ffn_w_up"]),
        "wd1": by_rows(x["L1_ffn_w_down"]),
    }
    nc = bacc.Bacc("TRN2", target_bir_lowering=False, num_devices=1)
    arrays = {f"in_{name}": np.ascontiguousarray(value) for name, value in host.items()}
    i = {name: nc.dram_tensor(f"in_{name}", value.shape, F32, kind="ExternalInput").ap() for name, value in host.items()}
    a = Buffers()
    a.x, a.wq, a.wk, a.wvr, a.mem, a.memn, a.mw = (i[n] for n in ("x", "wq", "wk", "wvr", "mem", "memn", "mw"))
    a.wgu, a.wd, a.wqkv1, a.feat, a.fbias, a.nw = (i[n] for n in ("wgu", "wd", "wqkv1", "feat", "fbias", "nw"))
    a.wo1, a.wg1, a.wu1, a.wd1 = (i[n] for n in ("wo1", "wg1", "wu1", "wd1"))
    q_pieces = nc.dram_tensor("q_pieces", [PIECES, 2, BATCH, DKV, NQ, HALF], BF16).ap()
    k_pieces = nc.dram_tensor("k_pieces", [PIECES, BATCH, DKV, SEQ], BF16).ap()
    a.q_pieces, a.k_pieces = q_pieces, k_pieces
    a.q_pieces_by_head = q_pieces.rearrange("p s b (h d) q c -> p s (b h) d (q c)", d=DH)
    a.k_pieces_by_head = k_pieces.rearrange("p b (h d) t -> p (b h) d t", d=DH)
    a.xn_flat = nc.dram_tensor("xn_rows", [TOKENS, D], F32).ap()
    a.xn_rows = a.xn_flat.rearrange("(t p) d -> p t d", p=P)
    a.slot_row = nc.dram_tensor("slot_row", [ROW_TILES * P, 1], F32).ap()
    a.expert_out = nc.dram_tensor("expert_out", [ROW_TILES * P, D], F32).ap()
    a.expert_out_tiles = a.expert_out.rearrange("(t p) d -> p t d", p=P)
    rows_out = nc.dram_tensor("rows_out", [BATCH, SEQ, D], F32, kind="ExternalOutput").ap()
    a.out = rows_out.rearrange("b (t p) d -> p (b t) d", p=P)
    build(nc, a)
    result = run_bass_kernel_spmd(nc, [arrays], core_ids=[0])
    return result.results[0]["rows_out"]
```

```python
from collections import namedtuple
from contextlib import ExitStack

import concourse.bass as bass
from concourse import mybir

F32 = mybir.dt.float32
BF16 = mybir.dt.bfloat16
I32 = mybir.dt.int32
U32 = mybir.dt.uint32
ALU = mybir.AluOpType
ACT = mybir.ActivationFunctionType
AX = mybir.AxisListType

P = 128
EPS = 1e-5

BATCH, SEQ, D = 2, 1024, 256
TOKENS = BATCH * SEQ
TILES = TOKENS // P
KD = D // P
NQ, NKV, DH = 4, 8, 8
HEADS = BATCH * NKV
DKV = NKV * DH
SM_SCALE = DH ** -0.5

PIECES = 3
PROD_ROWS = PIECES * PIECES * DH
STACK = 96
HALF = 512
CHUNK_TILES = HALF // P


class Buffers:
    pass


def named(names, make):
    names = names.split()
    return namedtuple("Named", names)(*[make(name) for name in names])


def wait(engine, sem, value):
    if not isinstance(value, int) or value > 0:
        engine.wait_ge(sem, value)


def wait_own(pool, passed, sem, value):
    wait(pool, sem, value)
    if not isinstance(value, int):
        pool.sem_inc(passed, 1)


class Chain:

    def __init__(self, engine, sem, base=0):
        self.engine, self.sem, self.base, self.n = engine, sem, base, 0

    def link(self, instruction):
        self.n += 1
        instruction.then_inc(self.sem, 1)
        self.engine.wait_ge(self.sem, self.base + self.n)


def layernorm_statistics(nc, g, tag):
    with ExitStack() as ctx:
        sem = lambda name: ctx.enter_context(nc.semaphore(f"{tag}_{name}"))
        stats_done, var_ready, sqrt_done, rstd_done = sem("stats"), sem("var"), sem("sqrt"), sem("rstd")
        bn = ctx.enter_context(nc.sbuf_tensor(f"{tag}_bn", [P, TILES, 6], F32))
        sd = ctx.enter_context(nc.sbuf_tensor(f"{tag}_sd", [P, TILES, 2], F32))
        y = ctx.enter_context(nc.sbuf_tensor(f"{tag}_y", [P, TILES, 4], F32))
        with nc.Block() as block:
            @block.vector
            def _(dve):
                with dve.Fori(0, TILES) as t:
                    dve.bn_stats(bn[:, bass.ds(t, 1), :], g.acc[:, bass.ds(t, 1), :]).then_inc(stats_done, 1)
                dve.wait_ge(stats_done, TILES)
                for t in range(TILES):
                    last = dve.bn_aggr(g.mean_var[:, t, :], bn[:, t, :])
                last.then_inc(var_ready, 1)
                dve.wait_ge(var_ready, 1)
                dve.tensor_scalar(sd[:, :, 0], g.mean_var[:, :, 1], EPS, None, ALU.add).then_inc(var_ready, 1)
                dve.wait_ge(sqrt_done, 1)
                dve.reciprocal(y[:, :, 0], sd[:, :, 1]).then_inc(rstd_done, 1)
                dve.wait_ge(rstd_done, 1)
                dve.tensor_tensor(y[:, :, 1], y[:, :, 0], y[:, :, 0], ALU.mult).then_inc(rstd_done, 1)
                dve.wait_ge(rstd_done, 2)
                dve.tensor_tensor(y[:, :, 2], y[:, :, 1], sd[:, :, 0], ALU.mult).then_inc(rstd_done, 1)
                dve.wait_ge(rstd_done, 3)
                dve.tensor_scalar(y[:, :, 3], y[:, :, 2], -0.5, 1.5, ALU.mult, ALU.add).then_inc(rstd_done, 1)
                dve.wait_ge(rstd_done, 4)
                dve.tensor_tensor(g.rstd[:, :], y[:, :, 3], y[:, :, 0], ALU.mult).then_inc(rstd_done, 1)

            @block.scalar
            def _(act):
                act.wait_ge(var_ready, 2)
                act.activation(sd[:, :, 1], sd[:, :, 0], ACT.Sqrt).then_inc(sqrt_done, 1)


def load_inputs(nc, g, a):
    with ExitStack() as ctx:
        sem = lambda name: ctx.enter_context(nc.semaphore(name))
        x_loaded, w_loaded, ident_zeroed = sem("x_loaded"), sem("w_loaded"), sem("ident_zeroed")
        with nc.Block() as block:
            @block.sync
            def _(sp):
                for b in range(4):
                    sp.dma_start(g.acc[:, 4 * b:4 * b + 4, :], a.x[:, 4 * b:4 * b + 4, :]).then_inc(x_loaded, 16)
                sp.wait_ge(x_loaded, 64)

            @block.scalar
            def _(act):
                loads = ((g.wq, a.wq), (g.wk, a.wk), (g.wvr, a.wvr), (g.mem, a.mem), (g.memn, a.memn), (g.mw, a.mw))
                for dst, src in loads:
                    act.dma_start(dst[:], src).then_inc(w_loaded, 16)
                act.dma_start(g.wgu[:], a.wgu).then_inc(g.experts_loaded, 16)
                act.dma_start(g.wd[:], a.wd).then_inc(g.experts_loaded, 16)
                act.wait_ge(w_loaded, 16 * len(loads))

            @block.gpsimd
            def _(pool):
                pool.memset(g.ident[:], 0.0).then_inc(ident_zeroed, 1)
                pool.wait_ge(ident_zeroed, 1)
                pool.affine_select(out=g.ident[:], in_=g.ident[:], compare_op=ALU.not_equal, fill=1.0, base=0,
                                   pattern=[[-1, P]], channel_multiplier=1).then_inc(ident_zeroed, 1)


def project(nc, g, a):
    with ExitStack() as ctx:
        sb = lambda name, shape, dt: ctx.enter_context(nc.sbuf_tensor(name, shape, dt))
        sem = lambda name: ctx.enter_context(nc.semaphore(name))
        bank = [ctx.enter_context(nc.psum_tensor(f"prj{i}", [P, HALF], F32)) for i in range(8)]
        xn = sb("xn", [P, CHUNK_TILES, D], F32)
        xt = sb("xt", [P, KD, HALF], F32)
        qp = sb("qp", [P, KD, PIECES, HALF], BF16)
        kp = sb("kp", [DKV, PIECES, HALF], BF16)
        rest = sb("rest", [P, 3, HALF], F32)
        qneg = sb("qneg", [P, KD, HALF], F32)
        th = sb("th", [P, KD, HALF], F32)
        ex = sb("ex", [P, KD, HALF], F32)
        expm1 = sb("expm1", [P, KD, HALF], F32)
        sigma = sb("sigma", [P, KD, HALF], F32)
        rden = sb("rden", [P, CHUNK_TILES * NQ], F32)
        wden = sb("wden", [P, CHUNK_TILES, KD, 2], F32)
        amem = sb("amem", [P, CHUNK_TILES, KD, 2, DKV], F32)
        gate = sb("gate", [P, 2], F32)
        names = ("gate_exp gate_ready xn_ready xt_ps xt_ready q_ps k_ps vr_ps piece0 rest1 piece1 piece2 vr_read "
                 "qneg_ready th_ready sigma_ready mem_ps amem_ready acc_added dve_own stored xn_stored stacks_set")
        s = named(names, lambda n: sem("p_" + n))
        STORES = 16 * (KD * PIECES * 2 + 1)
        LINKS = 4 * KD + 2

        def chunks(engine, body):
            with engine.Fori(0, BATCH) as b:
                with engine.Fori(0, SEQ // HALF) as half:
                    body(b, half, b * 2 + half)

        with nc.Block() as block:
            @block.vector
            def _(dve):
                dve.wait_ge(s.gate_exp, 1)
                own = Chain(dve, s.dve_own)
                own.link(dve.tensor_scalar(gate[:, 1:2], gate[:, 0:1], 1.0, None, ALU.add))
                own.link(dve.reciprocal(g.w[:, 0:1], gate[:, 1:2]))
                dve.tensor_scalar(g.w[:, 1:2], g.w[:, 0:1], -1.0, 1.0, ALU.mult, ALU.add).then_inc(s.gate_ready, 1)

                def body(b, half, n):
                    own = Chain(dve, s.dve_own, n * LINKS + 2)
                    dve.wait_ge(s.xt_ps, n * 2)
                    dve.wait_ge(s.xn_stored, n * 16)
                    for t in range(CHUNK_TILES):
                        dve.tensor_scalar(xn[:, t, :], g.acc[:, bass.ds(n * 4 + t, 1), :],
                                          g.mean_var[:, bass.ds(n * 4 + t, 1), 0:1].rearrange("p a b -> p (a b)"),
                                          g.rstd[:, bass.ds(n * 4 + t, 1)],
                                          ALU.subtract, ALU.mult).then_inc(s.xn_ready, 1)
                    for c in range(3):
                        rows = slice(0, DKV) if c == 2 else slice(0, P)
                        pieces = kp[:, :, :] if c == 2 else qp[:, c, :, :]
                        dve.wait_ge(s.piece0, n * 3 + c + 1)
                        dve.tensor_tensor(rest[rows, c, :], bank[2 + c][rows, :], pieces[:, 0, :],
                                          ALU.subtract).then_inc(s.rest1, 1)
                        if c < 2:
                            dve.tensor_scalar(qneg[:, c, :], bank[2 + c][:, :], 0.0, None,
                                              ALU.min).then_inc(s.qneg_ready, 1)
                    for c in range(3):
                        rows = slice(0, DKV) if c == 2 else slice(0, P)
                        pieces = kp[:, :, :] if c == 2 else qp[:, c, :, :]
                        dve.wait_ge(s.piece1, n * 3 + c + 1)
                        dve.tensor_tensor(pieces[:, 2, :], rest[rows, c, :], pieces[:, 1, :],
                                          ALU.subtract).then_inc(s.piece2, 1)
                    for c in range(KD):
                        dve.wait_ge(s.th_ready, (n * KD + c + 1) * 2)
                        rec, res, t = ex[:, c, :], expm1[:, c, :], th[:, c, :]
                        own.link(dve.tensor_scalar(rec, rec, 1.0, 0.5, ALU.add, ALU.mult))
                        own.link(dve.scalar_tensor_tensor(out=res, in0=t, scalar=-1.0, in1=rec,
                                                          op0=ALU.add, op1=ALU.mult))
                        own.link(dve.scalar_tensor_tensor(out=rec, in0=res, scalar=2.0, in1=rec,
                                                          op0=ALU.add, op1=ALU.mult))
                        own.link(dve.scalar_tensor_tensor(out=res, in0=t, scalar=2.0, in1=rec,
                                                          op0=ALU.mult, op1=ALU.mult))
                        dve.scalar_tensor_tensor(out=sigma[:, c, :], in0=bank[2 + c][:, :], scalar=0.0,
                                                 in1=expm1[:, c, :], op0=ALU.max,
                                                 op1=ALU.add).then_inc(s.sigma_ready, 1)
                    dve.wait_ge(s.mem_ps, n + 1)
                    own.link(dve.reciprocal(rden[:, :], bank[0][:, 0:CHUNK_TILES * NQ]))
                    own.link(dve.tensor_scalar(wden[:].rearrange("p t c g -> p (t c g)"), rden[:, :],
                                               g.w[:, 0:1], None, ALU.mult))
                    dve.wait_ge(s.acc_added, n)
                    for c in range(KD):
                        dve.tensor_tensor(amem[:, :, c, :, :],
                                          bank[6 + c][:, :].rearrange("p (t g e) -> p t g e", t=CHUNK_TILES, g=2),
                                          wden[:, :, c, :].unsqueeze(3).to_broadcast([P, CHUNK_TILES, 2, DKV]),
                                          ALU.mult).then_inc(s.amem_ready, 1)
                    assert own.n == LINKS
                chunks(dve, body)

            @block.scalar
            def _(act):
                act.activation(gate[:, 0:1], g.mw[:], ACT.Exp, scale=-1.0).then_inc(s.gate_exp, 1)
                act.wait_ge(s.gate_ready, 1)

                def body(b, half, n):
                    act.wait_ge(s.vr_ps, n)
                    for k in range(KD):
                        act.wait_ge(s.xt_ps, n * 2 + k + 1)
                        act.activation(xt[:, k, :], bank[k][:, :], ACT.Copy).then_inc(s.xt_ready, 1)
                    act.wait_ge(s.stored, n * STORES)
                    for c in range(3):
                        rows = slice(0, DKV) if c == 2 else slice(0, P)
                        pieces = kp[:, :, :] if c == 2 else qp[:, c, :, :]
                        act.wait_ge(s.q_ps, n * 3 + c + 1)
                        act.activation(pieces[:, 0, :], bank[2 + c][rows, :], ACT.Copy).then_inc(s.piece0, 1)
                    for c in range(3):
                        rows = slice(0, DKV) if c == 2 else slice(0, P)
                        pieces = kp[:, :, :] if c == 2 else qp[:, c, :, :]
                        act.wait_ge(s.rest1, n * 3 + c + 1)
                        act.activation(pieces[:, 1, :], rest[rows, c, :], ACT.Copy).then_inc(s.piece1, 1)
                    for c in range(KD):
                        act.wait_ge(s.qneg_ready, n * KD + c + 1)
                        act.activation(th[:, c, :], qneg[:, c, :], ACT.Tanh, scale=0.5).then_inc(s.th_ready, 1)
                        act.activation(ex[:, c, :], qneg[:, c, :], ACT.Exp).then_inc(s.th_ready, 1)
                    act.wait_ge(s.vr_ps, n + 1)
                    vr = bank[5][:, :].rearrange("p (t c) -> p t c", t=CHUNK_TILES)
                    for t in range(CHUNK_TILES):
                        act.activation(g.vp[:, bass.ds(b, 1), :, bass.ds(half * 4 + t, 1), :].rearrange("p b h t d -> p (b h t) d"),
                                       vr[:, t, 0:DKV].rearrange("p (h d) -> p h d", d=DH), ACT.Copy,
                                       scale=g.w[:, 1:2])
                    act.activation(g.logits[:, bass.ds(n * 4, 4), :], vr[:, :, DKV:DKV + 32],
                                   ACT.Copy).then_inc(s.vr_read, 1)
                chunks(act, body)

            @block.tensor
            def _(pe):
                def body(b, half, n):
                    pe.wait_ge(s.xn_ready, n * 4 + 4)
                    pe.wait_ge(s.amem_ready, n * 2)
                    for k in range(KD):
                        for t in range(CHUNK_TILES):
                            last = pe.transpose(bank[k][:, t * P:(t + 1) * P], xn[:, t, k * P:(k + 1) * P], g.ident[:])
                        last.then_inc(s.xt_ps, 1)
                    pe.wait_ge(s.sigma_ready, n * 2)
                    pe.wait_ge(s.xt_ready, n * 2 + 2)
                    for c in range(3):
                        w = g.wk if c == 2 else g.wq
                        cols = slice(0, DKV) if c == 2 else slice(c * P, (c + 1) * P)
                        rows = slice(0, DKV) if c == 2 else slice(0, P)
                        for k in range(KD):
                            last = pe.matmul(bank[2 + c][rows, :], w[:, k, cols], xt[:, k, :],
                                             start=(k == 0), stop=(k == KD - 1))
                        last.then_inc(s.q_ps, 1)
                    pe.wait_ge(s.vr_read, n)
                    for t in range(CHUNK_TILES):
                        for k in range(KD):
                            last = pe.matmul(bank[5][:, t * P:(t + 1) * P], xt[:, k, t * P:(t + 1) * P], g.wvr[:, k, :],
                                             start=(k == 0), stop=(k == KD - 1))
                    last.then_inc(s.vr_ps, 1)
                    for c in range(KD):
                        pe.wait_ge(s.sigma_ready, n * 2 + c + 1)
                        for t in range(CHUNK_TILES):
                            pe.matmul(bank[6 + c][:, t * P:(t + 1) * P], sigma[:, c, t * P:(t + 1) * P], g.mem[:],
                                      start=True, stop=True)
                    for t in range(CHUNK_TILES):
                        for c in range(KD):
                            o = (t * KD + c) * 2
                            last = pe.matmul(bank[0][:, o:o + 2], sigma[:, c, t * P:(t + 1) * P], g.memn[:],
                                             start=True, stop=True)
                    last.then_inc(s.mem_ps, 1)
                chunks(pe, body)

            @block.gpsimd
            def _(pool):
                for stack in g.q_stack + g.k_max:
                    pool.memset(stack[:], 0.0).then_inc(s.stacks_set, 1)
                for stack in g.k_st:
                    pool.memset(stack[:], 1.0).then_inc(s.stacks_set, 1)
                for stack in g.v_stack:
                    pool.memset(stack[:], 0.0).then_inc(s.stacks_set, 1)
                pool.wait_ge(s.stacks_set, 10)
                for stack in g.v_stack:
                    pool.memset(stack[:, :, DH:DH + 1], 1.0).then_inc(s.stacks_set, 1)

                def body(b, half, n):
                    wait_own(pool, g.passed, s.xn_ready, n * 4 + 4)
                    wait_own(pool, g.passed, s.amem_ready, n * 2 + 2)
                    rows = g.acc[:, bass.ds(n * 4, 4), :]
                    pool.tensor_tensor(rows, rows, amem[:].rearrange("p t c g e -> p t (c g e)"),
                                       ALU.add).then_inc(s.acc_added, 1)
                chunks(pool, body)

            @block.sync
            def _(sp):
                def body(b, half, n):
                    sp.wait_ge(s.xn_ready, n * 4 + 4)
                    sp.dma_start(a.xn_rows[:, bass.ds(n * 4, 4), :], xn[:]).then_inc(s.xn_stored, 16)
                    sp.wait_ge(s.piece2, n * 3 + 3)
                    for c in range(KD):
                        for p in range(PIECES):
                            for q in range(2):
                                dst = a.q_pieces[p, bass.ds(half, 1), bass.ds(b, 1), :, 2 * c + q, :]
                                sp.dma_start(dst.rearrange("x y r s -> (x y r) s"),
                                             qp[q * DKV:(q + 1) * DKV, c, p, :]).then_inc(s.stored, 16)
                    dst = a.k_pieces[:, bass.ds(b, 1), :, bass.ds(half * HALF, HALF)]
                    sp.dma_start(dst.rearrange("p x r s -> (x r) p s"), kp[:]).then_inc(s.stored, 16)
                chunks(sp, body)
                sp.wait_ge(s.xn_stored, 4 * 16)
                sp.wait_ge(s.stored, 4 * STORES)


def attention(nc, g, a, b, beside):
    first, heads = b * NKV, NKV
    units = 2 * heads
    pairs = heads // 2
    STEPS = SEQ // P
    MAXES = 2 * NQ * CHUNK_TILES
    with nc.cleanup_on_exit(), ExitStack() as ctx:
        sb = lambda name, shape, dt: ctx.enter_context(nc.sbuf_tensor(f"{name}_b{b}", shape, dt))
        sem = lambda name: nc.alloc_semaphore(f"{name}_b{b}")
        st_bank = [ctx.enter_context(nc.psum_tensor(f"st{i}_b{b}", [P, 2, HALF], F32)) for i in range(2)]
        mx_bank = [ctx.enter_context(nc.psum_tensor(f"mx{i}_b{b}", [P, HALF], F32)) for i in range(3)]
        o_bank = ctx.enter_context(nc.psum_tensor(f"o_bank_b{b}", [P, HALF], F32))
        TURN_MAX, TURN_OUT = 12, 20
        m_bank, t_bank = mx_bank[TURN_MAX % 3], mx_bank[TURN_OUT % 3]
        q_stack, k_max, k_st, v_stack = g.q_stack, g.k_max, g.k_st, g.v_stack
        probs = [sb(f"probs{i}", [P, NQ, HALF], F32) for i in range(2)]
        partial_max = sb("partial_max", [P, NQ * CHUNK_TILES, 2], F32)
        neg_max = [sb(f"neg_max{i}", [P, NQ * CHUNK_TILES], F32) for i in range(2)]
        m_pieces = [sb(f"m_pieces{i}", [NQ * CHUNK_TILES, PIECES, P], BF16) for i in range(2)]
        m_rest = sb("m_rest", [NQ * CHUNK_TILES, P], F32)
        o_sb = [sb(f"o_sb{i}", [P, HALF], F32) for i in range(2)]
        out = [sb(f"out{i}", [P, CHUNK_TILES, NQ, DH], F32) for i in range(4)]
        rsum = sb("rsum", [P, CHUNK_TILES, NQ], F32)
        q_loaded = [sem(f"q_loaded{i}") for i in range(4)]
        km_loaded = [sem(f"km_loaded{i}") for i in range(2)]
        kt_loaded = [sem(f"kt_loaded{i}") for i in range(2)]
        m_loaded = [sem(f"m_loaded{i}") for i in range(2)]
        names = ("st_done exp_done mx_done max_read negm_done mt_done mt_read m_pieces_ready pv_done "
                 "o_copied ot_done norm_done v_ready m_own rsum_done joined")
        s = named(names, lambda n: sem("a_" + n))

        def each_pair(engine, body):
            body(0)
            with engine.Fori(1, pairs - 1) as j:
                body(j)
            body(pairs - 1)

        def after(j, w, k, ahead):
            return not (isinstance(j, int) and j == pairs - 1) or k + ahead < 4

        with nc.Block() as block:
            @block.sync
            def _(sp):
                def load_q_unit(buf, half, head):
                    src = a.q_pieces_by_head[:, half, bass.ds(first + head, 1), :, :]
                    for copy in range(PIECES):
                        rows = slice(copy * PIECES * DH, (copy + 1) * PIECES * DH)
                        sp.dma_start(q_stack[buf][rows, :, :].rearrange("r q s -> r (q s)"),
                                     src.rearrange("p x d c -> p (x d) c")).then_inc(q_loaded[buf], 16)

                def load_k(stack, sem, head):
                    for p in range(PIECES):
                        rows = slice(p * PIECES * DH, (p + 1) * PIECES * DH)
                        src = a.k_pieces_by_head[p, bass.ds(first + head, 1), :, :]
                        sp.dma_start(stack[rows, :], src.to_broadcast([PIECES, DH, SEQ])).then_inc(sem, 16)

                load_k(k_max[0], km_loaded[0], 0)
                load_q_unit(0, 0, 0)
                load_q_unit(1, 1, 0)
                load_k(k_st[0], kt_loaded[0], 0)
                load_k(k_max[1], km_loaded[1], 1)
                load_q_unit(2, 0, 1)

                def body(j):
                    for k in range(4):
                        w = 4 * j + k
                        if after(j, w, k, 3):
                            wait(sp, s.st_done, 2 * STEPS * w)
                            load_q_unit((k + 3) % 4, (k + 3) % 2, 2 * j + (k + 3) // 2)
                        if k % 2 == 0 and after(j, w, k, 2):
                            wait(sp, s.st_done, 2 * STEPS * w)
                            load_k(k_st[(k // 2 + 1) % 2], kt_loaded[(k // 2 + 1) % 2], 2 * j + k // 2 + 1)
                            if after(j, w, k, 4):
                                sp.wait_ge(s.mx_done, MAXES * (w + 2))
                                load_k(k_max[k // 2], km_loaded[k // 2], 2 * j + k // 2 + 2)
                        if after(j, w, k, 1):
                            send_max((k + 1) % 4, (k + 1) % 2, w + 1)
                def send_max(buf, par, w):
                    sp.wait_ge(s.m_pieces_ready, w + 1)
                    for p in range(PIECES):
                        row = q_stack[buf][PROD_ROWS + p:PROD_ROWS + p + 1, :, :]
                        sp.dma_start(row.rearrange("o q (t c) -> o (q t) c", c=P),
                                     m_pieces[par][:, p, :]).then_inc(m_loaded[par], 16)
                send_max(0, 0, 0)
                each_pair(sp, body)

            @block.gpsimd
            def _(pool):
                beside.start(pool)

                def join(w, k, head):
                    wait_own(pool, g.passed, s.norm_done, w + 1)
                    wait_own(pool, g.passed, s.joined, w)
                    rows = g.acc[:, b * 8 + k % 2 * 4:b * 8 + k % 2 * 4 + 4, :].rearrange("p t (q h d) -> p t q h d", q=NQ, d=DH)
                    rows = rows[:, :, :, bass.ds(head, 1), :].rearrange("p t q x d -> p t q (x d)")
                    pool.tensor_tensor(rows, rows, out[k][:, :, :, :], ALU.add).then_inc(s.joined, 1)

                def body(j):
                    for u in range(2):
                        head = 2 * j + u
                        wait_own(pool, g.passed, s.pv_done, 2 * STEPS * (head - 1))
                        pool.tensor_copy(v_stack[u][:, :, 0:DH],
                                         g.vp[:].rearrange("p b h t d -> p (b h) t d")[:, bass.ds(first + head, 1), :, :]
                                         .rearrange("p x t d -> p (x t) d")).then_inc(s.v_ready, 1)
                        beside.head(pool, head)
                        if u == 1 or not isinstance(j, int) or j > 0:
                            for k in range(2):
                                join(2 * (head - 1) + k, (2 * (u + 1) + k) % 4, head - 1)
                each_pair(pool, body)
                for k in range(2):
                    join(units - 2 + k, 2 + k, heads - 1)
                beside.end(pool)

            @block.tensor
            def _(pe):
                def max_scores(buf, w, j2, m):
                    tile, half = m // 2, m % 2
                    if m == 0:
                        pe.wait_ge(q_loaded[buf], 16 * PIECES * (j2 + 1))
                        pe.wait_ge(km_loaded[buf // 2], 16 * PIECES * (j2 + 1))
                    wait(pe, s.max_read, MAXES * w + (m - 2 if m > 2 else (-1, 0, -2)[m]))
                    if m == TURN_MAX:
                        wait(pe, s.mt_read, w)
                    if m == TURN_OUT:
                        wait(pe, s.norm_done, w - 2)
                    q, t = tile // CHUNK_TILES, tile % CHUNK_TILES
                    pe.matmul(mx_bank[m % 3][:, :], q_stack[buf][:, q, t * P:(t + 1) * P],
                              k_max[buf // 2][:, half * HALF:(half + 1) * HALF],
                              start=True, stop=True).then_inc(s.mx_done, 1)

                def turn_max(par, w, ahead):
                    pe.wait_ge(s.negm_done, w + 1)
                    if ahead:
                        pe.wait_ge(s.max_read, MAXES * (w + 1) + TURN_MAX - 2)
                    pe.transpose(m_bank[0:NQ * CHUNK_TILES, 0:P], neg_max[par][:, :], g.ident[:]).then_inc(s.mt_done, 1)

                def scores(k, w, j, n, pair, between=None):
                    wait(pe, s.exp_done, 2 * STEPS * w + 2 * n + pair - 1)
                    if n == 0 and pair == 0:
                        pe.wait_ge(m_loaded[k % 2], 16 * PIECES * (2 * j + k // 2 + 1))
                        pe.wait_ge(kt_loaded[k // 2], 16 * PIECES * (j + 1))
                    for q in range(2):
                        if q and between:
                            between()
                        last = pe.matmul(st_bank[pair][:, q, :], k_st[k // 2][:, n * P:(n + 1) * P],
                                         q_stack[k][:, 2 * pair + q, :], start=True, stop=True)
                    last.then_inc(s.st_done, 1)

                def values(u, w, n, head):
                    pe.wait_ge(s.exp_done, 2 * STEPS * w + 2 * n + 2)
                    if n == 0:
                        wait(pe, s.o_copied, w)
                        pe.wait_ge(s.v_ready, head + 1)
                    for q in range(NQ):
                        last = pe.matmul(o_bank[32 * q:32 * q + 32, :], v_stack[u][:, n, :], probs[n % 2][:, q, :],
                                         start=(n == 0), stop=(n == STEPS - 1))
                    last.then_inc(s.pv_done, 1)

                def turn_outputs(par, w, ahead):
                    pe.wait_ge(s.o_copied, w + 1)
                    wait(pe, s.norm_done, w)
                    if ahead:
                        pe.wait_ge(s.max_read, MAXES * (w + 3) + TURN_OUT - 2)
                    for t in range(CHUNK_TILES):
                        last = pe.transpose(t_bank[:, t * P:(t + 1) * P], o_sb[par][:, t * P:(t + 1) * P], g.ident[:])
                    last.then_inc(s.ot_done, 1)

                for m in range(MAXES):
                    max_scores(0, 0, 0, m)
                for m in range(MAXES):
                    if m == TURN_MAX - 1:
                        turn_max(0, 0, True)
                    max_scores(1, 1, 0, m)

                def body(j):
                    for k in range(4):
                        w = 4 * j + k
                        ahead = after(j, w, k, 2)
                        buf, j2 = (k + 2) % 4, j + (k + 2) // 4
                        for n in range(STEPS):
                            def maxima(m):
                                if ahead:
                                    max_scores(buf, w + 2, j2, 4 * n + m)
                            maxima(0)
                            scores(k, w, j, n, 0)
                            maxima(1)
                            scores(k, w, j, n, 1, lambda: maxima(2))
                            if 4 * n + 4 == TURN_MAX and after(j, w, k, 1):
                                turn_max((k + 1) % 2, w + 1, ahead)
                            if 4 * n + 4 == TURN_OUT and not (isinstance(j, int) and j == 0 and k == 0):
                                turn_outputs((k + 1) % 2, w - 1, ahead)
                            maxima(3)
                            if n > 0:
                                values(k // 2, w, n - 1, 2 * j + k // 2)
                            elif not (isinstance(j, int) and j == 0 and k == 0):
                                values((k + 3) % 4 // 2, w - 1, STEPS - 1, 2 * j + (k - 1) // 2)
                each_pair(pe, body)
                values(1, units - 1, STEPS - 1, heads - 1)
                turn_outputs((units - 1) % 2, units - 1, False)

            @block.scalar
            def _(act):
                beside.loads(act)

                def copy_outputs(par, w):
                    act.wait_ge(s.pv_done, STEPS * (w + 1))
                    wait(act, s.ot_done, w - 1)
                    act.activation(o_sb[par][:, :], o_bank[:, :], ACT.Copy).then_inc(s.o_copied, 1)

                def body(j):
                    for k in range(4):
                        w = 4 * j + k
                        for n in range(STEPS):
                            for pair in range(2):
                                act.wait_ge(s.st_done, 2 * STEPS * w + 2 * n + pair + 1)
                                wait(act, s.pv_done, STEPS * w + n - 1)
                                act.activation(probs[n % 2][:, 2 * pair:2 * pair + 2, :], st_bank[pair][:, :, :],
                                               ACT.Exp, scale=SM_SCALE).then_inc(s.exp_done, 1)
                            if n == 0 and not (isinstance(j, int) and j == 0 and k == 0):
                                copy_outputs((k + 1) % 2, w - 1)
                each_pair(act, body)
                copy_outputs((units - 1) % 2, units - 1)

            @block.vector
            def _(dve):
                def take_max(w, m):
                    if m == 0:
                        wait(dve, s.negm_done, w)
                    dve.wait_ge(s.mx_done, MAXES * w + m + 1)
                    dve.tensor_reduce(partial_max[:, m // 2, m % 2:m % 2 + 1], mx_bank[m % 3][:, :], AX.X,
                                      ALU.max).then_inc(s.max_read, 1)

                def join_max(par, w):
                    dve.wait_ge(s.max_read, MAXES * (w + 1))
                    dve.tensor_reduce(neg_max[par][:, :], partial_max[:, :, :], AX.X, ALU.max,
                                      negate=True).then_inc(s.negm_done, 1)

                def split_max(par, w, sent, links):
                    own = Chain(dve, s.m_own, links)
                    dve.wait_ge(s.mt_done, w + 1)
                    wait(dve, m_loaded[par], 16 * PIECES * sent)
                    m, turned = m_pieces[par], m_bank[0:NQ * CHUNK_TILES, 0:P]
                    own.link(dve.tensor_copy(m[:, 0, :], turned))
                    dve.tensor_tensor(m_rest[:, :], turned, m[:, 0, :], ALU.subtract).then_inc(s.mt_read, 1)
                    dve.wait_ge(s.mt_read, w + 1)
                    own.link(dve.tensor_copy(m[:, 1, :], m_rest[:, :]))
                    dve.tensor_tensor(m[:, 2, :], m_rest[:, :], m[:, 1, :], ALU.subtract).then_inc(s.m_pieces_ready, 1)

                def normalise(w, k):
                    dve.wait_ge(s.ot_done, w + 1)
                    turned = t_bank[:, :].rearrange("p (t q c) -> p t q c", t=CHUNK_TILES, q=NQ)
                    dve.reciprocal(rsum[:, :, :], turned[:, :, :, DH]).then_inc(s.rsum_done, 1)
                    dve.wait_ge(s.rsum_done, w + 1)
                    wait(dve, s.joined, w - 3)
                    dve.tensor_tensor(out[k][:, :, :, :], turned[:, :, :, 0:DH],
                                      rsum[:, :, :].unsqueeze(3).to_broadcast([P, CHUNK_TILES, NQ, DH]),
                                      ALU.mult).then_inc(s.norm_done, 1)

                for m in range(MAXES):
                    take_max(0, m)
                join_max(0, 0)
                for m in range(MAXES):
                    if m == TURN_MAX - 1:
                        split_max(0, 0, 0, 0)
                    take_max(1, m)
                join_max(1, 1)

                def body(j):
                    for k in range(4):
                        w = 4 * j + k
                        for m in range(MAXES):
                            if m == TURN_MAX - 1 and after(j, w, k, 1):
                                split_max((k + 1) % 2, w + 1, 2 * j + (k + 1) // 2, 2 * (w + 1))
                            if m == TURN_OUT - 1 and not (isinstance(j, int) and j == 0 and k == 0):
                                normalise(w - 1, (k + 3) % 4)
                            if after(j, w, k, 2):
                                take_max(w + 2, m)
                        if after(j, w, k, 2):
                            join_max(k % 2, w + 2)
                each_pair(dve, body)
                normalise(units - 1, 3)


EXPERTS, TOP_K, INNER = 32, 4, 128
ROW_TILES = TOKENS * TOP_K // P + EXPERTS


def dispatch(nc, g, a):
    with ExitStack() as ctx:
        sb = lambda name, shape, dt=F32: ctx.enter_context(nc.sbuf_tensor(name, shape, dt))
        sem = lambda name: ctx.enter_context(nc.semaphore(name))
        prefix = ctx.enter_context(nc.psum_tensor("prefix", [P, TILES, EXPERTS], F32))
        total = ctx.enter_context(nc.psum_tensor("total", [P, TILES, EXPERTS], F32))
        top = sb("top", [P, TILES, 8])
        top_at = sb("top_at", [P, TILES, 8], U32)
        at = sb("at", [P, TOP_K, TILES])
        less = sb("less", [P, TILES, TOP_K])
        power = sb("power", [P, TILES, TOP_K])
        norm = sb("norm", [P, TILES, 2])
        lane = sb("lane", [P, EXPERTS])
        tile_no = sb("tile_no", [P, ROW_TILES])
        before = sb("before", [P, P])
        ones = sb("ones", [P, P])
        zeros = sb("zeros", [ROW_TILES, P])
        chosen = sb("chosen", [P, TOP_K, TILES, EXPERTS])
        mask = sb("mask", [P, TILES, EXPERTS])
        slot_of = sb("slot_of", [P, TILES, EXPERTS])
        start = sb("start", [P, 6, EXPERTS])
        tiles_i = sb("tiles_i", [P, EXPERTS], I32)
        picked = sb("picked", [P, TOP_K, TILES, EXPERTS])
        slot_f = sb("slot_f", [P, TOP_K, TILES])
        ended = sb("ended", [P, ROW_TILES, EXPERTS])
        expert_f = sb("expert_f", [P, 2, ROW_TILES])
        names = "consts table_zeroed top_done less_ready power_ready own mask_ready counted slots_ready"
        s = named(names, lambda n: sem("d_" + n))

        with nc.Block() as block:
            @block.gpsimd
            def _(pool):
                pool.memset(zeros[:], 0.0).then_inc(s.consts, 1)
                pool.iota(lane[:], [[1, EXPERTS]], base=0, channel_multiplier=0,
                          allow_small_or_imprecise_dtypes=True).then_inc(s.consts, 1)
                pool.iota(tile_no[:], [[1, ROW_TILES]], base=0, channel_multiplier=0,
                          allow_small_or_imprecise_dtypes=True).then_inc(s.consts, 1)
                pool.iota(g.row_no[:], [[P, TILES]], base=0, channel_multiplier=1,
                          allow_small_or_imprecise_dtypes=True).then_inc(s.consts, 1)
                pool.memset(ones[:], 1.0).then_inc(s.consts, 1)
                pool.wait_ge(s.consts, 5)
                pool.affine_select(out=before[:], in_=ones[:], compare_op=ALU.is_gt, fill=0.0, base=0,
                                   pattern=[[1, P]], channel_multiplier=-1).then_inc(s.consts, 1)
            @block.sync
            def _(sp):
                sp.wait_ge(s.consts, 1)
                sp.dma_start(a.slot_row.rearrange("(j p) o -> j (p o)", p=P), zeros[:]).then_inc(s.table_zeroed, 16)
                sp.wait_ge(s.table_zeroed, 16)

            @block.scalar
            def _(act):
                act.wait_ge(s.less_ready, 1)
                act.activation(power[:], less[:], ACT.Exp).then_inc(s.power_ready, 1)

            @block.tensor
            def _(pe):
                pe.wait_ge(s.mask_ready, 1)
                pe.wait_ge(s.consts, 6)
                flat = mask[:].rearrange("p t e -> p (t e)")
                pe.matmul(prefix[:].rearrange("p t e -> p (t e)"), before[:], flat, start=True, stop=True).then_inc(s.counted, 1)
                pe.matmul(total[:].rearrange("p t e -> p (t e)"), ones[:], flat, start=True, stop=True).then_inc(s.counted, 1)

            @block.vector
            def _(dve):
                own = Chain(dve, s.own)
                for t in range(TILES):
                    dve.max(top[:, t, :], g.logits[:, t, :]).then_inc(s.top_done, 1)
                dve.wait_ge(s.top_done, TILES)
                for t in range(TILES):
                    last = dve.max_index(top_at[:, t, :], top[:, t, :], g.logits[:, t, :])
                own.link(last)
                dve.tensor_tensor(less[:], top[:, :, 0:TOP_K], top[:, :, 0:1].to_broadcast([P, TILES, TOP_K]),
                                  ALU.subtract).then_inc(s.less_ready, 1)
                own.link(dve.tensor_copy(at[:], top_at[:, :, 0:TOP_K].rearrange("p t k -> p k t")))
                dve.wait_ge(s.consts, 6)
                for k in range(TOP_K):
                    own.link(dve.tensor_tensor(chosen[:, k, :, :], lane[:].unsqueeze(1).to_broadcast([P, TILES, EXPERTS]),
                                               at[:, k, :].unsqueeze(2).to_broadcast([P, TILES, EXPERTS]), ALU.is_equal))
                own.link(dve.tensor_tensor(mask[:], chosen[:, 0, :, :], chosen[:, 1, :, :], ALU.add))
                own.link(dve.tensor_tensor(mask[:], mask[:], chosen[:, 2, :, :], ALU.add))
                dve.tensor_tensor(mask[:], mask[:], chosen[:, 3, :, :], ALU.add).then_inc(s.mask_ready, 1)
                dve.wait_ge(s.power_ready, 1)
                own.link(dve.tensor_reduce(norm[:, :, 0], power[:], AX.X, ALU.add))
                own.link(dve.reciprocal(norm[:, :, 1], norm[:, :, 0]))
                own.link(dve.tensor_tensor(g.weight[:], power[:], norm[:, :, 1:2].to_broadcast([P, TILES, TOP_K]), ALU.mult))
                dve.wait_ge(s.counted, 2)
                own.link(dve.memset(slot_of[:, 0, :], 0.0))
                for t in range(1, TILES):
                    own.link(dve.tensor_tensor(slot_of[:, t, :], total[:, t - 1, :], slot_of[:, t - 1, :], ALU.add))
                own.link(dve.tensor_tensor(start[:, 0, :], total[:, TILES - 1, :], slot_of[:, TILES - 1, :], ALU.add))
                own.link(dve.tensor_scalar(tiles_i[:], start[:, 0, :], float(P - 1), None, ALU.add))
                own.link(dve.tensor_scalar(tiles_i[:], tiles_i[:], 7, None, ALU.arith_shift_right))
                own.link(dve.tensor_copy(start[:, 1, :], tiles_i[:]))
                own.link(dve.tensor_tensor_scan(start[:, 2, :], ones[:, 0:EXPERTS], start[:, 1, :], 0.0, ALU.mult, ALU.add))
                own.link(dve.tensor_tensor(start[:, 3, :], start[:, 2, :], start[:, 1, :], ALU.subtract))
                own.link(dve.tensor_scalar(start[:, 4, :], start[:, 3, :], float(P), None, ALU.mult))
                own.link(dve.tensor_tensor(slot_of[:], slot_of[:], prefix[:], ALU.add))
                own.link(dve.tensor_tensor(slot_of[:], slot_of[:], start[:, 4:5, :].to_broadcast([P, TILES, EXPERTS]), ALU.add))
                for k in range(TOP_K):
                    own.link(dve.tensor_tensor(picked[:, k, :, :], chosen[:, k, :, :], slot_of[:], ALU.mult))
                own.link(dve.tensor_reduce(slot_f[:].rearrange("p k t -> p (k t)"),
                                           picked[:].rearrange("p k t e -> p (k t) e"), AX.X, ALU.add))
                dve.tensor_copy(g.slot[:], slot_f[:]).then_inc(s.slots_ready, 1)
                own.link(dve.tensor_tensor(ended[:], tile_no[:].unsqueeze(2).to_broadcast([P, ROW_TILES, EXPERTS]),
                                           start[:, 2:3, :].to_broadcast([P, ROW_TILES, EXPERTS]), ALU.is_ge))
                own.link(dve.tensor_reduce(expert_f[:, 0, :], ended[:], AX.X, ALU.add))
                own.link(dve.tensor_scalar(g.tile_expert[:], expert_f[:, 0, :], float(EXPERTS - 1), None, ALU.min))


class NumberSlots:

    def __init__(self, nc, g, a, ctx):
        self.g, self.a = g, a
        self.slots_now = [ctx.enter_context(nc.sbuf_tensor(f"slots_now{i}", [P, 1], I32)) for i in range(TOP_K)]
        self.row_now = ctx.enter_context(nc.sbuf_tensor("row_now", [P, 2], F32))
        self.now_ready = ctx.enter_context(nc.semaphore("now_ready"))
        self.scattered = ctx.enter_context(nc.semaphore("scattered"))

    def loads(self, act):
        pass

    def start(self, pool):
        pass

    def head(self, pool, head):
        g, a = self.g, self.a
        for u in range(TILES // NKV):
            t = head * (TILES // NKV) + u
            wait_own(pool, g.passed, self.scattered, t * (16 * TOP_K))
            for k in range(TOP_K):
                pool.tensor_copy(self.slots_now[k][:], g.slot[:, k, bass.ds(t, 1)]).then_inc(self.now_ready, 1)
            pool.tensor_copy(self.row_now[:, 0:1], g.row_no[:, bass.ds(t, 1)]).then_inc(self.now_ready, 1)
            wait_own(pool, g.passed, self.now_ready, (t + 1) * (TOP_K + 1))
            for k in range(TOP_K):
                pool.indirect_dma_start(a.slot_row, bass.IndirectOffsetOnAxis(self.slots_now[k][:], 0),
                                        self.row_now[:, 0:1], None).then_inc(self.scattered, 16)

    def end(self, pool):
        pool.wait_ge(self.scattered, 16 * TOP_K * TILES)


class AddExperts:

    def __init__(self, nc, g, a, ctx):
        self.g, self.a = g, a
        sb = lambda name, shape, dt=F32: ctx.enter_context(nc.sbuf_tensor(name, shape, dt))
        sem = lambda name: ctx.enter_context(nc.semaphore(name))
        self.slots_now = [sb(f"c_slots{i}", [P, 1], I32) for i in range(TOP_K)]
        self.part = [sb(f"part{i}", [P, D]) for i in range(TOP_K)]
        self.slot_at, self.weighted, self.added = sem("c_slot_at"), sem("c_weighted"), sem("c_added")
        self.gathered = [sem(f"c_gathered{i}") for i in range(TOP_K)]
        self.loaded, self.zeroed, self.cut = sem("l1_loaded"), sem("l1_zeroed"), sem("l1_cut")

    def loads(self, act):
        second_weights(act, self.g, self.a, self.loaded)

    def start(self, pool):
        second_masks(pool, self.g, self.zeroed, self.cut)

    def head(self, pool, head):
        g, a = self.g, self.a
        for u in range(TILES // NKV):
            t = head * (TILES // NKV) + u
            wait_own(pool, g.passed, self.added, TOP_K * t)
            for k in range(TOP_K):
                pool.tensor_copy(self.slots_now[k][:], g.slot[:, k, bass.ds(t, 1)]).then_inc(self.slot_at, 1)
            wait_own(pool, g.passed, self.slot_at, TOP_K * (t + 1))
            for k in range(TOP_K):
                pool.indirect_dma_start(self.part[k][:], None, a.expert_out,
                                        bass.IndirectOffsetOnAxis(self.slots_now[k][:], 0)).then_inc(self.gathered[k], 16)
            row = g.acc[:, bass.ds(t, 1), :].rearrange("p x c -> p (x c)")
            for k in range(TOP_K):
                wait_own(pool, g.passed, self.gathered[k], 16 * (t + 1))
                weight = g.weight[:, bass.ds(t, 1), k:k + 1].rearrange("p x k -> p (x k)").to_broadcast([P, D])
                pool.tensor_tensor(self.part[k][:], self.part[k][:], weight, ALU.mult).then_inc(self.weighted, 1)
            for k in range(TOP_K):
                wait_own(pool, g.passed, self.weighted, TOP_K * t + k + 1)
                wait_own(pool, g.passed, self.added, TOP_K * t + k)
                pool.tensor_tensor(row, row, self.part[k][:], ALU.add).then_inc(self.added, 1)
        wait_own(pool, g.passed, self.added, TOP_K * (TILES // NKV) * (head + 1))

    def end(self, pool):
        pool.wait_ge(self.loaded, SECOND_LOADS)


def read_table(nc, g, a):
    with ExitStack() as ctx:
        rows_back = ctx.enter_context(nc.sbuf_tensor("rows_back", [ROW_TILES, P], F32))
        turned = ctx.enter_context(nc.psum_tensor("turned", [P, ROW_TILES], F32))
        table_back, table_turned = ctx.enter_context(nc.semaphore("table_back")), ctx.enter_context(nc.semaphore("table_turned"))
        with nc.Block() as block:
            @block.sync
            def _(sp):
                sp.dma_start(rows_back[:], a.slot_row.rearrange("(j p) o -> j (p o)", p=P)).then_inc(table_back, 16)

            @block.tensor
            def _(pe):
                pe.wait_ge(table_back, 16)
                pe.transpose(turned[:, :], rows_back[:], g.ident[0:ROW_TILES, 0:ROW_TILES]).then_inc(table_turned, 1)

            @block.vector
            def _(dve):
                dve.wait_ge(table_turned, 1)
                dve.tensor_copy(g.tile_rows[:], turned[:]).then_inc(table_turned, 1)


def experts(nc, g, a):
    STAGES = 4
    with ExitStack() as ctx:
        sb = lambda name, shape, dt=F32: ctx.enter_context(nc.sbuf_tensor(name, shape, dt))
        sem = lambda name: ctx.enter_context(nc.semaphore(name))
        two = lambda name, cols: [ctx.enter_context(nc.psum_tensor(f"{name}{i}", [P, cols], F32)) for i in range(2)]
        xt_ps, gu_ps, ht_ps, y_ps = two("xt_ps", D), two("gu_ps", 2 * INNER), two("ht_ps", INNER), two("y_ps", D)
        rows_now = [sb(f"rows_now{i}", [P, 1], I32) for i in range(4)]
        rows = [sb(f"rows{i}", [P, D]) for i in range(4)]
        xt = [sb(f"xt{i}", [P, KD, P]) for i in range(2)]
        silu = [sb(f"silu{i}", [P, INNER]) for i in range(2)]
        h = [sb(f"h{i}", [P, INNER]) for i in range(2)]
        ht = [sb(f"ht{i}", [P, INNER]) for i in range(2)]
        y = [sb(f"y{i}", [P, D]) for i in range(4)]
        names = ("rows_at xt_turned xt_ready gu_done silu_done h_ready h_turned ht_ready y_done y_ready")
        s = named(names, lambda n: sem("e_" + n))
        gathered = [sem(f"e_gathered{i}") for i in range(4)]
        stored = [sem(f"e_stored{i}") for i in range(4)]

        def tiles(engine, body, lag):
            for n in range(4):
                body(0, n, n)
            with engine.Fori(1, ROW_TILES // 4) as j:
                for u in range(4):
                    body(j, 4 * j + u, u)
            for n in range(ROW_TILES, ROW_TILES + lag):
                body(n // 4, n, n % 4)

        with nc.Block() as block:
            @block.gpsimd
            def _(pool):
                def body(j, n, u):
                    wait_own(pool, g.passed, s.xt_turned, n - 3)
                    pool.tensor_copy(rows_now[u][:], g.tile_rows[:, bass.ds(n, 1)]).then_inc(s.rows_at, 1)
                    wait_own(pool, g.passed, s.rows_at, n + 1)
                    pool.indirect_dma_start(rows[u][:], None, a.xn_flat,
                                            bass.IndirectOffsetOnAxis(rows_now[u][:], 0)).then_inc(gathered[u], 16)
                tiles(pool, body, 0)

            @block.tensor
            def _(pe):
                pe.wait_ge(g.experts_loaded, 32)

                def expert_of(m):
                    return nc.values_load(g.tile_expert[0:1, bass.ds(m, 1)], engines=[mybir.EngineType.PE], min_val=0,
                                          max_val=EXPERTS - 1, skip_runtime_bounds_check_because="a count of experts, "
                                          "clamped to the last one")

                def body(j, n, u):
                    whole = not isinstance(n, int)
                    gate_tile, down_tile = whole or 0 <= n - 1 < ROW_TILES, whole or 0 <= n - 3 < ROW_TILES
                    gate_expert = expert_of(n - 1) if gate_tile else None
                    down_expert = expert_of(n - 3) if down_tile else None
                    if whole or n < ROW_TILES:
                        pe.wait_ge(gathered[u], 16 * (j + 1))
                        wait(pe, s.xt_ready, n - 1)
                        for k in range(KD):
                            last = pe.transpose(xt_ps[u % 2][:, k * P:(k + 1) * P], rows[u][:, k * P:(k + 1) * P], g.ident[:])
                        last.then_inc(s.xt_turned, 1)
                    if gate_tile:
                        m = n - 1
                        pe.wait_ge(s.xt_ready, m + 1)
                        wait(pe, s.h_ready, m - 1)
                        for k in range(KD):
                            last = pe.matmul(gu_ps[(u - 1) % 2][:, :], xt[(u - 1) % 2][:, k, :],
                                             g.wgu[:, bass.ds(gate_expert, 1), k, :].rearrange("p x c -> p (x c)"),
                                             start=(k == 0), stop=(k == KD - 1))
                        last.then_inc(s.gu_done, 1)
                    if whole or 0 <= n - 2 < ROW_TILES:
                        m = n - 2
                        pe.wait_ge(s.h_ready, m + 1)
                        wait(pe, s.ht_ready, m - 1)
                        pe.transpose(ht_ps[u % 2][:, :], h[u % 2][:, :], g.ident[:]).then_inc(s.h_turned, 1)
                    if down_tile:
                        m = n - 3
                        pe.wait_ge(s.ht_ready, m + 1)
                        wait(pe, s.y_ready, m - 1)
                        pe.matmul(y_ps[(u - 3) % 2][:, :], ht[(u - 3) % 2][:, :],
                                  g.wd[:, bass.ds(down_expert, 1), :].rearrange("p x c -> p (x c)"),
                                  start=True, stop=True).then_inc(s.y_done, 1)
                tiles(pe, body, STAGES - 1)

            @block.scalar
            def _(act):
                def body(j, n, u):
                    whole = not isinstance(n, int)
                    if whole or n < ROW_TILES:
                        act.wait_ge(s.xt_turned, n + 1)
                        wait(act, s.gu_done, n - 1)
                        act.activation(xt[u % 2][:].rearrange("p k c -> p (k c)"), xt_ps[u % 2][:, :],
                                       ACT.Copy).then_inc(s.xt_ready, 1)
                    if whole or 0 <= n - 1 < ROW_TILES:
                        m = n - 1
                        act.wait_ge(s.gu_done, m + 1)
                        wait(act, s.h_ready, m - 1)
                        act.activation(silu[(u - 1) % 2][:], gu_ps[(u - 1) % 2][:, 0:INNER], ACT.Silu).then_inc(s.silu_done, 1)
                    if whole or 0 <= n - 2 < ROW_TILES:
                        m = n - 2
                        act.wait_ge(s.h_turned, m + 1)
                        wait(act, s.y_done, m - 1)
                        act.activation(ht[u % 2][:], ht_ps[u % 2][:, :], ACT.Copy).then_inc(s.ht_ready, 1)
                tiles(act, body, 2)

            @block.vector
            def _(dve):
                def body(j, n, u):
                    whole = not isinstance(n, int)
                    if whole or 0 <= n - 1 < ROW_TILES:
                        m = n - 1
                        dve.wait_ge(s.silu_done, m + 1)
                        wait(dve, s.h_turned, m - 1)
                        dve.tensor_tensor(h[(u - 1) % 2][:], gu_ps[(u - 1) % 2][:, INNER:2 * INNER],
                                          silu[(u - 1) % 2][:], ALU.mult).then_inc(s.h_ready, 1)
                    if whole or 0 <= n - 3 < ROW_TILES:
                        m = n - 3
                        dve.wait_ge(s.y_done, m + 1)
                        wait(dve, stored[(u - 3) % 4], 16 * (j if u == 3 else j - 1))
                        dve.tensor_copy(y[(u - 3) % 4][:], y_ps[(u - 3) % 2][:, :]).then_inc(s.y_ready, 1)
                tiles(dve, body, 3)

            @block.sync
            def _(sp):
                def body(j, n, u):
                    sp.wait_ge(s.y_ready, n + 1)
                    sp.dma_start(a.expert_out_tiles[:, bass.ds(n, 1), :].rearrange("p x c -> p (x c)"),
                                 y[u][:]).then_inc(stored[u], 16)
                tiles(sp, body, 0)
                for u in range(4):
                    sp.wait_ge(stored[u], 16 * (ROW_TILES // 4))




HEADS1, DK1 = 16, 16
GROUP = 4
GROUPS = HEADS1 // GROUP
PER_TILE = P // DK1
SCALE1 = DK1 ** -0.5
HIDDEN = 1024
HID_TILES = HIDDEN // P


SECOND_LOADS = 16 * 8


def second_weights(act, g, a, loaded):
    loads = ((g.wqkv1, a.wqkv1), (g.feat, a.feat), (g.fbias, a.fbias), (g.nw, a.nw), (g.wo1, a.wo1),
             (g.wg1, a.wg1), (g.wu1, a.wu1), (g.wd1, a.wd1))
    for dst, src in loads:
        act.dma_start(dst[:], src).then_inc(loaded, 16)
    assert SECOND_LOADS == 16 * len(loads)


def second_masks(pool, g, zeroed, cut):
    pool.memset(g.causal[:], SCALE1).then_inc(zeroed, 1)
    pool.memset(g.same_head[:], 1.0).then_inc(zeroed, 1)
    pool.memset(g.kv_mask[:], SCALE1).then_inc(zeroed, 1)
    pool.memset(g.mean32[:], 1.0 / DK1).then_inc(zeroed, 1)
    pool.memset(g.v_pad[:], 0.0).then_inc(zeroed, 1)
    pool.memset(g.eps[:], EPS).then_inc(zeroed, 1)
    pool.wait_ge(zeroed, 6)
    pool.affine_select(out=g.causal[:], in_=g.causal[:], compare_op=ALU.is_ge, fill=0.0, base=0,
                       pattern=[[1, P]], channel_multiplier=-1).then_inc(cut, 1)
    pool.affine_select(out=g.same_head[:], in_=g.same_head[:], compare_op=ALU.is_ge, fill=0.0, base=0,
                       pattern=[[-DK1, PER_TILE]], channel_multiplier=1).then_inc(cut, 1)
    pool.wait_ge(cut, 2)
    pool.affine_select(out=g.same_head[:], in_=g.same_head[:], compare_op=ALU.is_ge, fill=0.0,
                       base=DK1 - 1, pattern=[[DK1, PER_TILE]], channel_multiplier=-1).then_inc(cut, 1)
    pool.affine_select(out=g.kv_mask[:], in_=g.kv_mask[:], compare_op=ALU.is_ge, fill=0.0, base=0,
                       pattern=[[-DK1, PER_TILE], [0, 32]], channel_multiplier=1).then_inc(cut, 1)
    pool.wait_ge(cut, 4)
    pool.affine_select(out=g.kv_mask[:], in_=g.kv_mask[:], compare_op=ALU.is_ge, fill=0.0,
                       base=DK1 - 1, pattern=[[DK1, PER_TILE], [0, 32]],
                       channel_multiplier=-1).then_inc(cut, 1)
    pool.affine_select(out=g.mean32[:], in_=g.mean32[:], compare_op=ALU.is_ge, fill=0.0, base=0,
                       pattern=[[-32, GROUP], [0, 32]], channel_multiplier=1).then_inc(cut, 1)
    pool.wait_ge(cut, 6)
    pool.affine_select(out=g.mean32[:], in_=g.mean32[:], compare_op=ALU.is_ge, fill=0.0,
                       base=31, pattern=[[32, GROUP], [0, 32]], channel_multiplier=-1).then_inc(cut, 1)


def linear_attention(nc, g, a):
    SUB = CHUNK_TILES
    with ExitStack() as ctx:
        sb = lambda name, shape, dt=F32: ctx.enter_context(nc.sbuf_tensor(name, shape, dt))
        sem = lambda name: ctx.enter_context(nc.semaphore(name))
        bank = [ctx.enter_context(nc.psum_tensor(f"la{i}", [P, HALF], F32)) for i in range(8)]
        xn = sb("l_xn", [P, CHUNK_TILES, D])
        xt = sb("l_xt", [P, KD, HALF])
        qk = sb("l_qk", [P, 4, HALF])
        f2 = sb("l_f2", [P, 4, HALF])
        qkf = sb("l_qkf", [P, 4, HALF])
        kt = sb("l_kt", [P, SUB, KD, P])
        qm = [sb(f"l_qm{i}", [P, PER_TILE, P]) for i in range(2)]
        sm = [sb(f"l_sm{i}", [P, PER_TILE, P]) for i in range(2)]
        kv = sb("l_kv", [P, KD, 2 * P])
        kv_new = sb("l_kv_new", [P, KD, 2 * P])
        sq = sb("l_sq", [P, GROUPS, P])
        ln = sb("l_ln", [P, GROUPS, P])
        rs = sb("l_rs", [P, GROUPS, P])
        on = sb("l_on", [P, GROUPS, P])
        names = ("xn_ready xt_ps xt_ready xt_kept qk_ps qk_ready feat_ps f2_ready feat_ready v_ps v_ready kt_ps kt_ready "
                 "qm_ready sc_ps sm_ready kv_ps kv_cut kv_ready kv_zero o_ps sq_ready msq_ps ln_ready rs_ready on_ready "
                 "wo_ps acc_ready")
        s = named(names, lambda n: sem("l_s_" + n))

        def chunks(engine, body, behind=None):
            with engine.Fori(0, BATCH) as b:
                with engine.Fori(0, SEQ // HALF) as half:
                    body(b, b * 2 + half)
                if behind:
                    behind(b)

        with nc.Block() as block:
            @block.tensor
            def _(pe):
                def body(b, n):
                    pe.wait_ge(s.xn_ready, n * 4 + 4)
                    pe.wait_ge(s.acc_ready, n * SUB)
                    pe.wait_ge(s.sm_ready, n * SUB * 2)
                    pe.wait_ge(s.kv_cut, n * SUB)
                    for k in range(KD):
                        for t in range(CHUNK_TILES):
                            last = pe.transpose(bank[k][:, t * P:(t + 1) * P], xn[:, t, k * P:(k + 1) * P], g.ident[:])
                        last.then_inc(s.xt_ps, 1)
                    pe.wait_ge(s.xt_ready, n * 2 + 2)
                    for c in range(4):
                        for k in range(KD):
                            last = pe.matmul(bank[2 + c][:, :], g.wqkv1[:, k, c * P:(c + 1) * P], xt[:, k, :],
                                             start=(k == 0), stop=(k == KD - 1))
                        last.then_inc(s.qk_ps, 1)
                    for t in range(CHUNK_TILES):
                        for k in range(KD):
                            last = pe.matmul(bank[6 + t // 2][:, t % 2 * D:(t % 2 + 1) * D], xt[:, k, t * P:(t + 1) * P],
                                             g.wqkv1[:, k, 2 * D:3 * D], start=(k == 0), stop=(k == KD - 1))
                        if t % 2:
                            last.then_inc(s.v_ps, 1)
                    for c in range(4):
                        pe.wait_ge(s.qk_ready, n * 4 + (1, 2, 4, 4)[c])
                        if c == 3:
                            pe.wait_ge(s.v_ready, n * 2 + 2)
                        for f in range(2):
                            last = pe.matmul(bank[2 * c + f][:, :], g.feat[:, c // 2 * 2 + f, :], qk[:, c, :],
                                             start=True, stop=True)
                        last.then_inc(s.feat_ps, 1)
                    pe.wait_ge(s.feat_ready, n * 4 + 4)
                    for t in range(SUB):
                        for c in range(KD):
                            last = pe.transpose(bank[t // 2][:, (t % 2 * 2 + c) * P:(t % 2 * 2 + c + 1) * P],
                                                qkf[:, 2 + c, t * P:(t + 1) * P], g.ident[:])
                        if t % 2:
                            last.then_inc(s.kt_ps, 1)

                    def scores(u):
                        t, c = u // 2, u % 2
                        pe.wait_ge(s.qm_ready, n * 2 * SUB + u + 1)
                        if u > 1:
                            pe.wait_ge(s.sm_ready, n * 2 * SUB + u - 1)
                        for half in range(2):
                            last = pe.matmul(bank[4 + 2 * c + half][:, :], qkf[:, 2 + c, t * P:(t + 1) * P],
                                             qm[c][:, 4 * half:4 * half + 4, :], start=True, stop=True)
                        last.then_inc(s.sc_ps, 1)

                    def outputs(u):
                        t, c = u // 2, u % 2
                        if c == 0:
                            pe.wait_ge(s.kv_ready, n * SUB + t)
                            pe.wait_ge(s.on_ready, n * SUB + t)
                        if u == 0:
                            pe.wait_ge(s.kv_zero, b + 1)
                            pe.wait_ge(s.kt_ready, n * 2 + 2)
                        pe.wait_ge(s.sm_ready, n * 2 * SUB + u + 1)
                        for gr in (2 * c, 2 * c + 1):
                            o = bank[0][:, gr * P:(gr + 1) * P]
                            pe.matmul(o, kv[:, c, gr % 2 * P:(gr % 2 + 1) * P], qkf[:, c, t * P:(t + 1) * P],
                                      start=True, stop=False, skip_group_check=True)
                            for h in range(GROUP):
                                last = pe.matmul(o[32 * h:32 * h + 32, :], g.v_pad[:, t, gr * GROUP + h, :],
                                                 sm[c][:, gr % 2 * GROUP + h, :], start=False, stop=True,
                                                 skip_group_check=True)
                        if c:
                            last.then_inc(s.o_ps, 1)

                    def state(t):
                        pe.wait_ge(s.kv_cut, n * SUB + t)
                        for c in range(KD):
                            last = pe.matmul(bank[2][:, c * 2 * P:(c + 1) * 2 * P], kt[:, t, c, :],
                                             g.v_pad[:, t, c * PER_TILE:(c + 1) * PER_TILE, :], start=True, stop=True)
                        last.then_inc(s.kv_ps, 1)

                    def mean_square(t):
                        pe.wait_ge(s.sq_ready, n * SUB + t + 1)
                        pe.wait_ge(s.ln_ready, n * SUB + t)
                        pe.matmul(bank[3][:, :], g.mean32[:], sq[:].rearrange("p g c -> p (g c)"),
                                  start=True, stop=True).then_inc(s.msq_ps, 1)

                    def project_out(t):
                        pe.wait_ge(s.on_ready, n * SUB + t + 1)
                        pe.wait_ge(s.acc_ready, n * SUB + t)
                        for gr in range(GROUPS):
                            last = pe.matmul(bank[1][:, 0:D], on[:, gr, :], g.wo1[:, gr, :],
                                             start=(gr == 0), stop=(gr == GROUPS - 1))
                        last.then_inc(s.wo_ps, 1)

                    scores(0)
                    for t in range(SUB):
                        scores(2 * t + 1)
                        outputs(2 * t)
                        if t + 1 < SUB:
                            scores(2 * t + 2)
                        outputs(2 * t + 1)
                        state(t)
                        mean_square(t)
                        project_out(t)

                chunks(pe, body)

            @block.scalar
            def _(act):
                def body(b, n):
                    act.wait_ge(s.v_ps, n * 2)
                    act.wait_ge(s.xt_kept, n)
                    for k in range(KD):
                        act.wait_ge(s.xt_ps, n * 2 + k + 1)
                        act.activation(xt[:, k, :], bank[k][:, :], ACT.Copy).then_inc(s.xt_ready, 1)
                    for c in range(4):
                        act.wait_ge(s.qk_ps, n * 4 + c + 1)
                        act.activation(qk[:, c, :], bank[2 + c][:, :], ACT.Copy).then_inc(s.qk_ready, 1)
                    act.wait_ge(s.kv_ps, n * SUB)
                    for i in range(2):
                        act.wait_ge(s.v_ps, n * 2 + i + 1)
                        act.activation(g.v_pad[:, 2 * i:2 * i + 2, :, 0:DK1].rearrange("p t h e -> p (t h) e"),
                                       bank[6 + i][:, :].rearrange("p (x e) -> p x e", e=DK1), ACT.Copy).then_inc(s.v_ready, 1)
                    for c in range(4):
                        act.wait_ge(s.feat_ps, n * 4 + c + 1)
                        act.activation(f2[:, c, :], bank[2 * c + 1][:, :], ACT.Identity,
                                       bias=g.fbias[:, c // 2 * 2 + 1:c // 2 * 2 + 2]).then_inc(s.f2_ready, 1)
                    for i in range(2):
                        act.wait_ge(s.kt_ps, n * 2 + i + 1)
                        act.activation(kt[:, 2 * i:2 * i + 2, :, :].rearrange("p t c m -> p (t c m)"), bank[i][:, :],
                                       ACT.Copy).then_inc(s.kt_ready, 1)
                    for t in range(SUB):
                        act.wait_ge(s.o_ps, n * SUB + t + 1)
                        act.activation(sq[:].rearrange("p g c -> p (g c)"), bank[0][:, :], ACT.Square).then_inc(s.sq_ready, 1)
                        act.wait_ge(s.msq_ps, n * SUB + t + 1)
                        act.wait_ge(s.rs_ready, n * SUB + t)
                        act.activation(ln[:].rearrange("p g c -> p (g c)"), bank[3][:, :], ACT.Ln,
                                       bias=g.eps[:]).then_inc(s.ln_ready, 1)
                        act.wait_ge(s.ln_ready, n * SUB + t + 1)
                        act.wait_ge(s.on_ready, n * SUB + t)
                        act.activation(rs[:].rearrange("p g c -> p (g c)"), ln[:].rearrange("p g c -> p (g c)"), ACT.Exp,
                                       scale=-0.5).then_inc(s.rs_ready, 1)
                chunks(act, body)

            @block.vector
            def _(dve):
                def body(b, n):
                    dve.wait_ge(s.xt_ps, n * 2)
                    for t in range(CHUNK_TILES):
                        dve.tensor_scalar(xn[:, t, :], g.acc[:, bass.ds(n * 4 + t, 1), :],
                                          g.mean_var[:, bass.ds(n * 4 + t, 1), 0:1].rearrange("p a b -> p (a b)"),
                                          g.rstd[:, bass.ds(n * 4 + t, 1)],
                                          ALU.subtract, ALU.mult).then_inc(s.xn_ready, 1)
                    for c in range(4):
                        dve.wait_ge(s.f2_ready, n * 4 + c + 1)
                        i = c // 2 * 2
                        dve.scalar_tensor_tensor(out=qkf[:, c, :], in0=bank[2 * c][:, :], scalar=g.fbias[:, i:i + 1],
                                                 in1=f2[:, c, :], op0=ALU.add, op1=ALU.mult).then_inc(s.feat_ready, 1)
                    dve.wait_ge(s.feat_ready, n * 4 + 4)

                    def spread(u):
                        t, c = u // 2, u % 2
                        if u > 1:
                            dve.wait_ge(s.sc_ps, n * 2 * SUB + u - 1)
                        dve.tensor_tensor(qm[c][:], qkf[:, c:c + 1, t * P:(t + 1) * P].to_broadcast([P, PER_TILE, P]),
                                          g.same_head[:].unsqueeze(2).to_broadcast([P, PER_TILE, P]),
                                          ALU.mult).then_inc(s.qm_ready, 1)

                    def mask(u):
                        t, c = u // 2, u % 2
                        dve.wait_ge(s.sc_ps, n * 2 * SUB + u + 1)
                        if c == 0:
                            dve.wait_ge(s.o_ps, n * SUB + t)
                        for half in range(2):
                            last = dve.tensor_tensor(sm[c][:, 4 * half:4 * half + 4, :],
                                                     bank[4 + 2 * c + half][:, :].rearrange("p (h c) -> p h c", h=4),
                                                     g.causal[:].unsqueeze(1).to_broadcast([P, 4, P]), ALU.mult)
                        last.then_inc(s.sm_ready, 1)

                    spread(0)
                    spread(1)
                    for t in range(SUB):
                        mask(2 * t)
                        if t + 1 < SUB:
                            spread(2 * t + 2)
                        mask(2 * t + 1)
                        if t + 1 < SUB:
                            spread(2 * t + 3)
                        dve.wait_ge(s.kv_ps, n * SUB + t + 1)
                        dve.wait_ge(s.kv_ready, n * SUB + t)
                        dve.tensor_tensor(kv_new[:], bank[2][:, :].rearrange("p (c e) -> p c e", c=KD),
                                          g.kv_mask[:].rearrange("p h e -> p (h e)").unsqueeze(1).to_broadcast([P, KD, 2 * P]),
                                          ALU.mult).then_inc(s.kv_cut, 1)
                        dve.wait_ge(s.rs_ready, n * SUB + t + 1)
                        dve.wait_ge(s.wo_ps, n * SUB + t)
                        dve.scalar_tensor_tensor(out=on[:].rearrange("p g c -> p (g c)"), in0=bank[0][:, :],
                                                 scalar=g.nw[:, 0:1], in1=rs[:].rearrange("p g c -> p (g c)"),
                                                 op0=ALU.mult, op1=ALU.mult).then_inc(s.on_ready, 1)
                        dve.wait_ge(s.wo_ps, n * SUB + t + 1)
                        row = g.acc[:, bass.ds(n * 4 + t, 1), :].rearrange("p x c -> p (x c)")
                        dve.tensor_tensor(row, row, bank[1][:, 0:D], ALU.add).then_inc(s.acc_ready, 1)
                chunks(dve, body)

            @block.gpsimd
            def _(pool):
                def clear(b):
                    wait_own(pool, g.passed, s.o_ps, (b + 1) * (TILES // BATCH))
                    wait_own(pool, g.passed, s.kv_ready, (b + 1) * (TILES // BATCH))
                    pool.memset(kv[:], 0.0).then_inc(s.kv_zero, 1)
                    wait_own(pool, g.passed, s.kv_zero, b + 2)

                def body(b, n):
                    wait_own(pool, g.passed, s.xt_ready, n * 2 + 2)
                    pool.tensor_copy(g.xt_all[:, :, bass.ds(n * HALF, HALF)], xt[:]).then_inc(s.xt_kept, 1)
                    for t in range(SUB):
                        wait_own(pool, g.passed, s.o_ps, n * SUB + t + 1)
                        wait_own(pool, g.passed, s.kv_cut, n * SUB + t + 1)
                        pool.tensor_tensor(kv[:], kv[:], kv_new[:], ALU.add).then_inc(s.kv_ready, 1)
                        wait_own(pool, g.passed, s.kv_ready, n * SUB + t + 1)
                pool.memset(kv[:], 0.0).then_inc(s.kv_zero, 1)
                pool.wait_ge(s.kv_zero, 1)
                chunks(pool, body, clear)


def feed_forward(nc, g, a):
    with ExitStack() as ctx:
        sb = lambda name, shape, dt=F32: ctx.enter_context(nc.sbuf_tensor(name, shape, dt))
        sem = lambda name: ctx.enter_context(nc.semaphore(name))
        gate = [ctx.enter_context(nc.psum_tensor(f"gate{i}", [P, HALF], F32)) for i in range(2)]
        up = [ctx.enter_context(nc.psum_tensor(f"up{i}", [P, HALF], F32)) for i in range(2)]
        down = [ctx.enter_context(nc.psum_tensor(f"down{i}", [P, HALF], F32)) for i in range(4)]
        silu = [sb(f"f_silu{i}", [P, HALF]) for i in range(2)]
        h = [sb(f"f_h{i}", [P, HALF]) for i in range(2)]
        names = "gate_done up_done silu_done h_ready down_step down_done acc_done stored"
        s = named(names, lambda n: sem("f_" + n))
        T = HID_TILES
        with nc.Block() as block:
            @block.tensor
            def _(pe):
                def body(n):
                    rows = [g.xt_all[:, k, bass.ds(n * HALF, HALF)] for k in range(KD)]

                    def gate_up(i):
                        wait(pe, s.h_ready, T * n + i - 1)
                        for w, out, done in ((g.wg1, gate, s.gate_done), (g.wu1, up, s.up_done)):
                            for k in range(KD):
                                last = pe.matmul(out[i % 2][:, :], w[:, k, i * P:(i + 1) * P], rows[k],
                                                 start=(k == 0), stop=(k == KD - 1))
                            last.then_inc(done, 1)

                    def down_part(i):
                        pe.wait_ge(s.h_ready, T * n + i + 1)
                        if i == 0:
                            wait(pe, s.acc_done, 4 * n)
                        for t in range(CHUNK_TILES):
                            last = pe.matmul(down[t][:, 0:D], h[i % 2][:, t * P:(t + 1) * P], g.wd1[:, i, :],
                                             start=(i == 0), stop=(i == T - 1))
                            if i == T - 1:
                                last.then_inc(s.down_done, 1)
                        if i < T - 1:
                            last.then_inc(s.down_step, 1)
                    gate_up(0)
                    for i in range(1, T):
                        gate_up(i)
                        down_part(i - 1)
                    down_part(T - 1)
                body(0)
                with pe.Fori(1, TOKENS // HALF) as n:
                    body(n)

            @block.scalar
            def _(act):
                def body(n):
                    for i in range(T):
                        act.wait_ge(s.gate_done, T * n + i + 1)
                        wait(act, s.h_ready, T * n + i - 1)
                        act.activation(silu[i % 2][:], gate[i % 2][:, :], ACT.Silu).then_inc(s.silu_done, 1)
                body(0)
                with act.Fori(1, TOKENS // HALF) as n:
                    body(n)

            @block.vector
            def _(dve):
                def body(n):
                    for i in range(T):
                        dve.wait_ge(s.silu_done, T * n + i + 1)
                        dve.wait_ge(s.up_done, T * n + i + 1)
                        if i > 1:
                            dve.wait_ge(s.down_step, (T - 1) * n + i - 1)
                        dve.tensor_tensor(h[i % 2][:], up[i % 2][:, :], silu[i % 2][:], ALU.mult).then_inc(s.h_ready, 1)
                    for t in range(CHUNK_TILES):
                        dve.wait_ge(s.down_done, 4 * n + t + 1)
                        row = g.acc[:, bass.ds(n * 4 + t, 1), :].rearrange("p x c -> p (x c)")
                        dve.tensor_tensor(row, row, down[t][:, 0:D], ALU.add).then_inc(s.acc_done, 1)
                body(0)
                with dve.Fori(1, TOKENS // HALF) as n:
                    body(n)

            @block.sync
            def _(sp):
                with sp.Fori(0, TOKENS // HALF) as n:
                    sp.wait_ge(s.acc_done, 4 * n + 4)
                    sp.dma_start(a.out[:, bass.ds(n * 4, 4), :], g.acc[:, bass.ds(n * 4, 4), :]).then_inc(s.stored, 16)
                sp.wait_ge(s.stored, 16 * (TOKENS // HALF))


def build(nc, a):
    g = Buffers()
    with ExitStack() as ctx:
        def sb(name, shape, dt=F32, scope=ctx):
            return scope.enter_context(nc.sbuf_tensor(name, shape, dt))

        g.passed = ctx.enter_context(nc.semaphore("pool_passed"))
        g.experts_loaded = ctx.enter_context(nc.semaphore("experts_loaded"))
        g.acc = sb("acc", [P, TILES, D])
        g.ident = sb("ident", [P, P])
        g.mean_var = sb("mean_var", [P, TILES, 2])
        g.rstd = sb("rstd", [P, TILES])
        g.wq = sb("wq", [P, KD, D])
        g.wk = sb("wk", [P, KD, DKV])
        g.wvr = sb("wvr", [P, KD, P])
        g.mem = sb("mem", [P, P])
        g.memn = sb("memn", [P, 2])
        g.mw = sb("mw", [P, 1])
        g.w = sb("w", [P, 2])
        g.vp = sb("vp", [P, BATCH, NKV, SEQ // P, DH])
        g.q_stack = [sb(f"q_stack{i}", [STACK, NQ, HALF], BF16) for i in range(4)]
        g.k_max = [sb(f"k_max{i}", [STACK, SEQ], BF16) for i in range(2)]
        g.k_st = [sb(f"k_st{i}", [STACK, SEQ], BF16) for i in range(2)]
        g.v_stack = [sb(f"v_stack{i}", [P, SEQ // P, 32]) for i in range(2)]
        g.row_no = sb("row_no", [P, TILES])
        g.logits = sb("logits", [P, TILES, EXPERTS])
        g.weight = sb("weight", [P, TILES, TOP_K])
        g.slot = sb("slot", [P, TOP_K, TILES], I32)
        g.tile_expert = sb("tile_expert", [P, ROW_TILES], I32)
        g.tile_rows = sb("tile_rows", [P, ROW_TILES], I32)
        with ExitStack() as weights:
            g.wgu = sb("wgu", [P, EXPERTS, KD, 2 * INNER], scope=weights)
            g.wd = sb("wd", [P, EXPERTS, D], scope=weights)
            load_inputs(nc, g, a)
            layernorm_statistics(nc, g, "ln0")
            project(nc, g, a)
            dispatch(nc, g, a)
            with ExitStack() as beside:
                attention(nc, g, a, 0, NumberSlots(nc, g, a, beside))
            read_table(nc, g, a)
            experts(nc, g, a)
        g.wqkv1 = sb("wqkv1", [P, KD, 3 * D])
        g.feat = sb("feat", [P, 4, P])
        g.fbias = sb("fbias", [P, 4])
        g.nw = sb("nw", [P, 1])
        g.wo1 = sb("wo1", [P, GROUPS, D])
        g.wg1 = sb("wg1", [P, KD, HIDDEN])
        g.wu1 = sb("wu1", [P, KD, HIDDEN])
        g.wd1 = sb("wd1", [P, HID_TILES, D])
        g.causal = sb("causal", [P, P])
        g.same_head = sb("same_head", [P, PER_TILE])
        g.kv_mask = sb("kv_mask", [P, PER_TILE, 32])
        g.mean32 = sb("mean32", [P, GROUP, 32])
        g.v_pad = sb("v_pad", [P, CHUNK_TILES, HEADS1, 32])
        g.eps = sb("eps", [P, 1])
        with ExitStack() as beside:
            attention(nc, g, a, 1, AddExperts(nc, g, a, beside))
        g.xt_all = sb("xt_all", [P, KD, TOKENS])
        layernorm_statistics(nc, g, "ln1")
        linear_attention(nc, g, a)
        feed_forward(nc, g, a)


def kernel(**inputs):
    import numpy as np
    import concourse.bacc as bacc
    from concourse.bass_utils import run_bass_kernel_spmd

    x = {name: np.asarray(value) for name, value in inputs.items()}

    def by_rows(w):
        return w.T.reshape(w.shape[1] // P, P, w.shape[0]).transpose(1, 0, 2)

    def blocks(w, n):
        out = np.zeros((n * w.shape[0], n * w.shape[1]), w.dtype)
        for i in range(n):
            out[i * w.shape[0]:(i + 1) * w.shape[0], i * w.shape[1]:(i + 1) * w.shape[1]] = w
        return out

    def pad_heads(w):
        out = np.zeros((w.shape[0] // DK1, 32, w.shape[1]), w.dtype)
        out[:, 0:DK1] = w.reshape(-1, DK1, w.shape[1])
        return out.reshape(-1, w.shape[1])

    wv_router = np.concatenate([x["L0_attn_Wv"], x["L0_ffn_router_w"], np.zeros((P - DKV - EXPERTS, D), np.float32)])
    gate_up = np.concatenate([x["L0_ffn_w_gate"], x["L0_ffn_w_up"]], axis=1)
    features = [x[f"L1_attn_{n}_w"] for n in ("fq1", "fq2", "fk1", "fk2")]
    biases = [x[f"L1_attn_{n}_b"] for n in ("fq1", "fq2", "fk1", "fk2")]
    host = {
        "x": x["L0_attn_x"].reshape(TILES, P, D).transpose(1, 0, 2),
        "wq": by_rows(x["L0_attn_Wq"]),
        "wk": by_rows(x["L0_attn_Wk"]),
        "wvr": by_rows(wv_router),
        "mem": blocks(x["L0_attn_memory"], 2),
        "memn": blocks(x["L0_attn_memory_norm"], 2),
        "mw": np.broadcast_to(x["L0_attn_memory_weight"], (P, 1)),
        "wgu": gate_up.transpose(2, 0, 1).reshape(KD, P, EXPERTS, 2 * INNER).transpose(1, 2, 0, 3),
        "wd": x["L0_ffn_w_down"].transpose(2, 0, 1),
        "wqkv1": by_rows(np.concatenate([x["L1_attn_wq"], x["L1_attn_wk"], x["L1_attn_wv"]])),
        "feat": np.stack([blocks(w.T, PER_TILE) for w in features], axis=1),
        "fbias": np.stack([np.tile(b, PER_TILE) for b in biases], axis=1),
        "nw": np.tile(pad_heads(x["L1_attn_norm_w"].reshape(DK1, 1)), (GROUP, 1)),
        "wo1": pad_heads(x["L1_attn_wo"].T).reshape(GROUPS, P, D).transpose(1, 0, 2),
        "wg1": by_rows(x["L1_ffn_w_gate"]),
        "wu1": by_rows(x["L1_ffn_w_up"]),
        "wd1": by_rows(x["L1_ffn_w_down"]),
    }
    nc = bacc.Bacc("TRN2", target_bir_lowering=False, num_devices=1)
    arrays = {f"in_{name}": np.ascontiguousarray(value) for name, value in host.items()}
    i = {name: nc.dram_tensor(f"in_{name}", value.shape, F32, kind="ExternalInput").ap() for name, value in host.items()}
    a = Buffers()
    a.x, a.wq, a.wk, a.wvr, a.mem, a.memn, a.mw = (i[n] for n in ("x", "wq", "wk", "wvr", "mem", "memn", "mw"))
    a.wgu, a.wd, a.wqkv1, a.feat, a.fbias, a.nw = (i[n] for n in ("wgu", "wd", "wqkv1", "feat", "fbias", "nw"))
    a.wo1, a.wg1, a.wu1, a.wd1 = (i[n] for n in ("wo1", "wg1", "wu1", "wd1"))
    q_pieces = nc.dram_tensor("q_pieces", [PIECES, 2, BATCH, DKV, NQ, HALF], BF16).ap()
    k_pieces = nc.dram_tensor("k_pieces", [PIECES, BATCH, DKV, SEQ], BF16).ap()
    a.q_pieces, a.k_pieces = q_pieces, k_pieces
    a.q_pieces_by_head = q_pieces.rearrange("p s b (h d) q c -> p s (b h) d (q c)", d=DH)
    a.k_pieces_by_head = k_pieces.rearrange("p b (h d) t -> p (b h) d t", d=DH)
    a.xn_flat = nc.dram_tensor("xn_rows", [TOKENS, D], F32).ap()
    a.xn_rows = a.xn_flat.rearrange("(t p) d -> p t d", p=P)
    a.slot_row = nc.dram_tensor("slot_row", [ROW_TILES * P, 1], F32).ap()
    a.expert_out = nc.dram_tensor("expert_out", [ROW_TILES * P, D], F32).ap()
    a.expert_out_tiles = a.expert_out.rearrange("(t p) d -> p t d", p=P)
    rows_out = nc.dram_tensor("rows_out", [BATCH, SEQ, D], F32, kind="ExternalOutput").ap()
    a.out = rows_out.rearrange("b (t p) d -> p (b t) d", p=P)
    build(nc, a)
    result = run_bass_kernel_spmd(nc, [arrays], core_ids=[0])
    return result.results[0]["rows_out"]
```

```python
from collections import namedtuple
from contextlib import ExitStack

import concourse.bass as bass
from concourse import mybir

F32 = mybir.dt.float32
BF16 = mybir.dt.bfloat16
F32R = mybir.dt.float32r
I32 = mybir.dt.int32
U32 = mybir.dt.uint32
ALU = mybir.AluOpType
ACT = mybir.ActivationFunctionType
AX = mybir.AxisListType

P = 128
EPS = 1e-5

BATCH, SEQ, D = 2, 1024, 256
TOKENS = BATCH * SEQ
TILES = TOKENS // P
KD = D // P
NQ, NKV, DH = 4, 8, 8
HEADS = BATCH * NKV
DKV = NKV * DH
SM_SCALE = DH ** -0.5

PIECES = 3
PROD_ROWS = PIECES * PIECES * DH
STACK = 96
HALF = 512
CHUNK_TILES = HALF // P


class Buffers:
    pass


def named(names, make):
    names = names.split()
    return namedtuple("Named", names)(*[make(name) for name in names])


def wait(engine, sem, value):
    if not isinstance(value, int) or value > 0:
        engine.wait_ge(sem, value)


def wait_own(engine, passed, sem, value):
    wait(engine, sem, value)
    if not isinstance(value, int):
        engine.sem_inc(passed, 1)


class Chain:

    def __init__(self, engine, sem, base=0):
        self.engine, self.sem, self.base, self.n = engine, sem, base, 0

    def link(self, instruction):
        self.n += 1
        instruction.then_inc(self.sem, 1)
        self.engine.wait_ge(self.sem, self.base + self.n)


def layernorm_statistics(nc, g, tag, beside, rows_loaded=None, first_tile=0):
    with ExitStack() as ctx:
        sem = lambda name: ctx.enter_context(nc.semaphore(f"{tag}_{name}"))
        stats_done, var_ready, sqrt_done, rstd_done = sem("stats"), sem("var"), sem("sqrt"), sem("rstd")
        sd = ctx.enter_context(nc.sbuf_tensor(f"{tag}_sd", [P, TILES, 2], F32))
        y = ctx.enter_context(nc.sbuf_tensor(f"{tag}_y", [P, TILES, 4], F32))
        with nc.Block() as block:
            last_on_vector, last_on_scalar = beside(block) or (None, None)

            @block.vector
            def _(dve):
                for t in range(first_tile, TILES):
                    if rows_loaded and t % 4 == 0:
                        dve.wait_ge(rows_loaded[t // 4], 16)
                    dve.bn_stats(g.bn[:, t, :], g.acc[:, t, :]).then_inc(stats_done, 1)
                dve.wait_ge(stats_done, TILES - first_tile)
                for t in range(TILES):
                    last = dve.bn_aggr(g.mean_var[:, t, :], g.bn[:, t, :])
                last.then_inc(var_ready, 1)
                dve.wait_ge(var_ready, 1)
                dve.tensor_scalar(sd[:, :, 0], g.mean_var[:, :, 1], EPS, None, ALU.add).then_inc(var_ready, 1)
                dve.wait_ge(sqrt_done, 1)
                dve.reciprocal(y[:, :, 0], sd[:, :, 1]).then_inc(rstd_done, 1)
                dve.wait_ge(rstd_done, 1)
                dve.tensor_tensor(y[:, :, 1], y[:, :, 0], y[:, :, 0], ALU.mult).then_inc(rstd_done, 1)
                dve.wait_ge(rstd_done, 2)
                dve.tensor_tensor(y[:, :, 2], y[:, :, 1], sd[:, :, 0], ALU.mult).then_inc(rstd_done, 1)
                dve.wait_ge(rstd_done, 3)
                dve.tensor_scalar(y[:, :, 3], y[:, :, 2], -0.5, 1.5, ALU.mult, ALU.add).then_inc(rstd_done, 1)
                dve.wait_ge(rstd_done, 4)
                dve.tensor_tensor(g.rstd[:, :], y[:, :, 3], y[:, :, 0], ALU.mult).then_inc(rstd_done, 1)
                if last_on_vector:
                    last_on_vector(dve)

            @block.scalar
            def _(act):
                act.wait_ge(var_ready, 2)
                act.activation(sd[:, :, 1], sd[:, :, 0], ACT.Sqrt).then_inc(sqrt_done, 1)
                if last_on_scalar:
                    last_on_scalar(act)


def load_inputs(nc, g, a, block, x_loaded, w_loaded, set_up):
    @block.sync
    def _(sp):
        for q in range(4):
            sp.dma_start(g.acc[:, 4 * q:4 * q + 4, :], a.x[:, 4 * q:4 * q + 4, :]).then_inc(x_loaded[q], 16)
        loads = ((g.mw, a.mw), (g.wq, a.wq), (g.wk, a.wk), (g.wvr, a.wvr), (g.mem, a.mem), (g.memn, a.memn))
        for dst, src in loads:
            sp.dma_start(dst[:], src).then_inc(w_loaded, 16)
        sp.wait_ge(w_loaded, 16 * len(loads))

    @block.gpsimd
    def _(pool):
        pool.memset(g.ident[:], 0.0).then_inc(set_up, 1)
        pool.wait_ge(set_up, 1)
        pool.affine_select(out=g.ident[:], in_=g.ident[:], compare_op=ALU.not_equal, fill=1.0, base=0,
                           pattern=[[-1, P]], channel_multiplier=1).then_inc(set_up, 1)
        for stack in g.q_stack + g.k_max:
            pool.memset(stack[:], 0.0).then_inc(set_up, 1)
        for stack in g.k_st:
            pool.memset(stack[:], 1.0).then_inc(set_up, 1)
        for stack in g.v_stack:
            pool.memset(stack[:], 0.0).then_inc(set_up, 1)
        pool.wait_ge(set_up, 12)
        for stack in g.v_stack:
            pool.memset(stack[:, :, DH:DH + 1], 1.0).then_inc(set_up, 1)


def project(nc, g, a):
    CHUNKS = TOKENS // HALF
    with ExitStack() as ctx:
        sb = lambda name, shape, dt: ctx.enter_context(nc.sbuf_tensor(name, shape, dt))
        sem = lambda name: ctx.enter_context(nc.semaphore(name))
        bank = [ctx.enter_context(nc.psum_tensor(f"prj{i}", [P, HALF], F32)) for i in range(8)]
        xn = sb("xn", [P, CHUNK_TILES, D], F32)
        xt = sb("xt", [P, KD, HALF], F32)
        qp = sb("qp", [P, KD, PIECES, HALF], BF16)
        kp = sb("kp", [DKV, PIECES, HALF], BF16)
        rest = sb("rest", [P, 3, HALF], F32)
        qneg = sb("qneg", [P, KD, HALF], F32)
        th = sb("th", [P, KD, HALF], F32)
        ex = sb("ex", [P, KD, HALF], F32)
        expm1 = sb("expm1", [P, KD, HALF], F32)
        sigma = sb("sigma", [P, KD, HALF], F32)
        rden = sb("rden", [P, CHUNK_TILES * NQ], F32)
        wden = sb("wden", [P, CHUNK_TILES, KD, 2], F32)
        amem = sb("amem", [P, CHUNK_TILES, KD, 2, DKV], F32)
        gate = sb("gate", [P, 2], F32)
        names = ("gate_exp gate_ready xn_ready xt_ps xt_ready q_ps vr_ps piece0 rest1 piece1 piece2 vr_read "
                 "th_ready sigma_ready mem_ps rden_ready amem_ready acc_added dve_own xn_stored")
        s = named(names, lambda n: sem("p_" + n))
        stored, STORES = [sem(f"p_stored{c}") for c in range(3)], (32, 32, 16)
        LINKS = 4 * KD

        def chunks(engine, body):
            body(0, True)
            with engine.Fori(1, CHUNKS - 1) as n:
                body(n, True)
            body(CHUNKS - 1, False)

        ORDER = (0, 2, 1)

        def part(c):
            return (slice(0, DKV), kp[:, :, :]) if c == 2 else (slice(0, P), qp[:, c, :, :])

        with nc.Block() as block:
            @block.vector
            def _(dve):
                def normalise(n):
                    wait(dve, s.xt_ps, 2 * n)
                    wait(dve, s.xn_stored, 16 * n)
                    for t in range(CHUNK_TILES):
                        dve.tensor_scalar(xn[:, t, :], g.acc[:, bass.ds(n * 4 + t, 1), :],
                                          g.mean_var[:, bass.ds(n * 4 + t, 1), 0:1].rearrange("p a b -> p (a b)"),
                                          g.rstd[:, bass.ds(n * 4 + t, 1)],
                                          ALU.subtract, ALU.mult).then_inc(s.xn_ready, 1)

                def leave_rest(n, i, c):
                    rows, pieces = part(c)
                    dve.wait_ge(s.piece0, 3 * n + i + 1)
                    wait(dve, s.piece2, 3 * n + i - 2)
                    dve.tensor_tensor(rest[rows, c, :], bank[2 + c][rows, :], pieces[:, 0, :],
                                      ALU.subtract).then_inc(s.rest1, 1)

                def elu(n, c):
                    own = Chain(dve, s.dve_own, LINKS * n + 2 + 4 * c)
                    dve.wait_ge(s.th_ready, (2 * n + c + 1) * 2)
                    rec, res, t = ex[:, c, :], expm1[:, c, :], th[:, c, :]
                    own.link(dve.tensor_scalar(rec, rec, 1.0, 0.5, ALU.add, ALU.mult))
                    own.link(dve.scalar_tensor_tensor(out=res, in0=t, scalar=-1.0, in1=rec, op0=ALU.add, op1=ALU.mult))
                    own.link(dve.scalar_tensor_tensor(out=rec, in0=res, scalar=2.0, in1=rec, op0=ALU.add, op1=ALU.mult))
                    own.link(dve.scalar_tensor_tensor(out=res, in0=t, scalar=2.0, in1=rec, op0=ALU.mult, op1=ALU.mult))
                    wait(dve, s.mem_ps, n)
                    dve.scalar_tensor_tensor(out=sigma[:, c, :], in0=bank[2 + c][:, :], scalar=0.0, in1=res,
                                             op0=ALU.max, op1=ALU.add).then_inc(s.sigma_ready, 1)

                def memory_part(n):
                    dve.wait_ge(s.mem_ps, n + 1)
                    dve.reciprocal(rden[:, :], bank[5][:, 0:CHUNK_TILES * NQ]).then_inc(s.rden_ready, 1)
                    dve.wait_ge(s.rden_ready, 2 * n + 1)
                    dve.tensor_scalar(wden[:].rearrange("p t c g -> p (t c g)"), rden[:, :], g.w[:, 0:1], None,
                                      ALU.mult).then_inc(s.rden_ready, 1)
                    dve.wait_ge(s.rden_ready, 2 * n + 2)
                    dve.wait_ge(s.acc_added, n + 1)
                    for c in range(KD):
                        dve.tensor_tensor(amem[:, :, c, :, :],
                                          bank[6 + c][:, :].rearrange("p (t g e) -> p t g e", t=CHUNK_TILES, g=2),
                                          wden[:, :, c, :].unsqueeze(3).to_broadcast([P, CHUNK_TILES, 2, DKV]),
                                          ALU.mult).then_inc(s.amem_ready, 1)

                def body(n, more):
                    for i, c in enumerate(ORDER):
                        leave_rest(n, i, c)
                    if more:
                        normalise(n + 1)
                    if not isinstance(n, int) or n > 0:
                        memory_part(n - 1)
                    for c in range(KD):
                        elu(n, c)
                dve.sem_inc(s.amem_ready, 1)
                normalise(0)
                dve.wait_ge(s.gate_exp, 1)
                own = Chain(dve, s.dve_own)
                own.link(dve.tensor_scalar(gate[:, 1:2], gate[:, 0:1], 1.0, None, ALU.add))
                own.link(dve.reciprocal(g.w[:, 0:1], gate[:, 1:2]))
                dve.tensor_scalar(g.w[:, 1:2], g.w[:, 0:1], -1.0, 1.0, ALU.mult, ALU.add).then_inc(s.gate_ready, 1)
                chunks(dve, body)
                memory_part(CHUNKS - 1)

            @block.scalar
            def _(act):
                def keep_rows(n):
                    wait(act, s.vr_ps, n)
                    for k in range(KD):
                        act.wait_ge(s.xt_ps, 2 * n + k + 1)
                        act.activation(xt[:, k, :], bank[k][:, :], ACT.Copy).then_inc(s.xt_ready, 1)

                def body(n, more):
                    for i, c in enumerate(ORDER):
                        rows, pieces = part(c)
                        wait(act, stored[c], STORES[c] * n)
                        act.wait_ge(s.q_ps, 3 * n + i + 1)
                        first = act.activation(pieces[:, 0, :], bank[2 + c][rows, :], ACT.Copy)
                        if c < 2:
                            first = act.activation(qneg[:, c, :], bank[2 + c][:, :], ACT.Relu, scale=-1.0)
                        first.then_inc(s.piece0, 1)
                    for i, c in enumerate(ORDER):
                        rows, pieces = part(c)
                        act.wait_ge(s.rest1, 3 * n + i + 1)
                        act.activation(pieces[:, 1, :], rest[rows, c, :], ACT.Copy).then_inc(s.piece1, 1)
                    act.wait_ge(s.piece0, 3 * n + 3)
                    for c in range(KD):
                        wait(act, s.sigma_ready, 2 * n)
                        act.activation(th[:, c, :], qneg[:, c, :], ACT.Tanh, scale=-0.5).then_inc(s.th_ready, 1)
                        act.activation(ex[:, c, :], qneg[:, c, :], ACT.Exp, scale=-1.0).then_inc(s.th_ready, 1)
                    act.wait_ge(s.vr_ps, n + 1)
                    vr = bank[5][:, :].rearrange("p (t c) -> p t c", t=CHUNK_TILES)
                    act.activation(g.vp[:, bass.ds(n * 4, 4), :], vr[:, :, 0:DKV], ACT.Copy, scale=g.w[:, 1:2])
                    act.activation(g.logits[:, bass.ds(n * 4, 4), :], vr[:, :, DKV:DKV + 32],
                                   ACT.Copy).then_inc(s.vr_read, 1)
                    if more:
                        keep_rows(n + 1)
                act.activation(gate[:, 0:1], g.mw[:], ACT.Exp, scale=-1.0).then_inc(s.gate_exp, 1)
                keep_rows(0)
                act.wait_ge(s.gate_ready, 1)
                chunks(act, body)

            @block.tensor
            def _(pe):
                def turn(n):
                    pe.wait_ge(s.xn_ready, 4 * n + 4)
                    wait(pe, s.xt_ready, 2 * n)
                    for k in range(KD):
                        for t in range(CHUNK_TILES):
                            last = pe.transpose(bank[k][:, t * P:(t + 1) * P], xn[:, t, k * P:(k + 1) * P], g.ident[:])
                        last.then_inc(s.xt_ps, 1)

                def project_qk(n, c):
                    w = g.wk if c == 2 else g.wq
                    cols = slice(0, DKV) if c == 2 else slice(c * P, (c + 1) * P)
                    rows, _ = part(c)
                    if c < 2:
                        wait(pe, s.sigma_ready, 2 * n - 1 + c)
                    else:
                        wait(pe, s.rest1, 3 * n)
                    for k in range(KD):
                        last = pe.matmul(bank[2 + c][rows, :], w[:, k, cols], xt[:, k, :],
                                         start=(k == 0), stop=(k == KD - 1))
                    last.then_inc(s.q_ps, 1)

                def project_vr(n):
                    wait(pe, s.rden_ready, 2 * n)
                    for t in range(CHUNK_TILES):
                        for k in range(KD):
                            last = pe.matmul(bank[5][:, t * P:(t + 1) * P], xt[:, k, t * P:(t + 1) * P], g.wvr[:, k, :],
                                             start=(k == 0), stop=(k == KD - 1))
                    last.then_inc(s.vr_ps, 1)

                def memory(n):
                    pe.wait_ge(s.sigma_ready, 2 * n + 2)
                    pe.wait_ge(s.amem_ready, 2 * n + 1)
                    pe.wait_ge(s.vr_read, n + 1)
                    for c in range(KD):
                        for t in range(CHUNK_TILES):
                            pe.matmul(bank[6 + c][:, t * P:(t + 1) * P], sigma[:, c, t * P:(t + 1) * P], g.mem[:],
                                      start=True, stop=True)
                    for t in range(CHUNK_TILES):
                        for c in range(KD):
                            o = (t * KD + c) * 2
                            last = pe.matmul(bank[5][:, o:o + 2], sigma[:, c, t * P:(t + 1) * P], g.memn[:],
                                             start=True, stop=True)
                    last.then_inc(s.mem_ps, 1)

                def body(n, more):
                    pe.wait_ge(s.xt_ready, 2 * n + 2)
                    for c in ORDER:
                        project_qk(n, c)
                    if not isinstance(n, int) or n > 0:
                        memory(n - 1)
                    project_vr(n)
                    if more:
                        turn(n + 1)
                turn(0)
                chunks(pe, body)
                memory(CHUNKS - 1)

            @block.gpsimd
            def _(pool):
                def add_memory(n):
                    wait_own(pool, g.passed, s.xn_ready, 4 * n + 4)
                    wait_own(pool, g.passed, s.amem_ready, 2 * n + 3)
                    rows = g.acc[:, bass.ds(n * 4, 4), :]
                    pool.tensor_tensor(rows, rows, amem[:].rearrange("p t c g e -> p t (c g e)"),
                                       ALU.add).then_inc(s.acc_added, 1)

                def body(n, more):
                    for i, c in enumerate(ORDER):
                        rows, pieces = part(c)
                        wait_own(pool, g.passed, s.piece1, 3 * n + i + 1)
                        pool.tensor_tensor(pieces[:, 2, :], rest[rows, c, :], pieces[:, 1, :],
                                           ALU.subtract).then_inc(s.piece2, 1)
                    if not isinstance(n, int) or n > 0:
                        add_memory(n - 1)
                pool.sem_inc(s.acc_added, 1)
                chunks(pool, body)
                add_memory(CHUNKS - 1)

            @block.sync
            def _(sp):
                def body(n, more):
                    sp.wait_ge(s.xn_ready, 4 * n + 4)
                    sp.dma_start(a.xn_rows[:, bass.ds(n * 4, 4), :], xn[:]).then_inc(s.xn_stored, 16)
                    for i, c in enumerate(ORDER):
                        wait_own(sp, g.passed, s.piece2, 3 * n + i + 1)
                        if c == 2:
                            dst = a.k_pieces[:, :, bass.ds(n * HALF, HALF)]
                            sp.dma_start(dst.rearrange("p r s -> r p s"), kp[:]).then_inc(stored[c], 16)
                            continue
                        for q in range(2):
                            dst = a.q_pieces[:, bass.ds(n, 1), :, 2 * c + q, :]
                            sp.dma_start(dst.rearrange("p x r s -> (x r) p s"),
                                         qp[q * DKV:(q + 1) * DKV, c, :, :]).then_inc(stored[c], 16)
                chunks(sp, body)
                sp.wait_ge(s.xn_stored, 4 * 16)
                for c in range(3):
                    sp.wait_ge(stored[c], CHUNKS * STORES[c])




def attention(nc, g, a, b, beside, prelude):
    heads = NKV
    units = 2 * heads
    pairs = heads // 2
    STEPS = SEQ // P
    MAXES = 2 * NQ * CHUNK_TILES
    SHIFT = 12
    with nc.cleanup_on_exit(), ExitStack() as ctx:
        sem = lambda name: nc.alloc_semaphore(f"{name}_b{b}")
        q_stack, k_max, k_st, v_stack = g.q_stack, g.k_max, g.k_st, g.v_stack
        q_loaded = [sem(f"q_loaded{i}") for i in range(4)]
        km_loaded = [sem(f"km_loaded{i}") for i in range(2)]
        kt_loaded = [sem(f"kt_loaded{i}") for i in range(2)]
        m_loaded = [sem(f"m_loaded{i}") for i in range(2)]
        names = ("st_done exp_done mx_done max_read negm_done mt_done mt_read m_pieces_ready pv_done "
                 "o_copied ot_done norm_done v_ready m_own rsum_done joined")
        s = named(names, lambda n: sem("a_" + n))

        def each_pair(engine, body):
            body(0)
            with engine.Fori(1, pairs - 1) as j:
                body(j)
            body(pairs - 1)

        def after(j, w, k, ahead):
            return not (isinstance(j, int) and j == pairs - 1) or k + ahead < 4

        def load_q_unit(sp, buf, half, head):
            src = a.q_pieces_by_head[:, 2 * b + half, bass.ds(head, 1), :, :]
            for copy in range(PIECES):
                rows = slice(copy * PIECES * DH, (copy + 1) * PIECES * DH)
                sp.dma_start(q_stack[buf][rows, :, :].rearrange("r q s -> r (q s)"),
                             src.rearrange("p x d c -> p (x d) c")).then_inc(q_loaded[buf], 16)

        def load_k(sp, stack, sem, head):
            for p in range(PIECES):
                rows = slice(p * PIECES * DH, (p + 1) * PIECES * DH)
                src = a.k_pieces_by_head[p, bass.ds(head, 1), :, b * SEQ:(b + 1) * SEQ]
                sp.dma_start(stack[rows, :], src.to_broadcast([PIECES, DH, SEQ])).then_inc(sem, 16)

        def load_first(sp):
            load_k(sp, k_max[0], km_loaded[0], 0)
            load_q_unit(sp, 0, 0, 0)
            load_q_unit(sp, 1, 1, 0)
            load_k(sp, k_st[0], kt_loaded[0], 0)
            load_k(sp, k_max[1], km_loaded[1], 1)
            load_q_unit(sp, 2, 0, 1)

        prelude(load_first)
        sb = lambda name, shape, dt: ctx.enter_context(nc.sbuf_tensor(f"{name}_b{b}", shape, dt))
        st_bank = [ctx.enter_context(nc.psum_tensor(f"st{i}_b{b}", [P, 2, HALF], F32)) for i in range(2)]
        mx_bank = [ctx.enter_context(nc.psum_tensor(f"mx{i}_b{b}", [P, HALF], F32)) for i in range(3)]
        o_bank = ctx.enter_context(nc.psum_tensor(f"o_bank_b{b}", [P, HALF], F32))
        TURN_MAX, TURN_OUT = 4, 24
        m_bank, t_bank = mx_bank[TURN_MAX % 3], mx_bank[TURN_OUT % 3]
        probs = [sb(f"probs{i}", [P, NQ, HALF], F32) for i in range(2)]
        partial_max = sb("partial_max", [P, NQ * CHUNK_TILES, 2], F32)
        neg_max = [sb(f"neg_max{i}", [P, NQ * CHUNK_TILES], F32) for i in range(2)]
        m_pieces = [sb(f"m_pieces{i}", [NQ * CHUNK_TILES, PIECES, P], BF16) for i in range(2)]
        m_rest = sb("m_rest", [NQ * CHUNK_TILES, P], F32)
        o_sb = [sb(f"o_sb{i}", [P, HALF], F32) for i in range(2)]
        out = [sb(f"out{i}", [P, CHUNK_TILES, NQ, DH], F32) for i in range(4)]
        rsum = sb("rsum", [P, CHUNK_TILES, NQ], F32)

        with nc.Block() as block:
            @block.sync
            def _(sp):
                def body(j):
                    for k in range(4):
                        w = 4 * j + k
                        if after(j, w, k, 3):
                            wait_own(sp, g.passed, s.st_done, 2 * STEPS * w)
                            load_q_unit(sp, (k + 3) % 4, (k + 3) % 2, 2 * j + (k + 3) // 2)
                        if k % 2 == 0 and after(j, w, k, 2):
                            wait_own(sp, g.passed, s.st_done, 2 * STEPS * w)
                            load_k(sp, k_st[(k // 2 + 1) % 2], kt_loaded[(k // 2 + 1) % 2], 2 * j + k // 2 + 1)
                            if after(j, w, k, 4):
                                wait_own(sp, g.passed, s.mx_done, MAXES * (w + 2))
                                load_k(sp, k_max[k // 2], km_loaded[k // 2], 2 * j + k // 2 + 2)
                        if after(j, w, k, 1):
                            send_max((k + 1) % 4, (k + 1) % 2, w + 1)
                def send_max(buf, par, w):
                    wait_own(sp, g.passed, s.m_pieces_ready, w + 1)
                    for p in range(PIECES):
                        row = q_stack[buf][PROD_ROWS + p:PROD_ROWS + p + 1, :, :]
                        sp.dma_start(row.rearrange("o q (t c) -> o (q t) c", c=P),
                                     m_pieces[par][:, p, :]).then_inc(m_loaded[par], 16)
                send_max(0, 0, 0)
                each_pair(sp, body)

            @block.gpsimd
            def _(pool):
                def join(w, k, head):
                    wait_own(pool, g.passed, s.norm_done, w + 1)
                    wait_own(pool, g.passed, s.joined, w)
                    rows = g.acc[:, b * 8 + k % 2 * 4:b * 8 + k % 2 * 4 + 4, :].rearrange("p t (q h d) -> p t q h d", q=NQ, d=DH)
                    rows = rows[:, :, :, bass.ds(head, 1), :].rearrange("p t q x d -> p t q (x d)")
                    pool.tensor_tensor(rows, rows, out[k][:, :, :, :], ALU.add).then_inc(s.joined, 1)

                def body(j):
                    for u in range(2):
                        head = 2 * j + u
                        wait_own(pool, g.passed, s.pv_done, 2 * STEPS * (head - 1))
                        pool.tensor_copy(v_stack[u][:, :, 0:DH],
                                         g.vp[:, b * STEPS:(b + 1) * STEPS, :].rearrange("p t (h d) -> p t h d", d=DH)
                                         [:, :, bass.ds(head, 1), :].rearrange("p t x d -> p t (x d)")).then_inc(s.v_ready, 1)
                        beside.head(pool, head)
                        if u == 1 or not isinstance(j, int) or j > 0:
                            for k in range(2):
                                join(2 * (head - 1) + k, (2 * (u + 1) + k) % 4, head - 1)
                each_pair(pool, body)
                for k in range(2):
                    join(units - 2 + k, 2 + k, heads - 1)
                beside.end(pool)

            @block.tensor
            def _(pe):
                def max_scores(buf, w, j2, m):
                    tile, half = m // 2, m % 2
                    if m == 0:
                        pe.wait_ge(q_loaded[buf], 16 * PIECES * (j2 + 1))
                        pe.wait_ge(km_loaded[buf // 2], 16 * PIECES * (j2 + 1))
                    wait(pe, s.max_read, MAXES * w + (m - 2 if m > 2 else (-1, 0, -2)[m]))
                    if m == TURN_MAX:
                        wait(pe, s.mt_read, w)
                    if m == TURN_OUT:
                        wait(pe, s.norm_done, w - 1)
                    q, t = tile // CHUNK_TILES, tile % CHUNK_TILES
                    pe.matmul(mx_bank[m % 3][:, :], q_stack[buf][:, q, t * P:(t + 1) * P],
                              k_max[buf // 2][:, half * HALF:(half + 1) * HALF],
                              start=True, stop=True).then_inc(s.mx_done, 1)

                def turn_max(par, w, ahead):
                    pe.wait_ge(s.negm_done, w + 1)
                    if ahead:
                        pe.wait_ge(s.max_read, MAXES * (w + 1) + TURN_MAX - 2)
                    pe.transpose(m_bank[0:NQ * CHUNK_TILES, 0:P], neg_max[par][:, :], g.ident[:]).then_inc(s.mt_done, 1)

                def scores(k, w, j, n, pair, between=None):
                    wait(pe, s.exp_done, 2 * STEPS * w + 2 * n + pair - 1)
                    if n == 0 and pair == 0:
                        pe.wait_ge(m_loaded[k % 2], 16 * PIECES * (2 * j + k // 2 + 1))
                        pe.wait_ge(kt_loaded[k // 2], 16 * PIECES * (j + 1))
                    for q in range(2):
                        if q and between:
                            between()
                        last = pe.matmul(st_bank[pair][:, q, :], k_st[k // 2][:, n * P:(n + 1) * P],
                                         q_stack[k][:, 2 * pair + q, :], start=True, stop=True)
                    last.then_inc(s.st_done, 1)

                def values(u, w, n, head):
                    pe.wait_ge(s.exp_done, 2 * STEPS * w + 2 * n + 2)
                    if n == 0:
                        wait(pe, s.o_copied, w)
                        pe.wait_ge(s.v_ready, head + 1)
                    for q in range(NQ):
                        last = pe.matmul(o_bank[32 * q:32 * q + 32, :], v_stack[u][:, n, :], probs[n % 2][:, q, :],
                                         start=(n == 0), stop=(n == STEPS - 1))
                    last.then_inc(s.pv_done, 1)

                def turn_outputs(par, w, ahead):
                    pe.wait_ge(s.o_copied, w + 1)
                    wait(pe, s.norm_done, w)
                    if ahead:
                        pe.wait_ge(s.max_read, MAXES * (w + 2) + TURN_OUT - 2)
                    for t in range(CHUNK_TILES):
                        last = pe.transpose(t_bank[:, t * P:(t + 1) * P], o_sb[par][:, t * P:(t + 1) * P], g.ident[:])
                    last.then_inc(s.ot_done, 1)

                for m in range(MAXES):
                    max_scores(0, 0, 0, m)
                for m in range(SHIFT):
                    if m == TURN_MAX - 1:
                        turn_max(0, 0, True)
                    max_scores(1, 1, 0, m)

                def body(j):
                    for k in range(4):
                        w = 4 * j + k
                        for n in range(STEPS):
                            def maxima(m):
                                unit, m = divmod(4 * n + m + SHIFT, MAXES)
                                unit += 1
                                if after(j, w, k, unit):
                                    max_scores((k + unit) % 4, w + unit, j + (k + unit) // 4, m)
                            maxima(0)
                            scores(k, w, j, n, 0)
                            maxima(1)
                            scores(k, w, j, n, 1, lambda: maxima(2))
                            slot = (4 * n + 4 + SHIFT) % MAXES
                            if slot == TURN_MAX and after(j, w, k, 1):
                                turn_max((k + 1) % 2, w + 1, after(j, w, k, 2))
                            if slot == TURN_OUT and not (isinstance(j, int) and j == 0 and k == 0):
                                turn_outputs((k + 1) % 2, w - 1, after(j, w, k, 1))
                            maxima(3)
                            if n > 0:
                                values(k // 2, w, n - 1, 2 * j + k // 2)
                            elif not (isinstance(j, int) and j == 0 and k == 0):
                                values((k + 3) % 4 // 2, w - 1, STEPS - 1, 2 * j + (k - 1) // 2)
                each_pair(pe, body)
                values(1, units - 1, STEPS - 1, heads - 1)
                turn_outputs((units - 1) % 2, units - 1, False)

            @block.scalar
            def _(act):
                def copy_outputs(par, w):
                    act.wait_ge(s.pv_done, STEPS * (w + 1))
                    wait(act, s.ot_done, w - 1)
                    act.activation(o_sb[par][:, :], o_bank[:, :], ACT.Copy).then_inc(s.o_copied, 1)

                def body(j):
                    for k in range(4):
                        w = 4 * j + k
                        for n in range(STEPS):
                            for pair in range(2):
                                act.wait_ge(s.st_done, 2 * STEPS * w + 2 * n + pair + 1)
                                wait(act, s.pv_done, STEPS * w + n - 1)
                                act.activation(probs[n % 2][:, 2 * pair:2 * pair + 2, :], st_bank[pair][:, :, :],
                                               ACT.Exp, scale=SM_SCALE).then_inc(s.exp_done, 1)
                            if n == 0 and not (isinstance(j, int) and j == 0 and k == 0):
                                copy_outputs((k + 1) % 2, w - 1)
                each_pair(act, body)
                copy_outputs((units - 1) % 2, units - 1)

            @block.vector
            def _(dve):
                def take_max(w, m):
                    if m == 0:
                        wait(dve, s.negm_done, w)
                    dve.wait_ge(s.mx_done, MAXES * w + m + 1)
                    dve.tensor_reduce(partial_max[:, m // 2, m % 2:m % 2 + 1], mx_bank[m % 3][:, :], AX.X,
                                      ALU.max).then_inc(s.max_read, 1)

                def join_max(par, w):
                    dve.wait_ge(s.max_read, MAXES * (w + 1))
                    dve.tensor_reduce(neg_max[par][:, :], partial_max[:, :, :], AX.X, ALU.max,
                                      negate=True).then_inc(s.negm_done, 1)

                def split_max(par, w, sent, links):
                    own = Chain(dve, s.m_own, links)
                    dve.wait_ge(s.mt_done, w + 1)
                    wait(dve, m_loaded[par], 16 * PIECES * sent)
                    m, turned = m_pieces[par], m_bank[0:NQ * CHUNK_TILES, 0:P]
                    own.link(dve.tensor_copy(m[:, 0, :], turned))
                    dve.tensor_tensor(m_rest[:, :], turned, m[:, 0, :], ALU.subtract).then_inc(s.mt_read, 1)
                    dve.wait_ge(s.mt_read, w + 1)
                    own.link(dve.tensor_copy(m[:, 1, :], m_rest[:, :]))
                    dve.tensor_tensor(m[:, 2, :], m_rest[:, :], m[:, 1, :], ALU.subtract).then_inc(s.m_pieces_ready, 1)

                def normalise(w, k):
                    dve.wait_ge(s.ot_done, w + 1)
                    turned = t_bank[:, :].rearrange("p (t q c) -> p t q c", t=CHUNK_TILES, q=NQ)
                    dve.reciprocal(rsum[:, :, :], turned[:, :, :, DH]).then_inc(s.rsum_done, 1)
                    dve.wait_ge(s.rsum_done, w + 1)
                    wait(dve, s.joined, w - 3)
                    dve.tensor_tensor(out[k][:, :, :, :], turned[:, :, :, 0:DH],
                                      rsum[:, :, :].unsqueeze(3).to_broadcast([P, CHUNK_TILES, NQ, DH]),
                                      ALU.mult).then_inc(s.norm_done, 1)

                for m in range(MAXES):
                    take_max(0, m)
                join_max(0, 0)
                for m in range(SHIFT):
                    if m == TURN_MAX - 1:
                        split_max(0, 0, 0, 0)
                    take_max(1, m)

                def body(j):
                    for k in range(4):
                        w = 4 * j + k
                        for slot in range(MAXES):
                            unit, m = divmod(slot + SHIFT, MAXES)
                            unit += 1
                            if m == TURN_MAX - 1 and after(j, w, k, 1):
                                split_max((k + 1) % 2, w + 1, 2 * j + (k + 1) // 2, 2 * (w + 1))
                            if m == TURN_OUT - 1 and not (isinstance(j, int) and j == 0 and k == 0):
                                normalise(w - 1, (k + 3) % 4)
                            if after(j, w, k, unit):
                                take_max(w + unit, m)
                                if m == MAXES - 1:
                                    join_max((k + 1) % 2, w + 1)
                each_pair(dve, body)
                beside.tail(dve)
                normalise(units - 1, 3)


EXPERTS, TOP_K, INNER = 32, 4, 128
ROW_TILES = TOKENS * TOP_K // P + EXPERTS


def dispatch(nc, g, a, load):
    with ExitStack() as ctx:
        sb = lambda name, shape, dt=F32: ctx.enter_context(nc.sbuf_tensor(name, shape, dt))
        sem = lambda name: ctx.enter_context(nc.semaphore(name))
        prefix = ctx.enter_context(nc.psum_tensor("prefix", [P, TILES, EXPERTS], F32))
        total = ctx.enter_context(nc.psum_tensor("total", [P, TILES, EXPERTS], F32))
        top = sb("top", [P, TILES, 8])
        top_at = sb("top_at", [P, TILES, 8], U32)
        at = sb("at", [P, TOP_K, TILES])
        less = sb("less", [P, TILES, TOP_K])
        power = sb("power", [P, TILES, TOP_K])
        norm = sb("norm", [P, TILES, 2])
        lane = sb("lane", [P, EXPERTS])
        before, all_rows = sb("before", [P, P], BF16), sb("all_rows", [P, P], BF16)
        ones = sb("ones", [P, P])
        zeros = sb("zeros", [ROW_TILES, P])
        chosen = sb("chosen", [P, TOP_K, TILES, EXPERTS])
        mask = sb("mask", [P, TILES, EXPERTS])
        mask_bf = sb("mask_bf", [P, TILES, EXPERTS], BF16)
        slot_of = sb("slot_of", [P, TILES, EXPERTS])
        start = sb("start", [P, 6, EXPERTS])
        tiles_i = sb("tiles_i", [P, EXPERTS], I32)
        picked = sb("picked", [P, TOP_K, TILES, EXPERTS])
        slot_f = sb("slot_f", [P, TOP_K, TILES])
        names = "consts table_zeroed top_done less_ready power_ready own mask_ready counted slots_ready"
        s = named(names, lambda n: sem("d_" + n))

        with nc.Block() as block:
            @block.gpsimd
            def _(pool):
                pool.memset(zeros[:], 0.0).then_inc(s.consts, 1)
                pool.iota(lane[:], [[1, EXPERTS]], base=0, channel_multiplier=0,
                          allow_small_or_imprecise_dtypes=True).then_inc(s.consts, 1)
                pool.iota(g.tile_no[:], [[1, ROW_TILES]], base=0, channel_multiplier=0,
                          allow_small_or_imprecise_dtypes=True).then_inc(s.consts, 1)
                pool.iota(g.row_no[:], [[P, TILES]], base=0, channel_multiplier=1,
                          allow_small_or_imprecise_dtypes=True).then_inc(s.consts, 1)
                pool.memset(ones[:], 1.0).then_inc(s.consts, 1)
                pool.memset(all_rows[:], 1.0).then_inc(s.consts, 1)
                pool.wait_ge(s.consts, 6)
                pool.affine_select(out=before[:], in_=all_rows[:], compare_op=ALU.is_gt, fill=0.0, base=0,
                                   pattern=[[1, P]], channel_multiplier=-1).then_inc(s.consts, 1)
            @block.sync
            def _(sp):
                load(sp)
                sp.wait_ge(s.consts, 1)
                sp.dma_start(a.slot_row.rearrange("(j p) o -> j (p o)", p=P), zeros[:]).then_inc(s.table_zeroed, 16)
                sp.wait_ge(s.table_zeroed, 16)

            @block.scalar
            def _(act):
                act.wait_ge(s.less_ready, 1)
                act.activation(power[:], less[:], ACT.Exp).then_inc(s.power_ready, 1)

            @block.tensor
            def _(pe):
                pe.wait_ge(s.mask_ready, 1)
                pe.wait_ge(s.consts, 7)
                flat = mask_bf[:].rearrange("p t e -> p (t e)")
                pe.matmul(prefix[:].rearrange("p t e -> p (t e)"), before[:], flat, start=True, stop=True).then_inc(s.counted, 1)
                pe.matmul(total[:].rearrange("p t e -> p (t e)"), all_rows[:], flat, start=True, stop=True).then_inc(s.counted, 1)

            @block.vector
            def _(dve):
                own = Chain(dve, s.own)
                for t in range(TILES):
                    dve.max(top[:, t, :], g.logits[:, t, :]).then_inc(s.top_done, 1)
                dve.wait_ge(s.top_done, TILES)
                for t in range(TILES):
                    last = dve.max_index(top_at[:, t, :], top[:, t, :], g.logits[:, t, :])
                own.link(last)
                dve.tensor_tensor(less[:], top[:, :, 0:TOP_K], top[:, :, 0:1].to_broadcast([P, TILES, TOP_K]),
                                  ALU.subtract).then_inc(s.less_ready, 1)
                own.link(dve.tensor_copy(at[:], top_at[:, :, 0:TOP_K].rearrange("p t k -> p k t")))
                dve.wait_ge(s.consts, 7)
                for k in range(TOP_K):
                    own.link(dve.tensor_tensor(chosen[:, k, :, :], lane[:].unsqueeze(1).to_broadcast([P, TILES, EXPERTS]),
                                               at[:, k, :].unsqueeze(2).to_broadcast([P, TILES, EXPERTS]), ALU.is_equal))
                own.link(dve.tensor_tensor(mask[:], chosen[:, 0, :, :], chosen[:, 1, :, :], ALU.add))
                own.link(dve.tensor_tensor(mask[:], mask[:], chosen[:, 2, :, :], ALU.add))
                dve.tensor_tensor(mask_bf[:], mask[:], chosen[:, 3, :, :], ALU.add).then_inc(s.mask_ready, 1)
                dve.wait_ge(s.power_ready, 1)
                own.link(dve.tensor_reduce(norm[:, :, 0], power[:], AX.X, ALU.add))
                own.link(dve.reciprocal(norm[:, :, 1], norm[:, :, 0]))
                own.link(dve.tensor_tensor(g.weight[:], power[:], norm[:, :, 1:2].to_broadcast([P, TILES, TOP_K]), ALU.mult))
                dve.wait_ge(s.counted, 2)
                own.link(dve.memset(slot_of[:, 0, :], 0.0))
                for t in range(1, TILES):
                    own.link(dve.tensor_tensor(slot_of[:, t, :], total[:, t - 1, :], slot_of[:, t - 1, :], ALU.add))
                own.link(dve.tensor_tensor(start[:, 0, :], total[:, TILES - 1, :], slot_of[:, TILES - 1, :], ALU.add))
                own.link(dve.tensor_scalar(tiles_i[:], start[:, 0, :], float(P - 1), None, ALU.add))
                own.link(dve.tensor_scalar(tiles_i[:], tiles_i[:], 7, None, ALU.arith_shift_right))
                own.link(dve.tensor_copy(start[:, 1, :], tiles_i[:]))
                own.link(dve.tensor_tensor_scan(g.tiles_end[:], ones[:, 0:EXPERTS], start[:, 1, :], 0.0, ALU.mult, ALU.add))
                own.link(dve.tensor_tensor(start[:, 3, :], g.tiles_end[:], start[:, 1, :], ALU.subtract))
                own.link(dve.tensor_scalar(start[:, 4, :], start[:, 3, :], float(P), None, ALU.mult))
                own.link(dve.tensor_tensor(slot_of[:], slot_of[:], prefix[:], ALU.add))
                own.link(dve.tensor_tensor(slot_of[:], slot_of[:], start[:, 4:5, :].to_broadcast([P, TILES, EXPERTS]), ALU.add))
                for k in range(TOP_K):
                    own.link(dve.tensor_tensor(picked[:, k, :, :], chosen[:, k, :, :], slot_of[:], ALU.mult))
                own.link(dve.tensor_reduce(slot_f[:].rearrange("p k t -> p (k t)"),
                                           picked[:].rearrange("p k t e -> p (k t) e"), AX.X, ALU.add))
                dve.tensor_copy(g.slot[:], slot_f[:]).then_inc(s.slots_ready, 1)


class NumberSlots:

    def __init__(self, nc, g, a, ctx):
        self.g, self.a = g, a
        self.slots_now = [ctx.enter_context(nc.sbuf_tensor(f"slots_now{i}", [P, 1], I32)) for i in range(TOP_K)]
        self.row_now = ctx.enter_context(nc.sbuf_tensor("row_now", [P, 2], F32))
        self.now_ready = ctx.enter_context(nc.semaphore("now_ready"))
        self.scattered = ctx.enter_context(nc.semaphore("scattered"))
        self.own = ctx.enter_context(nc.semaphore("tile_expert_own"))
        self.ended = ctx.enter_context(nc.sbuf_tensor("ended", [P, ROW_TILES, EXPERTS], F32))
        self.expert = ctx.enter_context(nc.sbuf_tensor("expert_f", [P, ROW_TILES], F32))

    def head(self, pool, head):
        g, a = self.g, self.a
        for u in range(TILES // NKV):
            t = head * (TILES // NKV) + u
            wait_own(pool, g.passed, self.scattered, t * (16 * TOP_K))
            for k in range(TOP_K):
                pool.tensor_copy(self.slots_now[k][:], g.slot[:, k, bass.ds(t, 1)]).then_inc(self.now_ready, 1)
            pool.tensor_copy(self.row_now[:, 0:1], g.row_no[:, bass.ds(t, 1)]).then_inc(self.now_ready, 1)
            wait_own(pool, g.passed, self.now_ready, (t + 1) * (TOP_K + 1))
            for k in range(TOP_K):
                pool.indirect_dma_start(a.slot_row, bass.IndirectOffsetOnAxis(self.slots_now[k][:], 0),
                                        self.row_now[:, 0:1], None).then_inc(self.scattered, 16)
                if k % 2:
                    expert = 2 * t + k // 2
                    pool.dma_start(g.wgu[:, bass.ds(expert, 1), :, :], a.wgu[:, bass.ds(expert, 1), :, :]).then_inc(g.experts_loaded, 16)
                    pool.dma_start(g.wd[:, bass.ds(expert, 1), :], a.wd[:, bass.ds(expert, 1), :]).then_inc(g.experts_loaded, 16)

    def end(self, pool):
        pool.wait_ge(self.scattered, 16 * TOP_K * TILES)

    def tail(self, dve):
        g, own = self.g, Chain(dve, self.own)
        own.link(dve.tensor_tensor(self.ended[:], g.tile_no[:].unsqueeze(2).to_broadcast([P, ROW_TILES, EXPERTS]),
                                   g.tiles_end[:].unsqueeze(1).to_broadcast([P, ROW_TILES, EXPERTS]), ALU.is_ge))
        own.link(dve.tensor_reduce(self.expert[:], self.ended[:], AX.X, ALU.add))
        own.link(dve.tensor_scalar(g.tile_expert[:], self.expert[:], float(EXPERTS - 1), None, ALU.min))


class AddExperts:

    def __init__(self, nc, g, a, ctx):
        self.g, self.a = g, a
        sb = lambda name, shape, dt=F32: ctx.enter_context(nc.sbuf_tensor(name, shape, dt))
        sem = lambda name: ctx.enter_context(nc.semaphore(name))
        self.slots_now = [sb(f"c_slots{i}", [P, 1], I32) for i in range(TOP_K)]
        self.part = [sb(f"part{i}", [P, D]) for i in range(TOP_K)]
        self.slot_at, self.weighted, self.added = sem("c_slot_at"), sem("c_weighted"), sem("c_added")
        self.counted = sem("c_counted")
        self.gathered = [sem(f"c_gathered{i}") for i in range(TOP_K)]

    def head(self, pool, head):
        g, a = self.g, self.a
        for u in range(TILES // NKV):
            t = head * (TILES // NKV) + u
            wait_own(pool, g.passed, self.added, TOP_K * t)
            for k in range(TOP_K):
                pool.tensor_copy(self.slots_now[k][:], g.slot[:, k, bass.ds(t, 1)]).then_inc(self.slot_at, 1)
            wait_own(pool, g.passed, self.slot_at, TOP_K * (t + 1))
            for k in range(TOP_K):
                pool.indirect_dma_start(self.part[k][:], None, a.expert_out,
                                        bass.IndirectOffsetOnAxis(self.slots_now[k][:], 0)).then_inc(self.gathered[k], 16)
            row = g.acc[:, bass.ds(t, 1), :].rearrange("p x c -> p (x c)")
            for k in range(TOP_K):
                wait_own(pool, g.passed, self.gathered[k], 16 * (t + 1))
                weight = g.weight[:, bass.ds(t, 1), k:k + 1].rearrange("p x k -> p (x k)").to_broadcast([P, D])
                pool.tensor_tensor(self.part[k][:], self.part[k][:], weight, ALU.mult).then_inc(self.weighted, 1)
            for k in range(TOP_K):
                wait_own(pool, g.passed, self.weighted, TOP_K * t + k + 1)
                wait_own(pool, g.passed, self.added, TOP_K * t + k)
                pool.tensor_tensor(row, row, self.part[k][:], ALU.add).then_inc(self.added, 1)
        wait_own(pool, g.passed, self.added, TOP_K * (TILES // NKV) * (head + 1))

    def end(self, pool):
        pool.wait_ge(self.added, TOP_K * TILES)

    def tail(self, dve):
        dve.wait_ge(self.added, TOP_K * TILES // BATCH)
        for t in range(TILES // BATCH):
            dve.bn_stats(self.g.bn[:, t, :], self.g.acc[:, t, :]).then_inc(self.counted, 1)


def read_table(nc, g, a):
    with ExitStack() as ctx:
        rows_back = ctx.enter_context(nc.sbuf_tensor("rows_back", [ROW_TILES, P], F32))
        turned = ctx.enter_context(nc.psum_tensor("turned", [P, ROW_TILES], F32))
        table_back, table_turned = ctx.enter_context(nc.semaphore("table_back")), ctx.enter_context(nc.semaphore("table_turned"))
        with nc.Block() as block:
            @block.sync
            def _(sp):
                sp.dma_start(rows_back[:], a.slot_row.rearrange("(j p) o -> j (p o)", p=P)).then_inc(table_back, 16)

            @block.tensor
            def _(pe):
                pe.wait_ge(table_back, 16)
                pe.transpose(turned[:, :], rows_back[:], g.ident[0:ROW_TILES, 0:ROW_TILES]).then_inc(table_turned, 1)

            @block.vector
            def _(dve):
                dve.wait_ge(table_turned, 1)
                dve.tensor_copy(g.tile_rows[:], turned[:]).then_inc(table_turned, 1)


def experts(nc, g, a, load):
    STAGES, TURN = 4, 8
    with ExitStack() as ctx:
        sb = lambda name, shape, dt=F32: ctx.enter_context(nc.sbuf_tensor(name, shape, dt))
        sem = lambda name: ctx.enter_context(nc.semaphore(name))
        two = lambda name, cols: [ctx.enter_context(nc.psum_tensor(f"{name}{i}", [P, HALF], F32))[:, 0:cols]
                                   for i in range(2)]
        xt_ps, gu_ps, ht_ps, y_ps = two("xt_ps", D), two("gu_ps", 2 * INNER), two("ht_ps", INNER), two("y_ps", D)
        rows_now = [sb(f"rows_now{i}", [P, 1], I32) for i in range(4)]
        rows = [sb(f"rows{i}", [P, D]) for i in range(4)]
        xt = [sb(f"xt{i}", [P, KD, P]) for i in range(2)]
        silu = [sb(f"silu{i}", [P, INNER]) for i in range(2)]
        h = [sb(f"h{i}", [P, INNER]) for i in range(2)]
        ht = [sb(f"ht{i}", [P, INNER]) for i in range(2)]
        y = [sb(f"y{i}", [P, D]) for i in range(4)]
        names = ("rows_at xt_turned xt_ready gu_done silu_done h_ready h_turned ht_ready y_done y_ready")
        s = named(names, lambda n: sem("e_" + n))
        gathered = [sem(f"e_gathered{i}") for i in range(4)]
        stored = [sem(f"e_stored{i}") for i in range(4)]

        def tiles(engine, body, lag):
            for n in range(TURN):
                body(n // 4, n, n)
            with engine.Fori(1, ROW_TILES // TURN) as turn:
                for u in range(TURN):
                    body(turn * (TURN // 4) + u // 4, turn * TURN + u, u)
            for n in range(ROW_TILES, ROW_TILES + lag):
                body(n // 4, n, n % TURN)

        with nc.Block() as block:
            @block.gpsimd
            def _(pool):
                def body(j, n, u):
                    wait_own(pool, g.passed, s.xt_turned, n - 3)
                    pool.tensor_copy(rows_now[u % 4][:], g.tile_rows[:, bass.ds(n, 1)]).then_inc(s.rows_at, 1)
                    wait_own(pool, g.passed, s.rows_at, n + 1)
                    pool.indirect_dma_start(rows[u % 4][:], None, a.xn_flat,
                                            bass.IndirectOffsetOnAxis(rows_now[u % 4][:], 0)).then_inc(gathered[u % 4], 16)
                tiles(pool, body, 0)

            @block.tensor
            def _(pe):
                pe.wait_ge(g.experts_loaded, 32 * EXPERTS)

                def expert_of(m):
                    return nc.values_load(g.tile_expert[0:1, bass.ds(m, 1)], engines=[mybir.EngineType.PE], min_val=0,
                                          max_val=EXPERTS - 1, skip_runtime_bounds_check_because="a count of experts, "
                                          "clamped to the last one")

                held = [None] * TURN

                def body(j, n, u):
                    whole = not isinstance(n, int)
                    gate_tile, down_tile = whole or 0 <= n - 1 < ROW_TILES, whole or 0 <= n - 3 < ROW_TILES
                    gate_expert = expert_of(n - 1) if gate_tile else None
                    down_expert = held[u - 2] if u > 1 else expert_of(n - 3) if down_tile else None
                    held[u] = gate_expert
                    if whole or n < ROW_TILES:
                        pe.wait_ge(gathered[u % 4], 16 * (j + 1))
                        wait(pe, s.xt_ready, n - 1)
                        for k in range(KD):
                            last = pe.transpose(xt_ps[u % 2][:, k * P:(k + 1) * P], rows[u % 4][:, k * P:(k + 1) * P], g.ident[:])
                        last.then_inc(s.xt_turned, 1)
                    if gate_tile:
                        m = n - 1
                        pe.wait_ge(s.xt_ready, m + 1)
                        wait(pe, s.h_ready, m - 1)
                        for k in range(KD):
                            last = pe.matmul(gu_ps[(u - 1) % 2][:, :], xt[(u - 1) % 2][:, k, :],
                                             g.wgu[:, bass.ds(gate_expert, 1), k, :].rearrange("p x c -> p (x c)"),
                                             start=(k == 0), stop=(k == KD - 1))
                        last.then_inc(s.gu_done, 1)
                    if whole or 0 <= n - 2 < ROW_TILES:
                        m = n - 2
                        pe.wait_ge(s.h_ready, m + 1)
                        wait(pe, s.ht_ready, m - 1)
                        pe.transpose(ht_ps[u % 2][:, :], h[u % 2][:, :], g.ident[:]).then_inc(s.h_turned, 1)
                    if down_tile:
                        m = n - 3
                        pe.wait_ge(s.ht_ready, m + 1)
                        wait(pe, s.y_ready, m - 1)
                        pe.matmul(y_ps[(u - 3) % 2][:, :], ht[(u - 3) % 2][:, :],
                                  g.wd[:, bass.ds(down_expert, 1), :].rearrange("p x c -> p (x c)"),
                                  start=True, stop=True).then_inc(s.y_done, 1)
                tiles(pe, body, STAGES - 1)

            @block.scalar
            def _(act):
                def body(j, n, u):
                    whole = not isinstance(n, int)
                    if whole or n < ROW_TILES:
                        act.wait_ge(s.xt_turned, n + 1)
                        wait(act, s.gu_done, n - 1)
                        act.activation(xt[u % 2][:].rearrange("p k c -> p (k c)"), xt_ps[u % 2][:, :],
                                       ACT.Copy).then_inc(s.xt_ready, 1)
                    if whole or 0 <= n - 1 < ROW_TILES:
                        m = n - 1
                        act.wait_ge(s.gu_done, m + 1)
                        wait(act, s.h_ready, m - 1)
                        act.activation(silu[(u - 1) % 2][:], gu_ps[(u - 1) % 2][:, 0:INNER], ACT.Silu).then_inc(s.silu_done, 1)
                    if whole or 0 <= n - 2 < ROW_TILES:
                        m = n - 2
                        act.wait_ge(s.h_turned, m + 1)
                        wait(act, s.y_done, m - 1)
                        act.activation(ht[u % 2][:], ht_ps[u % 2][:, :], ACT.Copy).then_inc(s.ht_ready, 1)
                tiles(act, body, 2)

            @block.vector
            def _(dve):
                def body(j, n, u):
                    whole = not isinstance(n, int)
                    if whole or 0 <= n - 1 < ROW_TILES:
                        m = n - 1
                        dve.wait_ge(s.silu_done, m + 1)
                        wait(dve, s.h_turned, m - 1)
                        dve.tensor_tensor(h[(u - 1) % 2][:], gu_ps[(u - 1) % 2][:, INNER:2 * INNER],
                                          silu[(u - 1) % 2][:], ALU.mult).then_inc(s.h_ready, 1)
                    if whole or 0 <= n - 3 < ROW_TILES:
                        m = n - 3
                        dve.wait_ge(s.y_done, m + 1)
                        wait(dve, stored[(u - 3) % 4], 16 * (j if u % 4 == 3 else j - 1))
                        dve.tensor_copy(y[(u - 3) % 4][:], y_ps[(u - 3) % 2][:, :]).then_inc(s.y_ready, 1)
                tiles(dve, body, 3)

            @block.sync
            def _(sp):
                load(sp)

                def body(j, n, u):
                    sp.wait_ge(s.y_ready, n + 1)
                    sp.dma_start(a.expert_out_tiles[:, bass.ds(n, 1), :].rearrange("p x c -> p (x c)"),
                                 y[u % 4][:]).then_inc(stored[u % 4], 16)
                tiles(sp, body, 0)
                for u in range(4):
                    sp.wait_ge(stored[u], 16 * (ROW_TILES // 4))




HEADS1, DK1 = 16, 16
GROUP = 4
GROUPS = HEADS1 // GROUP
PER_TILE = P // DK1
SCALE1 = DK1 ** -0.5
HIDDEN = 1024
HID_TILES = HIDDEN // P


def second_weights(sp, g, a, first_loaded, loaded):
    for dst, src in ((g.wqkv1, a.wqkv1), (g.feat, a.feat), (g.fbias, a.fbias)):
        sp.dma_start(dst[:], src).then_inc(first_loaded, 16)
    for dst, src in ((g.nw, a.nw), (g.wo1, a.wo1), (g.wg1, a.wg1), (g.wu1, a.wu1), (g.wd1, a.wd1)):
        sp.dma_start(dst[:], src).then_inc(loaded, 16)
    sp.wait_ge(first_loaded, 16 * 3)


def second_masks(pool, g, zeroed, cut):
    pool.memset(g.causal[:], SCALE1).then_inc(zeroed, 1)
    pool.memset(g.same_head[:], 1.0).then_inc(zeroed, 1)
    pool.memset(g.kv_mask[:], SCALE1).then_inc(zeroed, 1)
    pool.memset(g.mean32[:], 1.0 / DK1).then_inc(zeroed, 1)
    pool.memset(g.eps[:], EPS).then_inc(zeroed, 1)
    pool.wait_ge(zeroed, 5)
    pool.affine_select(out=g.causal[:], in_=g.causal[:], compare_op=ALU.is_ge, fill=0.0, base=0,
                       pattern=[[1, P]], channel_multiplier=-1).then_inc(cut, 1)
    pool.affine_select(out=g.same_head[:], in_=g.same_head[:], compare_op=ALU.is_ge, fill=0.0, base=0,
                       pattern=[[-DK1, PER_TILE]], channel_multiplier=1).then_inc(cut, 1)
    pool.wait_ge(cut, 2)
    pool.affine_select(out=g.same_head[:], in_=g.same_head[:], compare_op=ALU.is_ge, fill=0.0,
                       base=DK1 - 1, pattern=[[DK1, PER_TILE]], channel_multiplier=-1).then_inc(cut, 1)
    pool.affine_select(out=g.kv_mask[:], in_=g.kv_mask[:], compare_op=ALU.is_ge, fill=0.0, base=0,
                       pattern=[[-DK1, PER_TILE], [0, DK1]], channel_multiplier=1).then_inc(cut, 1)
    pool.wait_ge(cut, 4)
    pool.affine_select(out=g.kv_mask[:], in_=g.kv_mask[:], compare_op=ALU.is_ge, fill=0.0,
                       base=DK1 - 1, pattern=[[DK1, PER_TILE], [0, DK1]],
                       channel_multiplier=-1).then_inc(cut, 1)
    pool.affine_select(out=g.mean32[:], in_=g.mean32[:], compare_op=ALU.is_ge, fill=0.0, base=0,
                       pattern=[[-32, GROUP], [0, 32]], channel_multiplier=1).then_inc(cut, 1)
    pool.wait_ge(cut, 6)
    pool.affine_select(out=g.mean32[:], in_=g.mean32[:], compare_op=ALU.is_ge, fill=0.0,
                       base=31, pattern=[[32, GROUP], [0, 32]], channel_multiplier=-1).then_inc(cut, 1)


def split_second(g, first_loaded, high_ready, rest_ready):
    parts = ((g.wqkv_high, g.wqkv_rest, g.wqkv1), (g.feat_high, g.feat_rest, g.feat))

    def highs(act):
        act.wait_ge(first_loaded, 16 * 3)
        for high, _, w in parts:
            act.activation(high[:], w[:], ACT.Copy).then_inc(high_ready, 1)

    def rests(dve):
        for i, (high, rest, w) in enumerate(parts):
            dve.wait_ge(high_ready, i + 1)
            dve.tensor_tensor(rest[:], w[:], high[:].bitcast(F32), ALU.subtract).then_inc(rest_ready, 1)
    return rests, highs


def products(pe, out, left, right, start, stop):
    pe.matmul(out, left[0], right[0], start=start, stop=False)
    pe.matmul(out, left[0], right[1], start=False, stop=False)
    return pe.matmul(out, left[1], right[0], start=False, stop=stop)


def project_second(nc, g, a):
    CHUNKS = TOKENS // HALF
    with ExitStack() as ctx:
        sb = lambda name, shape, dt=F32: ctx.enter_context(nc.sbuf_tensor(name, shape, dt))
        sem = lambda name: ctx.enter_context(nc.semaphore(name))
        bank = [ctx.enter_context(nc.psum_tensor(f"ps{i}", [P, HALF], F32)) for i in range(8)]
        xn = sb("ps_xn", [P, CHUNK_TILES, D])
        x_high, x_rest = sb("ps_xh", [P, KD, HALF], F32R), sb("ps_xr", [P, KD, HALF], F32R)
        qk_high, qk_rest = sb("ps_qkh", [P, 4, HALF], F32R), sb("ps_qkr", [P, 4, HALF], F32R)
        wqkv, feat = (g.wqkv_high[:], g.wqkv_rest[:]), (g.feat_high[:], g.feat_rest[:])
        f2 = sb("ps_f2", [P, 2, HALF])
        kf = sb("ps_kf", [P, KD, HALF])
        names = ("xn_ready xt_ps x_high_ready x_rest_ready x_kept qk_ps qk_high_ready qk_ready feat_ps f2_ready feat_ready v_ps v_ready kt_ps kt_ready "
                 "kf_kept")
        s = named(names, lambda n: sem("ps_" + n))

        def chunks(engine, body):
            body(0, True)
            with engine.Fori(1, CHUNKS - 1) as n:
                body(n, True)
            body(CHUNKS - 1, False)

        with nc.Block() as block:
            @block.tensor
            def _(pe):
                def turn(n):
                    pe.wait_ge(s.xn_ready, 4 * n + 4)
                    wait(pe, s.v_ready, 2 * n)
                    for k in range(KD):
                        for t in range(CHUNK_TILES):
                            last = pe.transpose(bank[k][:, t * P:(t + 1) * P], xn[:, t, k * P:(k + 1) * P], g.ident[:])
                        last.then_inc(s.xt_ps, 1)

                def projection(n, c):
                    wait(pe, s.qk_ready, 4 * n + c - 1)
                    for k in range(KD):
                        last = products(pe, bank[2 + c % 2][:, :], [w[:, k, c * P:(c + 1) * P] for w in wqkv],
                                        (x_high[:, k, :], x_rest[:, k, :]), k == 0, k == KD - 1)
                    last.then_inc(s.qk_ps, 1)

                def features(n, c):
                    pe.wait_ge(s.qk_ready, 4 * n + c + 1)
                    wait(pe, s.feat_ready, 4 * n + c - 1)
                    if c == 0:
                        wait(pe, s.kt_ready, 2 * n)
                    for f in range(2):
                        last = products(pe, bank[4 + c % 2 * 2 + f][:, :], [w[:, c // 2 * 2 + f, :] for w in feat],
                                        (qk_high[:, c, :], qk_rest[:, c, :]), True, True)
                    last.then_inc(s.feat_ps, 1)

                def values(n):
                    for t in range(CHUNK_TILES):
                        for k in range(KD):
                            rows = slice(t * P, (t + 1) * P)
                            last = products(pe, bank[t // 2][:, t % 2 * D:(t % 2 + 1) * D],
                                            (x_high[:, k, rows], x_rest[:, k, rows]),
                                            [w[:, k, 2 * D:3 * D] for w in wqkv], k == 0, k == KD - 1)
                        if t % 2:
                            last.then_inc(s.v_ps, 1)

                def turn_features(n):
                    pe.wait_ge(s.feat_ready, 4 * n + 4)
                    for t in range(CHUNK_TILES):
                        for c in range(KD):
                            last = pe.transpose(bank[4 + t // 2][:, (t % 2 * 2 + c) * P:(t % 2 * 2 + c + 1) * P],
                                                kf[:, c, t * P:(t + 1) * P], g.ident[:])
                        if t % 2:
                            last.then_inc(s.kt_ps, 1)

                def body(n, more):
                    pe.wait_ge(s.x_rest_ready, 2 * n + 2)
                    projection(n, 0)
                    projection(n, 1)
                    features(n, 0)
                    projection(n, 2)
                    features(n, 1)
                    projection(n, 3)
                    features(n, 2)
                    values(n)
                    features(n, 3)
                    if more:
                        turn(n + 1)
                    turn_features(n)
                turn(0)
                chunks(pe, body)

            @block.scalar
            def _(act):
                def keep_rows(n):
                    wait(act, s.v_ps, 2 * n)
                    wait(act, s.x_kept, 2 * n)
                    for k in range(KD):
                        act.wait_ge(s.xt_ps, 2 * n + k + 1)
                        act.activation(x_high[:, k, :], bank[k][:, :], ACT.Copy).then_inc(s.x_high_ready, 1)

                def keep_projection(n, c):
                    act.wait_ge(s.qk_ps, 4 * n + c + 1)
                    wait(act, s.feat_ps, 4 * n + c - 3)
                    act.activation(qk_high[:, c, :], bank[2 + c % 2][:, :], ACT.Copy).then_inc(s.qk_high_ready, 1)

                def second_map(n, c):
                    act.wait_ge(s.feat_ps, 4 * n + c + 1)
                    wait(act, s.feat_ready, 4 * n + c - 1)
                    act.activation(f2[:, c % 2, :], bank[5 + c % 2 * 2][:, :], ACT.Identity,
                                   bias=g.fbias[:, c // 2 * 2 + 1:c // 2 * 2 + 2]).then_inc(s.f2_ready, 1)

                def body(n, more):
                    keep_projection(n, 0)
                    keep_projection(n, 1)
                    second_map(n, 0)
                    keep_projection(n, 2)
                    second_map(n, 1)
                    keep_projection(n, 3)
                    second_map(n, 2)
                    for i in range(2):
                        act.wait_ge(s.v_ps, 2 * n + i + 1)
                        act.activation(g.v_all[:, bass.ds(4 * n + 2 * i, 2), :].rearrange("p t c -> p (t c)"),
                                       bank[i][:, :], ACT.Copy).then_inc(s.v_ready, 1)
                    second_map(n, 3)
                    if more:
                        keep_rows(n + 1)
                    for i in range(2):
                        act.wait_ge(s.kt_ps, 2 * n + i + 1)
                        act.activation(g.kt_all[:, bass.ds(4 * n + 2 * i, 2), :].rearrange("p t c -> p (t c)"),
                                       bank[4 + i][:, :], ACT.Copy).then_inc(s.kt_ready, 1)
                keep_rows(0)
                chunks(act, body)

            @block.vector
            def _(dve):
                def normalise(n):
                    wait(dve, s.xt_ps, 2 * n)
                    for t in range(CHUNK_TILES):
                        dve.tensor_scalar(xn[:, t, :], g.acc[:, bass.ds(4 * n + t, 1), :],
                                          g.mean_var[:, bass.ds(4 * n + t, 1), 0:1].rearrange("p a b -> p (a b)"),
                                          g.rstd[:, bass.ds(4 * n + t, 1)],
                                          ALU.subtract, ALU.mult).then_inc(s.xn_ready, 1)

                def rows_rest(n):
                    for k in range(KD):
                        dve.wait_ge(s.x_high_ready, 2 * n + k + 1)
                        dve.tensor_tensor(x_rest[:, k, :], bank[k][:, :], x_high[:, k, :].bitcast(F32),
                                          ALU.subtract).then_inc(s.x_rest_ready, 1)

                def projection_rest(n, c):
                    dve.wait_ge(s.qk_high_ready, 4 * n + c + 1)
                    dve.tensor_tensor(qk_rest[:, c, :], bank[2 + c % 2][:, :], qk_high[:, c, :].bitcast(F32),
                                      ALU.subtract).then_inc(s.qk_ready, 1)

                def product(n, c):
                    dve.wait_ge(s.f2_ready, 4 * n + c + 1)
                    if c == 2:
                        wait(dve, s.kt_ps, 2 * n)
                        wait(dve, s.kf_kept, n)
                    out = g.q_all[:, c, bass.ds(n * HALF, HALF)] if c < 2 else kf[:, c - 2, :]
                    i = c // 2 * 2
                    dve.scalar_tensor_tensor(out=out, in0=bank[4 + c % 2 * 2][:, :], scalar=g.fbias[:, i:i + 1],
                                             in1=f2[:, c % 2, :], op0=ALU.add, op1=ALU.mult).then_inc(s.feat_ready, 1)

                def body(n, more):
                    projection_rest(n, 0)
                    projection_rest(n, 1)
                    product(n, 0)
                    projection_rest(n, 2)
                    product(n, 1)
                    projection_rest(n, 3)
                    if more:
                        normalise(n + 1)
                    product(n, 2)
                    product(n, 3)
                    if more:
                        rows_rest(n + 1)
                normalise(0)
                rows_rest(0)
                chunks(dve, body)

            @block.gpsimd
            def _(pool):
                def body(n, more):
                    wait_own(pool, g.passed, s.x_rest_ready, 2 * n + 2)
                    for kept, x in ((g.xh_all, x_high), (g.xr_all, x_rest)):
                        pool.tensor_copy(kept[:, :, bass.ds(n * HALF, HALF)], x[:].bitcast(F32)).then_inc(s.x_kept, 1)
                    wait_own(pool, g.passed, s.feat_ready, 4 * n + 4)
                    pool.tensor_copy(g.k_all[:, :, bass.ds(n * HALF, HALF)], kf[:]).then_inc(s.kf_kept, 1)
                chunks(pool, body)


def linear_attention(nc, g, a, loaded, loads):
    PAIRS = TILES // 2
    PER_BATCH = TILES // BATCH
    with ExitStack() as ctx:
        sb = lambda name, shape, dt=F32: ctx.enter_context(nc.sbuf_tensor(name, shape, dt))
        sem = lambda name: ctx.enter_context(nc.semaphore(name))
        sc_bank = [[ctx.enter_context(nc.psum_tensor(f"sc{c}{i}", [P, HALF], F32)) for i in range(2)] for c in range(KD)]
        o_bank, kv_bank, msq_bank, wo_bank = (ctx.enter_context(nc.psum_tensor(n, [P, HALF], F32))
                                              for n in ("l_o", "l_kvp", "l_msq", "l_wo"))
        qm = [sb(f"l_qm{i}", [P, PER_TILE, P]) for i in range(KD)]
        sm = [sb(f"l_sm{i}", [P, PER_TILE, P]) for i in range(KD)]
        k_now = [sb(f"l_k{i}", [P, KD, P]) for i in range(2)]
        kt_now = [sb(f"l_kt{i}", [P, KD * P]) for i in range(2)]
        v_now = [sb(f"l_v{i}", [P, D]) for i in range(2)]
        kv = sb("l_kv", [P, KD, PER_TILE, 32])
        kv_new = sb("l_kv_new", [P, KD, PER_TILE, DK1])
        sq = sb("l_sq", [P, HALF])
        o_sb = [sb(f"l_o_sb{i}", [P, HALF]) for i in range(2)]
        rs = sb("l_rs", [P, 2, HALF])
        names = ("staged qm_ready sc_ps sm_ready kv_ps kv_cut kv_ready o_half o_taken sq_ready msq_ps ln_ready rs_ready "
                 "on_ready wo_ps acc_ready")
        s = named(names, lambda n: sem("l_" + n))

        def pairs(engine, body):
            body(0, True, False)
            with engine.Fori(1, PAIRS - 1) as p:
                body(p, False, False)
            body(PAIRS - 1, False, True)

        with nc.Block() as block:
            @block.sync
            def _(sp):
                sp.wait_ge(loaded, loads)

            @block.tensor
            def _(pe):
                def scores(t, u, c):
                    pe.wait_ge(s.staged, 3 * t + 3)
                    pe.wait_ge(s.qm_ready, 2 * t + c + 1)
                    wait(pe, s.sm_ready, 2 * t + c - 1)
                    for half in range(2):
                        last = pe.matmul(sc_bank[c][half][:, :], k_now[u][:, c, :],
                                         qm[c][:, 4 * half:4 * half + 4, :], start=True, stop=True)
                    last.then_inc(s.sc_ps, 1)

                def outputs(t, u, c):
                    if c == 0:
                        pe.wait_ge(s.kv_ready, t + 1)
                        wait(pe, s.o_taken, t)
                    pe.wait_ge(s.sm_ready, 2 * t + c + 1)
                    for gr in (2 * c, 2 * c + 1):
                        o = o_bank[:, gr * P:(gr + 1) * P]
                        pe.matmul(o, kv[:, c, gr % 2 * GROUP:(gr % 2 + 1) * GROUP, :],
                                  g.q_all[:, c, bass.ds(t * P, P)], start=True, stop=False, skip_group_check=True)
                        for h in range(GROUP):
                            head = gr * GROUP + h
                            last = pe.matmul(o[32 * h:32 * h + DK1, :], v_now[u][:, head * DK1:(head + 1) * DK1],
                                             sm[c][:, gr % 2 * GROUP + h, :], start=False, stop=True,
                                             skip_group_check=True)
                    last.then_inc(s.o_half, 1)

                def state(t, u):
                    wait(pe, s.kv_cut, t)
                    for c in range(KD):
                        last = pe.matmul(kv_bank[:, c * P:(c + 1) * P], kt_now[u][:, c * P:(c + 1) * P],
                                         v_now[u][:, c * P:(c + 1) * P], start=True, stop=True)
                    last.then_inc(s.kv_ps, 1)

                def mean_square(t):
                    pe.wait_ge(s.sq_ready, t + 1)
                    wait(pe, s.ln_ready, t)
                    pe.matmul(msq_bank[:, :], g.mean32[:], sq[:], start=True, stop=True).then_inc(s.msq_ps, 1)

                def project_out(t, u):
                    pe.wait_ge(s.on_ready, t + 1)
                    pe.wait_ge(s.acc_ready, t + 1)
                    for gr in range(GROUPS):
                        last = pe.matmul(wo_bank[:, 0:D], o_sb[u][:, gr * P:(gr + 1) * P], g.wo1[:, gr, :],
                                         start=(gr == 0), stop=(gr == GROUPS - 1))
                    last.then_inc(s.wo_ps, 1)

                def body(p, first, last):
                    for u in range(2):
                        t = 2 * p + u
                        scores(t, u, 1)
                        outputs(t, u, 0)
                        if not (last and u):
                            scores(t + 1, 1 - u, 0)
                        outputs(t, u, 1)
                        state(t, u)
                        if not first:
                            project_out(t - 2, u)
                        mean_square(t)
                pe.wait_ge(loaded, loads)
                scores(0, 0, 0)
                pairs(pe, body)
                project_out(TILES - 2, 0)
                project_out(TILES - 1, 1)

            @block.scalar
            def _(act):
                def body(p, first, last):
                    for u in range(2):
                        t = 2 * p + u
                        act.wait_ge(s.o_half, 2 * t + 2)
                        wait(act, s.msq_ps, t)
                        act.activation(sq[:], o_bank[:, :], ACT.Square).then_inc(s.sq_ready, 1)
                        if not first:
                            act.wait_ge(s.wo_ps, t - 1)
                        act.activation(o_sb[u][:], o_bank[:, :], ACT.Copy).then_inc(s.o_taken, 1)
                        act.wait_ge(s.msq_ps, t + 1)
                        if u == 0 and not first:
                            act.wait_ge(s.on_ready, t)
                        act.activation(rs[:, u, :], msq_bank[:, :], ACT.Ln, bias=g.eps[:]).then_inc(s.ln_ready, 1)
                    act.wait_ge(s.ln_ready, 2 * p + 2)
                    act.activation(rs[:], rs[:], ACT.Exp, scale=-0.5).then_inc(s.rs_ready, 1)
                act.wait_ge(loaded, loads)
                pairs(act, body)

            @block.vector
            def _(dve):
                def spread(t, c):
                    wait(dve, s.sc_ps, 2 * t + c - 1)
                    dve.tensor_tensor(qm[c][:], g.q_all[:, c:c + 1, bass.ds(t * P, P)].to_broadcast([P, PER_TILE, P]),
                                      g.same_head[:].unsqueeze(2).to_broadcast([P, PER_TILE, P]),
                                      ALU.mult).then_inc(s.qm_ready, 1)

                def mask(t, c):
                    dve.wait_ge(s.sc_ps, 2 * t + c + 1)
                    wait(dve, s.o_half, 2 * t + c - 1)
                    for half in range(2):
                        last = dve.tensor_tensor(sm[c][:, 4 * half:4 * half + 4, :],
                                                 sc_bank[c][half][:, :].rearrange("p (h c) -> p h c", h=4),
                                                 g.causal[:].unsqueeze(1).to_broadcast([P, 4, P]), ALU.mult)
                    last.then_inc(s.sm_ready, 1)

                def cut_state(t):
                    dve.wait_ge(s.kv_ps, t + 1)
                    dve.wait_ge(s.kv_ready, t + 1)
                    dve.tensor_tensor(kv_new[:].rearrange("p c h e -> p c (h e)"),
                                      kv_bank[:, 0:KD * P].rearrange("p (c e) -> p c e", c=KD),
                                      g.kv_mask[:].rearrange("p h e -> p (h e)").unsqueeze(1).to_broadcast([P, KD, P]),
                                      ALU.mult).then_inc(s.kv_cut, 1)

                def scale(t, u, pair):
                    dve.wait_ge(s.rs_ready, pair + 1)
                    dve.scalar_tensor_tensor(out=o_sb[u][:], in0=o_sb[u][:], scalar=g.nw[:, 0:1], in1=rs[:, u, :],
                                             op0=ALU.mult, op1=ALU.mult).then_inc(s.on_ready, 1)

                def add_rows(t):
                    dve.wait_ge(s.wo_ps, t + 1)
                    row = g.acc[:, bass.ds(t, 1), :].rearrange("p x c -> p (x c)")
                    dve.tensor_tensor(row, row, wo_bank[:, 0:D], ALU.add).then_inc(s.acc_ready, 1)

                def body(p, first, last):
                    for u in range(2):
                        t = 2 * p + u
                        mask(t, 0)
                        if not (last and u):
                            spread(t + 1, 0)
                        mask(t, 1)
                        if not (last and u):
                            spread(t + 1, 1)
                        if not first:
                            scale(t - 2, u, p - 1)
                        cut_state(t)
                        if not first:
                            add_rows(t - 2)
                dve.wait_ge(loaded, loads)
                dve.sem_inc(s.acc_ready, 1)
                spread(0, 0)
                spread(0, 1)
                pairs(dve, body)
                for u in range(2):
                    scale(TILES - 2 + u, u, PAIRS - 1)
                    add_rows(TILES - 2 + u)

            @block.gpsimd
            def _(pool):
                def stage(t, u):
                    wait_own(pool, g.passed, s.o_half, 2 * t - 2)
                    wait_own(pool, g.passed, s.kv_ps, t - 1)
                    pool.tensor_copy(k_now[u][:], g.k_all[:, :, bass.ds(t * P, P)]).then_inc(s.staged, 1)
                    pool.tensor_copy(v_now[u][:], g.v_all[:, bass.ds(t, 1), :].rearrange("p t c -> p (t c)")).then_inc(s.staged, 1)
                    pool.tensor_copy(kt_now[u][:], g.kt_all[:, bass.ds(t, 1), :].rearrange("p t c -> p (t c)")).then_inc(s.staged, 1)

                def used(t):
                    wait_own(pool, g.passed, s.o_half, 2 * t + 2)
                    wait_own(pool, g.passed, s.kv_cut, t + 1)
                    wait_own(pool, g.passed, s.kv_ready, t + 1)

                def add(t):
                    used(t)
                    pool.tensor_tensor(kv[:, :, :, 0:DK1], kv[:, :, :, 0:DK1], kv_new[:], ALU.add).then_inc(s.kv_ready, 1)

                def step(p):
                    for u in range(2):
                        stage(2 * p + u + 1, 1 - u)
                        add(2 * p + u)
                stage(0, 0)
                pool.memset(kv[:], 0.0).then_inc(s.kv_ready, 1)
                step(0)
                half = PER_BATCH // 2
                with pool.Fori(1, half - 1) as p:
                    step(p)
                stage(PER_BATCH - 1, 1)
                add(PER_BATCH - 2)
                stage(PER_BATCH, 0)
                used(PER_BATCH - 1)
                pool.memset(kv[:], 0.0).then_inc(s.kv_ready, 1)
                with pool.Fori(half, PAIRS - 1) as p:
                    step(p)
                stage(TILES - 1, 1)
                add(TILES - 2)


def feed_forward(nc, g, a):
    T = HID_TILES
    with ExitStack() as ctx:
        sb = lambda name, shape, dt=F32: ctx.enter_context(nc.sbuf_tensor(name, shape, dt))
        sem = lambda name: ctx.enter_context(nc.semaphore(name))
        gate = [ctx.enter_context(nc.psum_tensor(f"gate{i}", [P, HALF], F32)) for i in range(2)]
        up = [ctx.enter_context(nc.psum_tensor(f"up{i}", [P, HALF], F32)) for i in range(2)]
        down = [ctx.enter_context(nc.psum_tensor(f"down{i}", [P, HALF], F32)) for i in range(4)]
        silu = [sb(f"f_silu{i}", [P, HALF]) for i in range(2)]
        h = [sb(f"f_h{i}", [P, HALF]) for i in range(2)]
        h_high = [sb(f"f_hh{i}", [P, HALF], F32R) for i in range(2)]
        h_rest = [sb(f"f_hr{i}", [P, HALF], F32R) for i in range(2)]
        wg_high, wg_rest = sb("f_wgh", [P, KD, HIDDEN], F32R), sb("f_wgr", [P, KD, HIDDEN], F32R)
        wu_high, wu_rest = sb("f_wuh", [P, KD, HIDDEN], F32R), sb("f_wur", [P, KD, HIDDEN], F32R)
        wd_high, wd_rest = sb("f_wdh", [P, T, D], F32R), sb("f_wdr", [P, T, D], F32R)
        names = ("w_high w_rest gate_done up_done silu_done h_ready h_high h_rest down_step down_done "
                 "acc_done stored")
        s = named(names, lambda n: sem("f_" + n))

        def weights(i):
            cols = slice(i * P, (i + 1) * P)
            return ((g.wg1[:, :, cols], wg_high[:, :, cols], wg_rest[:, :, cols]),
                    (g.wu1[:, :, cols], wu_high[:, :, cols], wu_rest[:, :, cols]),
                    (g.wd1[:, i, :], wd_high[:, i, :], wd_rest[:, i, :]))

        def chunks(engine, body):
            body(0)
            with engine.Fori(1, TOKENS // HALF) as n:
                body(n)

        def is_first(n):
            return isinstance(n, int)

        with nc.Block() as block:
            @block.tensor
            def _(pe):
                def gate_up(n, i):
                    if is_first(n):
                        pe.wait_ge(s.w_rest, 3 * i + 3)
                    wait(pe, s.h_ready, T * n + i - 1)
                    cols = slice(i * P, (i + 1) * P)
                    for high, rest, out, done in ((wg_high, wg_rest, gate, s.gate_done), (wu_high, wu_rest, up, s.up_done)):
                        for k in range(KD):
                            x = [x_all[:, k, bass.ds(n * HALF, HALF)] for x_all in (g.xh_all, g.xr_all)]
                            last = products(pe, out[i % 2][:, :], (high[:, k, cols], rest[:, k, cols]), x,
                                            k == 0, k == KD - 1)
                        last.then_inc(done, 1)

                def down_part(n, i):
                    pe.wait_ge(s.h_rest, T * n + i + 1)
                    if i == 0:
                        wait(pe, s.acc_done, 4 * n)
                    for t in range(CHUNK_TILES):
                        rows = slice(t * P, (t + 1) * P)
                        last = products(pe, down[t][:, 0:D], (h_high[i % 2][:, rows], h_rest[i % 2][:, rows]),
                                        (wd_high[:, i, :], wd_rest[:, i, :]), i == 0, i == T - 1)
                        if i == T - 1:
                            last.then_inc(s.down_done, 1)
                    if i < T - 1:
                        last.then_inc(s.down_step, 1)

                def body(n):
                    gate_up(n, 0)
                    for i in range(1, T):
                        gate_up(n, i)
                        down_part(n, i - 1)
                    down_part(n, T - 1)
                chunks(pe, body)

            @block.scalar
            def _(act):
                def split_weights(i):
                    for w, high, _ in weights(i):
                        act.activation(high, w, ACT.Copy).then_inc(s.w_high, 1)

                def body(n):
                    if is_first(n):
                        split_weights(0)
                        split_weights(1)
                    for i in range(T):
                        act.wait_ge(s.gate_done, T * n + i + 1)
                        wait(act, s.h_ready, T * n + i - 1)
                        act.activation(silu[i % 2][:], gate[i % 2][:, :], ACT.Silu).then_inc(s.silu_done, 1)
                        if is_first(n) and i + 2 < T:
                            split_weights(i + 2)
                        act.wait_ge(s.h_ready, T * n + i + 1)
                        if i > 1:
                            act.wait_ge(s.down_step, (T - 1) * n + i - 1)
                        else:
                            wait(act, s.down_done, CHUNK_TILES * n)
                        act.activation(h_high[i % 2][:], h[i % 2][:], ACT.Copy).then_inc(s.h_high, 1)
                chunks(act, body)

            @block.vector
            def _(dve):
                def split_weights(i):
                    for m, (w, high, rest) in enumerate(weights(i)):
                        dve.wait_ge(s.w_high, 3 * i + m + 1)
                        dve.tensor_tensor(rest, w, high.bitcast(F32), ALU.subtract).then_inc(s.w_rest, 1)

                def add_rows(n):
                    for t in range(CHUNK_TILES):
                        dve.wait_ge(s.down_done, 4 * n + t + 1)
                        row = g.acc[:, bass.ds(n * 4 + t, 1), :].rearrange("p x c -> p (x c)")
                        dve.tensor_tensor(row, row, down[t][:, 0:D], ALU.add).then_inc(s.acc_done, 1)

                def body(n):
                    if is_first(n):
                        split_weights(0)
                        split_weights(1)
                    else:
                        add_rows(n - 1)
                    for i in range(T):
                        dve.wait_ge(s.silu_done, T * n + i + 1)
                        dve.wait_ge(s.up_done, T * n + i + 1)
                        wait(dve, s.h_rest, T * n + i - 1)
                        dve.tensor_tensor(h[i % 2][:], up[i % 2][:, :], silu[i % 2][:], ALU.mult).then_inc(s.h_ready, 1)
                        if is_first(n) and i + 2 < T:
                            split_weights(i + 2)
                        dve.wait_ge(s.h_high, T * n + i + 1)
                        dve.tensor_tensor(h_rest[i % 2][:], h[i % 2][:], h_high[i % 2][:].bitcast(F32),
                                          ALU.subtract).then_inc(s.h_rest, 1)
                chunks(dve, body)
                add_rows(TOKENS // HALF - 1)

            @block.sync
            def _(sp):
                def body(n):
                    sp.wait_ge(s.acc_done, 4 * n + 4)
                    sp.dma_start(a.out[:, bass.ds(n * 4, 4), :], g.acc[:, bass.ds(n * 4, 4), :]).then_inc(s.stored, 16)
                chunks(sp, body)
                sp.wait_ge(s.stored, 16 * (TOKENS // HALF))


def build(nc, a):
    g = Buffers()
    with ExitStack() as ctx:
        def sb(name, shape, dt=F32, scope=ctx):
            return scope.enter_context(nc.sbuf_tensor(name, shape, dt))

        g.passed = ctx.enter_context(nc.semaphore("pool_passed"))
        g.experts_loaded = ctx.enter_context(nc.semaphore("experts_loaded"))
        g.acc = sb("acc", [P, TILES, D])
        g.ident = sb("ident", [P, P])
        g.mean_var = sb("mean_var", [P, TILES, 2])
        g.rstd = sb("rstd", [P, TILES])
        g.bn = sb("bn", [P, TILES, 6])
        with ExitStack() as first:
            g.wq = sb("wq", [P, KD, D], scope=first)
            g.wk = sb("wk", [P, KD, DKV], scope=first)
            g.wvr = sb("wvr", [P, KD, P], scope=first)
            g.mem = sb("mem", [P, P], scope=first)
            g.memn = sb("memn", [P, 2], scope=first)
            g.mw = sb("mw", [P, 1], scope=first)
            g.w = sb("w", [P, 2], scope=first)
            g.vp = sb("vp", [P, TILES, DKV], scope=first)
            g.q_stack = [sb(f"q_stack{i}", [STACK, NQ, HALF], BF16, scope=first) for i in range(4)]
            g.k_max = [sb(f"k_max{i}", [STACK, SEQ], BF16, scope=first) for i in range(2)]
            g.k_st = [sb(f"k_st{i}", [STACK, SEQ], BF16, scope=first) for i in range(2)]
            g.v_stack = [sb(f"v_stack{i}", [P, SEQ // P, 32], scope=first) for i in range(2)]
            g.row_no = sb("row_no", [P, TILES], scope=first)
            g.tile_no = sb("tile_no", [P, ROW_TILES], scope=first)
            g.tiles_end = sb("tiles_end", [P, EXPERTS], scope=first)
            g.logits = sb("logits", [P, TILES, EXPERTS], scope=first)
            g.weight = sb("weight", [P, TILES, TOP_K], scope=first)
            g.slot = sb("slot", [P, TOP_K, TILES], I32, scope=first)
            g.tile_expert = sb("tile_expert", [P, ROW_TILES], I32, scope=first)
            g.tile_rows = sb("tile_rows", [P, ROW_TILES], I32, scope=first)
            with ExitStack() as weights:
                g.wgu = sb("wgu", [P, EXPERTS, KD, 2 * INNER], scope=weights)
                g.wd = sb("wd", [P, EXPERTS, D], scope=weights)
                x_loaded = [ctx.enter_context(nc.semaphore(f"x_loaded{q}")) for q in range(4)]
                w_loaded, set_up = ctx.enter_context(nc.semaphore("w_loaded")), ctx.enter_context(nc.semaphore("set_up"))
                layernorm_statistics(nc, g, "ln0", lambda block: load_inputs(nc, g, a, block, x_loaded, w_loaded, set_up),
                                     x_loaded)
                project(nc, g, a)
                with ExitStack() as beside:
                    attention(nc, g, a, 0, NumberSlots(nc, g, a, beside), lambda load: dispatch(nc, g, a, load))
                read_table(nc, g, a)
                with ExitStack() as beside:
                    attention(nc, g, a, 1, AddExperts(nc, g, a, beside), lambda load: experts(nc, g, a, load))
        g.wqkv1 = sb("wqkv1", [P, KD, 3 * D])
        g.feat = sb("feat", [P, 4, P])
        g.fbias = sb("fbias", [P, 4])
        g.nw = sb("nw", [P, 1])
        g.wo1 = sb("wo1", [P, GROUPS, D])
        g.wg1 = sb("wg1", [P, KD, HIDDEN])
        g.wu1 = sb("wu1", [P, KD, HIDDEN])
        g.wd1 = sb("wd1", [P, HID_TILES, D])
        g.causal = sb("causal", [P, P])
        g.same_head = sb("same_head", [P, PER_TILE])
        g.kv_mask = sb("kv_mask", [P, PER_TILE, DK1])
        g.mean32 = sb("mean32", [P, GROUP, 32])
        g.eps = sb("eps", [P, 1])
        g.wqkv_high = sb("wqkv_high", [P, KD, 3 * D], F32R)
        g.feat_high = sb("feat_high", [P, 4, P], F32R)
        g.wqkv_rest = sb("wqkv_rest", [P, KD, 3 * D], F32R)
        g.feat_rest = sb("feat_rest", [P, 4, P], F32R)
        g.xh_all = sb("xh_all", [P, KD, TOKENS], F32R)
        g.xr_all = sb("xr_all", [P, KD, TOKENS], F32R)
        high_ready = ctx.enter_context(nc.semaphore("l1_high_ready"))
        rest_ready = ctx.enter_context(nc.semaphore("l1_rest_ready"))
        first_loaded = ctx.enter_context(nc.semaphore("l1_first_loaded"))
        loaded = ctx.enter_context(nc.semaphore("l1_loaded"))
        zeroed = ctx.enter_context(nc.semaphore("l1_zeroed"))
        cut = ctx.enter_context(nc.semaphore("l1_cut"))

        def second_inputs(block):
            @block.sync
            def _(sp):
                second_weights(sp, g, a, first_loaded, loaded)

            @block.gpsimd
            def _(pool):
                second_masks(pool, g, zeroed, cut)
            return split_second(g, first_loaded, high_ready, rest_ready)
        layernorm_statistics(nc, g, "ln1", second_inputs, first_tile=TILES // BATCH)
        with ExitStack() as features:
            g.q_all = sb("q_all", [P, KD, TOKENS], scope=features)
            g.k_all = sb("k_all", [P, KD, TOKENS], scope=features)
            g.kt_all = sb("kt_all", [P, TILES, KD * P], scope=features)
            g.v_all = sb("v_all", [P, TILES, D], scope=features)
            project_second(nc, g, a)
            linear_attention(nc, g, a, loaded, 16 * 5)
        feed_forward(nc, g, a)


def kernel(**inputs):
    import numpy as np
    import concourse.bacc as bacc
    from concourse.bass_utils import run_bass_kernel_spmd

    x = {name: np.asarray(value) for name, value in inputs.items()}

    def by_rows(w):
        return w.T.reshape(w.shape[1] // P, P, w.shape[0]).transpose(1, 0, 2)

    def blocks(w, n):
        out = np.zeros((n * w.shape[0], n * w.shape[1]), w.dtype)
        for i in range(n):
            out[i * w.shape[0]:(i + 1) * w.shape[0], i * w.shape[1]:(i + 1) * w.shape[1]] = w
        return out

    def pad_heads(w):
        out = np.zeros((w.shape[0] // DK1, 32, w.shape[1]), w.dtype)
        out[:, 0:DK1] = w.reshape(-1, DK1, w.shape[1])
        return out.reshape(-1, w.shape[1])

    wv_router = np.concatenate([x["L0_attn_Wv"], x["L0_ffn_router_w"], np.zeros((P - DKV - EXPERTS, D), np.float32)])
    gate_up = np.concatenate([x["L0_ffn_w_gate"], x["L0_ffn_w_up"]], axis=1)
    features = [x[f"L1_attn_{n}_w"] for n in ("fq1", "fq2", "fk1", "fk2")]
    biases = [x[f"L1_attn_{n}_b"] for n in ("fq1", "fq2", "fk1", "fk2")]
    host = {
        "x": x["L0_attn_x"].reshape(TILES, P, D).transpose(1, 0, 2),
        "wq": by_rows(x["L0_attn_Wq"]),
        "wk": by_rows(x["L0_attn_Wk"]),
        "wvr": by_rows(wv_router),
        "mem": blocks(x["L0_attn_memory"], 2),
        "memn": blocks(x["L0_attn_memory_norm"], 2),
        "mw": np.broadcast_to(x["L0_attn_memory_weight"], (P, 1)),
        "wgu": gate_up.transpose(2, 0, 1).reshape(KD, P, EXPERTS, 2 * INNER).transpose(1, 2, 0, 3),
        "wd": x["L0_ffn_w_down"].transpose(2, 0, 1),
        "wqkv1": by_rows(np.concatenate([x["L1_attn_wq"], x["L1_attn_wk"], x["L1_attn_wv"]])),
        "feat": np.stack([blocks(w.T, PER_TILE) for w in features], axis=1),
        "fbias": np.stack([np.tile(b, PER_TILE) for b in biases], axis=1),
        "nw": np.tile(pad_heads(x["L1_attn_norm_w"].reshape(DK1, 1)), (GROUP, 1)),
        "wo1": pad_heads(x["L1_attn_wo"].T).reshape(GROUPS, P, D).transpose(1, 0, 2),
        "wg1": by_rows(x["L1_ffn_w_gate"]),
        "wu1": by_rows(x["L1_ffn_w_up"]),
        "wd1": by_rows(x["L1_ffn_w_down"]),
    }
    nc = bacc.Bacc("TRN2", target_bir_lowering=False, num_devices=1)
    arrays = {f"in_{name}": np.ascontiguousarray(value) for name, value in host.items()}
    i = {name: nc.dram_tensor(f"in_{name}", value.shape, F32, kind="ExternalInput").ap() for name, value in host.items()}
    a = Buffers()
    a.x, a.wq, a.wk, a.wvr, a.mem, a.memn, a.mw = (i[n] for n in ("x", "wq", "wk", "wvr", "mem", "memn", "mw"))
    a.wgu, a.wd, a.wqkv1, a.feat, a.fbias, a.nw = (i[n] for n in ("wgu", "wd", "wqkv1", "feat", "fbias", "nw"))
    a.wo1, a.wg1, a.wu1, a.wd1 = (i[n] for n in ("wo1", "wg1", "wu1", "wd1"))
    q_pieces = nc.dram_tensor("q_pieces", [PIECES, TOKENS // HALF, DKV, NQ, HALF], BF16).ap()
    k_pieces = nc.dram_tensor("k_pieces", [PIECES, DKV, TOKENS], BF16).ap()
    a.q_pieces, a.k_pieces = q_pieces, k_pieces
    a.q_pieces_by_head = q_pieces.rearrange("p n (h d) q c -> p n h d (q c)", d=DH)
    a.k_pieces_by_head = k_pieces.rearrange("p (h d) t -> p h d t", d=DH)
    a.xn_flat = nc.dram_tensor("xn_rows", [TOKENS, D], F32).ap()
    a.xn_rows = a.xn_flat.rearrange("(t p) d -> p t d", p=P)
    a.slot_row = nc.dram_tensor("slot_row", [ROW_TILES * P, 1], F32).ap()
    a.expert_out = nc.dram_tensor("expert_out", [ROW_TILES * P, D], F32).ap()
    a.expert_out_tiles = a.expert_out.rearrange("(t p) d -> p t d", p=P)
    rows_out = nc.dram_tensor("rows_out", [BATCH, SEQ, D], F32, kind="ExternalOutput").ap()
    a.out = rows_out.rearrange("b (t p) d -> p (b t) d", p=P)
    build(nc, a)
    result = run_bass_kernel_spmd(nc, [arrays], core_ids=[0])
    return result.results[0]["rows_out"]
```
